# Optimizing a Trainium2 kernel written in Bass

```python
import numpy as np
import jax
import jax.numpy as jnp

def _softmax(x, axis=-1):
    return jax.nn.softmax(x, axis=axis)

def _gelu(x):
    return jax.nn.gelu(x, approximate=True)

def _silu(x):
    return jax.nn.silu(x)

def _sigmoid(x):
    return jax.nn.sigmoid(x)

def _layernorm(x, axis=-1, eps=1e-05):
    m = jnp.mean(x, axis=axis, keepdims=True)
    v = jnp.var(x, axis=axis, keepdims=True)
    return (x - m) / jnp.sqrt(v + eps)

def _scatter_add(tgt, idx, src, axis=0):
    return tgt.at[idx].add(src)

def _segment_sum(src, seg, n):
    return jax.ops.segment_sum(src, seg, n)
kernel_name = 'mk_decoder_postln_d1_seqx_r8_80e7e4'

def setup_inputs(seed: int=0):
    np.random.seed(seed)
    _w = jnp.asarray

    def _rec_inputs():
        import jax
        import jax.numpy as jnp
        _rk = jax.random.key(seed)
        x = -0.0005207 + 1.001 * jax.random.normal(jax.random.fold_in(_rk, 1), (4, 256, 512), jnp.float32)
        _lenS = 256 - jax.random.randint(jax.random.fold_in(_rk, 7), (4,), 0, max(1, 256 // 4) + 1, jnp.int32)
        _lenS2 = 1601 - jax.random.randint(jax.random.fold_in(_rk, 8), (4,), 0, max(1, 1601 // 4) + 1, jnp.int32)
        _ctx_4096P = jax.random.normal(jax.random.fold_in(_rk, 11), (4, 16, 512), jnp.float32)
        _ctx_4096c = jax.random.dirichlet(jax.random.fold_in(_rk, 511), 0.3 * jnp.ones((16,), jnp.float32), (4, 1601))
        _ctx_4096t = jnp.einsum('bsk,bkd->bsd', _ctx_4096c, _ctx_4096P)
        _ctx_4096t = _ctx_4096t * jax.lax.rsqrt(jnp.mean(jnp.square(_ctx_4096t)) + 1e-12) * 0.953939
        ctx_4096 = -0.00010331 + 0.999899 * (_ctx_4096t + 0.3 * jax.random.normal(jax.random.fold_in(_rk, 611), (4, 1601, 512), jnp.float32))
        return (x, ctx_4096)
    x, ctx_4096 = _rec_inputs()

    def _L0_attn_setup():
        import jax, jax.numpy as jnp
        import numpy as np
        HIDDEN = 512
        N_HEADS = 32
        N_KV_HEADS = 8
        HEAD_DIM = 128
        ROPE_THETA = 10000.0
        Q_SIZE = N_HEADS * HEAD_DIM
        KV_SIZE = N_KV_HEADS * HEAD_DIM
        N_KV_GROUPS = N_HEADS // N_KV_HEADS
        SCALING = HEAD_DIM ** (-0.5)

        def _rope_cos_sin(T, dtype):
            inv_freq = 1.0 / ROPE_THETA ** (jnp.arange(0, HEAD_DIM, 2, dtype=jnp.float32) / HEAD_DIM)
            pos = jnp.arange(T, dtype=jnp.float32)
            freqs = jnp.einsum('t,f->tf', pos, inv_freq)
            emb = jnp.concatenate([freqs, freqs], axis=-1)
            return (jnp.cos(emb).astype(dtype), jnp.sin(emb).astype(dtype))

        def _rotate_half(x):
            x1, x2 = jnp.split(x, 2, axis=-1)
            return jnp.concatenate([-x2, x1], axis=-1)

        def _apply_rope(q, k, cos, sin):
            cos = cos[None, None]
            sin = sin[None, None]
            q = q * cos + _rotate_half(q) * sin
            k = k * cos + _rotate_half(k) * sin
            return (q, k)
        key = jax.random.key(seed)
        k1, k2, k3 = jax.random.split(key, 3)
        B, T = (2, 256)
        hidden_states = jax.random.normal(k1, (B, T, HIDDEN), dtype=jnp.float32)
        w_qkv = jax.random.normal(k2, (HIDDEN, Q_SIZE + 2 * KV_SIZE), dtype=jnp.float32) * HIDDEN ** (-0.5)
        w_o = jax.random.normal(k3, (Q_SIZE, HIDDEN), dtype=jnp.float32) * Q_SIZE ** (-0.5)
        return {'hidden_states': hidden_states, 'w_qkv': w_qkv, 'w_o': w_o}
    _L0_attn_all = _L0_attn_setup()
    _L0_attn_in = {k: v for k, v in _L0_attn_all.items() if k in ('w_qkv', 'w_o')}
    del _L0_attn_all

    def _L0_xattn_setup():
        import jax, jax.numpy as jnp
        import numpy as np
        B, Q, D = (8, 64, 512)
        CTX = 512
        H, KV, HD = (16, 4, 96)
        G = H // KV
        key = jax.random.key(seed)
        ks = jax.random.split(key, 6)
        s = 0.02
        return {'latents': jax.random.normal(ks[0], (B, Q, D), jnp.float32), 'context': jax.random.normal(ks[1], (B, CTX, D), jnp.float32), 'Wq': jax.random.normal(ks[2], (H * HD, D), jnp.float32) * s, 'Wk': jax.random.normal(ks[3], (KV * HD, D), jnp.float32) * s, 'Wv': jax.random.normal(ks[4], (KV * HD, D), jnp.float32) * s, 'Wo': jax.random.normal(ks[5], (D, H * HD), jnp.float32) * s}
    _L0_xattn_all = _L0_xattn_setup()
    _L0_xattn_in = {k: v for k, v in _L0_xattn_all.items() if k in ('Wq', 'Wk', 'Wv', 'Wo')}
    del _L0_xattn_all

    def _L0_ffn_setup():
        import jax, jax.numpy as jnp
        import numpy as np
        B_, S, D_IN, D_OUT = (4, 256, 512, 512)
        N, RANK, ALPHA = (8, 16, 32)
        SCALE = ALPHA / RANK
        key = jax.random.key(seed)
        kx, ka, kb, kw, kbias = jax.random.split(key, 5)
        x = jax.random.normal(kx, (B_, S, D_IN), dtype=jnp.float32)
        lora_A = jax.random.normal(ka, (N, RANK, D_IN), dtype=jnp.float32) * (1.0 / np.sqrt(D_IN))
        lora_B = jax.random.normal(kb, (N, D_OUT, RANK), dtype=jnp.float32) * (1.0 / np.sqrt(RANK))
        W = jax.random.normal(kw, (D_OUT, D_IN), dtype=jnp.float32) * (1.0 / np.sqrt(D_IN))
        bias = jax.random.normal(kbias, (D_OUT,), dtype=jnp.float32) * 0.01
        lora_weights = jnp.full((N,), 1.0 / N, dtype=jnp.float32)
        return {'x': x, 'lora_A': lora_A, 'lora_B': lora_B, 'W': W, 'bias': bias, 'lora_weights': lora_weights}
    _L0_ffn_all = _L0_ffn_setup()
    _L0_ffn_in = {k: v for k, v in _L0_ffn_all.items() if k in ('lora_A', 'lora_B', 'W', 'bias', 'lora_weights')}
    del _L0_ffn_all
    return {'x': x, 'ctx_4096': ctx_4096, 'L0_attn_w_qkv': _L0_attn_in['w_qkv'], 'L0_attn_w_o': _L0_attn_in['w_o'], 'L0_xattn_Wq': _L0_xattn_in['Wq'], 'L0_xattn_Wk': _L0_xattn_in['Wk'], 'L0_xattn_Wv': _L0_xattn_in['Wv'], 'L0_xattn_Wo': _L0_xattn_in['Wo'], 'L0_ffn_lora_A': _L0_ffn_in['lora_A'], 'L0_ffn_lora_B': _L0_ffn_in['lora_B'], 'L0_ffn_W': _L0_ffn_in['W'], 'L0_ffn_bias': _L0_ffn_in['bias'], 'L0_ffn_lora_weights': _L0_ffn_in['lora_weights']}

def reference(x, ctx_4096, L0_attn_w_qkv, L0_attn_w_o, L0_xattn_Wq, L0_xattn_Wk, L0_xattn_Wv, L0_xattn_Wo, L0_ffn_lora_A, L0_ffn_lora_B, L0_ffn_W, L0_ffn_bias, L0_ffn_lora_weights):
    import jax
    import jax.numpy as jnp

    def _L0_attn_ref(hidden_states, w_qkv, w_o):
        import jax, jax.numpy as jnp
        import numpy as np
        HIDDEN = 512
        N_HEADS = 32
        N_KV_HEADS = 8
        HEAD_DIM = 128
        ROPE_THETA = 10000.0
        Q_SIZE = N_HEADS * HEAD_DIM
        KV_SIZE = N_KV_HEADS * HEAD_DIM
        N_KV_GROUPS = N_HEADS // N_KV_HEADS
        SCALING = HEAD_DIM ** (-0.5)

        def _rope_cos_sin(T, dtype):
            inv_freq = 1.0 / ROPE_THETA ** (jnp.arange(0, HEAD_DIM, 2, dtype=jnp.float32) / HEAD_DIM)
            pos = jnp.arange(T, dtype=jnp.float32)
            freqs = jnp.einsum('t,f->tf', pos, inv_freq)
            emb = jnp.concatenate([freqs, freqs], axis=-1)
            return (jnp.cos(emb).astype(dtype), jnp.sin(emb).astype(dtype))

        def _rotate_half(x):
            x1, x2 = jnp.split(x, 2, axis=-1)
            return jnp.concatenate([-x2, x1], axis=-1)

        def _apply_rope(q, k, cos, sin):
            cos = cos[None, None]
            sin = sin[None, None]
            q = q * cos + _rotate_half(q) * sin
            k = k * cos + _rotate_half(k) * sin
            return (q, k)
        B, T, _ = hidden_states.shape
        qkv = hidden_states @ w_qkv
        q, k, v = jnp.split(qkv, [Q_SIZE, Q_SIZE + KV_SIZE], axis=-1)
        q = q.reshape(B, T, N_HEADS, HEAD_DIM).transpose(0, 2, 1, 3)
        k = k.reshape(B, T, N_KV_HEADS, HEAD_DIM).transpose(0, 2, 1, 3)
        v = v.reshape(B, T, N_KV_HEADS, HEAD_DIM).transpose(0, 2, 1, 3)
        cos, sin = _rope_cos_sin(T, q.dtype)
        q, k = _apply_rope(q, k, cos, sin)
        qg = q.reshape(B, N_KV_HEADS, N_KV_GROUPS, T, HEAD_DIM)
        att = jnp.einsum('bkgtd,bksd->bkgts', qg, k) * SCALING
        causal = jnp.tril(jnp.ones((T, T), dtype=bool))
        att = jnp.where(causal, att, -jnp.inf)
        att = jax.nn.softmax(att, axis=-1)
        y = jnp.einsum('bkgts,bksd->bkgtd', att, v)
        y = y.reshape(B, N_HEADS, T, HEAD_DIM).transpose(0, 2, 1, 3).reshape(B, T, Q_SIZE)
        return y @ w_o

    def _L0_xattn_ref(latents, context, Wq, Wk, Wv, Wo):
        import jax, jax.numpy as jnp
        import numpy as np
        B, Q, D = (8, 64, 512)
        CTX = 512
        H, KV, HD = (16, 4, 96)
        G = H // KV
        b, q_len, _ = latents.shape
        hidden = jnp.concatenate([context, latents], axis=1)
        s_len = hidden.shape[1]
        q = (latents @ Wq.T).reshape(b, q_len, H, HD)
        k = (hidden @ Wk.T).reshape(b, s_len, KV, HD)
        v = (hidden @ Wv.T).reshape(b, s_len, KV, HD)
        q = q.transpose(0, 2, 1, 3).reshape(b, KV, G, q_len, HD)
        k = k.transpose(0, 2, 1, 3)
        v = v.transpose(0, 2, 1, 3)
        scale = 1.0 / jnp.sqrt(jnp.asarray(HD, q.dtype))
        scores = jnp.einsum('bkgqd,bksd->bkgqs', q, k) * scale
        attn = jax.nn.softmax(scores.astype(jnp.float32), axis=-1).astype(q.dtype)
        out = jnp.einsum('bkgqs,bksd->bkgqd', attn, v)
        out = out.reshape(b, H, q_len, HD).transpose(0, 2, 1, 3).reshape(b, q_len, H * HD)
        return out @ Wo.T

    def _L0_ffn_ref(x, lora_A, lora_B, W, bias, lora_weights):
        import jax, jax.numpy as jnp
        import numpy as np
        B_, S, D_IN, D_OUT = (4, 256, 512, 512)
        N, RANK, ALPHA = (8, 16, 32)
        SCALE = ALPHA / RANK
        h = jnp.einsum('bsd,nrd->nbsr', x, lora_A)
        coef = (SCALE * lora_weights)[:, None, None]
        lora_out = jnp.einsum('nbsr,nor->bso', h, lora_B * coef)
        base = jnp.einsum('bsd,od->bso', x, W) + bias
        return base + lora_out
    x = _layernorm(x + _L0_attn_ref(x, L0_attn_w_qkv, L0_attn_w_o), axis=-1)
    x = _layernorm(x + _L0_xattn_ref(x, ctx_4096, L0_xattn_Wq, L0_xattn_Wk, L0_xattn_Wv, L0_xattn_Wo), axis=-1)
    x = _layernorm(x + _L0_ffn_ref(x, L0_ffn_lora_A, L0_ffn_lora_B, L0_ffn_W, L0_ffn_bias, L0_ffn_lora_weights), axis=-1)
    return x

_drawn_inputs = setup_inputs


def setup_inputs(seed=0):
    import zlib

    import numpy as np

    out = dict(_drawn_inputs(seed))
    spreads = {'L0_ffn_lora_weights': (0.125, 0.2)}
    factors = {'L0_xattn_Wq': 5.222, 'L0_xattn_Wk': 5.206, 'L0_ffn_bias': 8.0}
    for name, (base, spread) in spreads.items():
        noise = np.random.default_rng([zlib.crc32(name.encode()), seed]).standard_normal(out[name].shape)
        drawn = base * np.exp(spread * noise) if base else spread * noise
        out[name] = jnp.asarray(drawn.astype(out[name].dtype))
    for name, factor in factors.items():
        out[name] = (out[name] * factor).astype(out[name].dtype)
    return out
```

```python
from contextlib import ExitStack

import concourse.bass as bass
import numpy as np
from concourse import mybir

F32 = mybir.dt.float32
F32R = mybir.dt.float32r
ALU = mybir.AluOpType
ACT = mybir.ActivationFunctionType
X = mybir.AxisListType.X

P = 128
BANK = 512
HI, LO = 0, 1
PARTS = ((HI, HI), (HI, LO), (LO, HI))
NEG = -1e30

B, T, D = 4, 256, 512
TOK = B * T
C = D // P
TILES = TOK // P
EPS = 1e-5

KVH, GRP, HD = 8, 4, 128
NHALF, HALF = 2, 512
SCALE_A = HD ** -0.5
FEAT_A = (GRP + 2) * HD

CTX, KV2, G2, HD2 = 1601, 4, 4, 96
H2 = KV2 * G2
CTXP = CTX + 1
S2 = CTXP + T
SCALE_B = HD2 ** -0.5
KT2 = [(i * P, P) for i in range(12)] + [(CTXP, P), (CTXP + P, P), (12 * P, CTX - 12 * P)]
NT2 = len(KT2)
CHUNKS2 = [(0, 512), (512, 512), (1024, 512), (1536, S2 - 1536)]
ROWB = HD2


def f(ap):
    return ap.bitcast(F32)


class Sem:

    def __init__(self, nc, stack, name, per=0, start=0):
        self.sem, self.per, self.start = stack.enter_context(nc.semaphore(name)), per, start

    def at(self, g, k):
        return g * self.per + (k + self.start)



TILE_V, TILE_K = GRP + 1, GRP
ROPED = (TILE_K, *range(GRP))
UNITS = 2 * B


def schedule_a():
    s = []
    for n in range(NHALF):
        s += [("proj", n, TILE_V)] + [("proj", n, t) for t in ROPED]
        if n:
            s += [("pv", 3), ("wo", 1, 0), ("wo", 1, 1)]
        s += [("vtr", n)]
        b = 2 * n
        s += [("max", b, h) for h in range(GRP)] + [("row", b, 0), ("row", b, 1)]
        for i in range(4):
            u = 4 * n + i
            s += [("scores", u)]
            if i < 2:
                s += [("max", b + 1, 2 * i), ("max", b + 1, 2 * i + 1)]
            if i == 1:
                s += [("row", b + 1, 0), ("row", b + 1, 1)]
            if i:
                s += [("pv", u - 1)]
            if i == 3:
                s += [("wo", b, 0), ("wo", b, 1)]
    return s + [("pv", 7), ("wo", 3, 0), ("wo", 3, 1)]


RINGED = ("proj", "vtr", "max", "row", "wo")


def self_attention(nc, x_t, x_rows, w_qkv, w_o, cos_t, sin_t, mask, eye, acc):
    sched = schedule_a()
    order = [s for s in sched if s[0] in RINGED]
    place = {s: k for k, s in enumerate(order)}
    ringed = len(order)
    assert ringed % 2 == 0
    NR = len(ROPED)

    with ExitStack() as st:
        def sb(name, shape, dt=F32):
            return st.enter_context(nc.sbuf_tensor(name, shape, dt))

        def sem(name, per=0, start=0):
            return Sem(nc, st, name, per, start)

        xt = sb("a_xt", [P, 2, C, TOK], F32R)
        raw = sb("a_raw", [P, C, FEAT_A])
        w = sb("a_w", [P, 2, C, FEAT_A], F32R)
        wo = sb("a_wo", [P, 2, GRP, D], F32R)
        cos, sin = sb("a_cos", [P, HALF]), sb("a_sin", [P, HALF])
        msk = sb("a_mask", [P, 2, T])
        idf, idr = sb("a_idf", [P, P]), sb("a_idr", [P, P], F32R)
        ones = sb("a_ones", [P, P], F32R)
        swapped = sb("a_swapped", [P, 2, HALF])
        roped = sb("a_roped", [P, 2, HALF])
        qk = sb("a_qk", [P, 2, GRP + 1, HALF], F32R)
        vt = sb("a_vt", [P, HALF])
        v = sb("a_v", [P, 2, 4, HD], F32R)
        neg = sb("a_neg", [P, B, GRP, 2])
        negr = sb("a_negr", [P, B, GRP, 2], F32R)
        junk = sb("a_junk", [P, 2, T])
        row = sb("a_row", [1, 2, 2, HALF], F32R)
        pf = sb("a_pf", [P, 2, 3 * T])
        pr = sb("a_pr", [P, 2, 2, 3 * T], F32R)
        rsum = sb("a_rsum", [P, HALF])
        yf = sb("a_yf", [P, 2, HALF])
        y = sb("a_y", [P, 2, 2, GRP, T], F32R)

        ring = [st.enter_context(nc.psum_tensor(f"a_ring{i}", [P, BANK], F32)) for i in range(2)]
        ps_s = [st.enter_context(nc.psum_tensor(f"a_s{i}", [P, 2 * BANK], F32)) for i in range(2)]
        ps_o = st.enter_context(nc.psum_tensor("a_o", [P, BANK], F32))
        ps_l = st.enter_context(nc.psum_tensor("a_l", [P, BANK], F32))

        x_in, consts_in = sem("a_x_in"), sem("a_consts_in")
        x_hi, x_lo, const_made = sem("a_x_hi"), sem("a_x_lo"), sem("a_const_made")
        w_in, wo_in = sem("a_w_in", 16), sem("a_wo_in", 16)
        w_hi, w_lo = sem("a_w_hi", C), sem("a_w_lo", C)
        wo_hi, wo_lo = sem("a_wo_hi", GRP), sem("a_wo_lo", GRP)
        full = sem("a_ring_full", ringed)
        was_swapped = sem("a_was_swapped", NHALF * NR)
        was_turned = sem("a_was_turned", NHALF * NR)
        was_cos = sem("a_was_cos", NHALF * NR)
        rope_sum = sem("a_rope_sum", NHALF * NR, 2)
        rope_hi, rope_lo = sem("a_rope_hi", NHALF * NR), sem("a_rope_lo", NHALF * NR, 2)
        vt_made, v_hi, v_lo = sem("a_vt_made", NHALF), sem("a_v_hi", NHALF), sem("a_v_lo", NHALF)
        mx_made, neg_made = sem("a_mx_made", 2 * B * GRP), sem("a_neg_made", B)
        row_made = sem("a_row_made", 2 * B)
        s_made, exp_done, masked = sem("a_s_made", UNITS), sem("a_exp_done", UNITS, 2), sem("a_masked", 2 * UNITS)
        p_hi, p_lo, pv_done = sem("a_p_hi", UNITS), sem("a_p_lo", UNITS, 2), sem("a_pv_done", UNITS)
        r_made, y_made = sem("a_r_made", UNITS), sem("a_y_made", UNITS, 1)
        y_hi, y_lo = sem("a_y_hi", UNITS), sem("a_y_lo", UNITS, 2)
        acc_done = sem("a_acc_done", 2 * B, 2)
        held = sem("a_held")

        blk = st.enter_context(nc.Block())

        def loop(e, body):
            with e.Fori(0, KVH - 1) as g:
                body(g, False)
            body(KVH - 1, True)

        def left(step, g):
            kind = step[0]
            if kind == "proj" and step[2] == TILE_V:
                return vt_made, vt_made.at(g, step[1] + 1)
            if kind == "proj":
                return was_cos, was_cos.at(g, step[1] * NR + ROPED.index(step[2]) + 1)
            if kind == "vtr":
                return v_lo, v_lo.at(g, step[1] + 1)
            if kind == "max":
                return mx_made, mx_made.at(g, 2 * (step[1] * GRP + step[2]) + 2)
            if kind == "row":
                return row_made, row_made.at(g, 2 * step[1] + step[2] + 1)
            return acc_done, acc_done.at(g, 2 * step[1] + step[2] + 1)

        def x_stage(c):
            home = (pf[:].rearrange("p a b -> p (a b)"), yf[:].rearrange("p a b -> p (a b)"),
                    swapped[:].rearrange("p a b -> p (a b)"), roped[:].rearrange("p a b -> p (a b)"))[c]
            return home[:, 0:TOK]

        @blk.sync
        def _(sp):
            for c in range(C):
                sp.dma_start(x_stage(c), x_t[:, c, :]).then_inc(x_in.sem, 16)
            sp.dma_start(raw[:], w_qkv[0]).then_inc(w_in.sem, 16)
            for dst, src in ((cos, cos_t), (sin, sin_t), (msk, mask), (idf, eye), (acc, x_rows)):
                sp.dma_start(dst[:], src).then_inc(consts_in.sem, 16)
            sp.wait_ge(w_hi.sem, w_hi.at(0, C))
            sp.wait_ge(w_lo.sem, w_lo.at(0, C))
            sp.dma_start(raw[:, :, 0:D], w_o[0]).then_inc(wo_in.sem, 16)
            for g in range(1, KVH):
                sp.wait_ge(wo_hi.sem, wo_hi.at(g, 0))
                sp.wait_ge(wo_lo.sem, wo_lo.at(g, 0))
                sp.dma_start(raw[:], w_qkv[g]).then_inc(w_in.sem, 16)
                sp.wait_ge(w_hi.sem, w_hi.at(g, C))
                sp.wait_ge(w_lo.sem, w_lo.at(g, C))
                sp.dma_start(raw[:, :, 0:D], w_o[g]).then_inc(wo_in.sem, 16)

        @blk.tensor
        def _(pe):
            pe.wait_ge(x_hi.sem, C)
            pe.wait_ge(x_lo.sem, C)
            pe.wait_ge(const_made.sem, 2)
            pe.wait_ge(consts_in.sem, 80)

            def take(step, g):
                k = place[step]
                if k >= 2:
                    s, value = left(order[k - 2], g)
                else:
                    assert order[-2][0] == order[-1][0] == "wo"
                    s, value = acc_done, acc_done.at(g, k - 1)
                pe.wait_ge(s.sem, value)
                return ring[k % 2]

            def project(step, g):
                _, n, t = step
                if (n, t) == (0, TILE_V):
                    pe.wait_ge(w_hi.sem, w_hi.at(g, C))
                    pe.wait_ge(w_lo.sem, w_lo.at(g, C))
                bank, i = take(step, g), 0
                for c in range(C):
                    for a, m in PARTS:
                        mm = pe.matmul(bank[:], w[:, a, c, t * HD:(t + 1) * HD],
                                       xt[:, m, c, n * HALF:(n + 1) * HALF], start=i == 0, stop=i == 3 * C - 1)
                        i += 1
                mm.then_inc(full.sem, 1)

            def turn_values(step, g):
                pe.wait_ge(vt_made.sem, vt_made.at(g, step[1] + 1))
                bank = take(step, g)
                for i in range(4):
                    mm = pe.transpose(bank[:, i * P:(i + 1) * P], vt[:, i * P:(i + 1) * P], idf[:])
                mm.then_inc(full.sem, 1)

            def coarse_scores(step, g):
                _, b, h = step
                q0 = (b % 2) * T
                pe.wait_ge(rope_hi.sem, rope_hi.at(g, (b // 2 + 1) * NR))
                pe.wait_ge(rope_lo.sem, rope_lo.at(g, (b // 2 + 1) * NR))
                bank = take(step, g)
                for qt in range(2):
                    mm = pe.matmul(bank[:, qt * T:(qt + 1) * T], qk[:, HI, 1 + h, q0 + qt * P:q0 + (qt + 1) * P],
                                   qk[:, HI, 0, q0:q0 + T], start=True, stop=True)
                mm.then_inc(full.sem, 1)

            def shift_row(step, g):
                _, b, hp = step
                pe.wait_ge(neg_made.sem, neg_made.at(g, b + 1))
                bank = take(step, g)
                for i in range(4):
                    h, qt = 2 * hp + i // 2, i % 2
                    mm = pe.transpose(bank[0:1, i * P:(i + 1) * P].bitcast(F32R), negr[:, b, h, qt:qt + 1], idr[:])
                mm.then_inc(full.sem, 1)

            def scores(u, g):
                b, hp = u // 2, u % 2
                q0, heads = (b % 2) * T, slice(1 + 2 * hp, 3 + 2 * hp)
                pe.wait_ge(row_made.sem, row_made.at(g, u + 1))
                pe.wait_ge(exp_done.sem, exp_done.at(g, u - 1))
                s = ps_s[u % 2]
                for kt in range(2):
                    out = s[:, 0:BANK] if kt == 0 else s[:, BANK:BANK + T]
                    at = kt * P
                    for i, (a, m) in enumerate(PARTS):
                        pe.matmul(out, qk[:, a, 0, q0 + at:q0 + at + P], qk[:, m, heads, q0 + at:q0 + T],
                                  start=i == 0, stop=False)
                    shift = row[:, b % 2, hp, :].rearrange("o (h q) -> o h q", h=2)[:, :, at:T]
                    mm = pe.matmul(out, ones[0:1, :], shift, start=False, stop=True)
                mm.then_inc(s_made.sem, 1)

            def values(u, g):
                b = u // 2
                pe.wait_ge(v_lo.sem, v_lo.at(g, b // 2 + 1))
                pe.wait_ge(p_hi.sem, p_hi.at(g, u + 1))
                pe.wait_ge(p_lo.sem, p_lo.at(g, u + 1))
                pe.wait_ge(y_made.sem, y_made.at(g, u))
                late = [x[:].rearrange("p (h q) -> p h q", h=2)[:, :, P:T] for x in (ps_o, ps_l)]
                for kt in range(2):
                    for i, (a, m) in enumerate(PARTS):
                        pe.matmul(late[0] if kt else ps_o[:], v[:, a, 2 * (b % 2) + kt, :],
                                  pr[:, u % 2, m, 2 * T * kt:2 * T + T * kt], start=kt == 0 and i == 0,
                                  stop=kt == 1 and i == 2, skip_group_check=True)
                for kt in range(2):
                    for m in (HI, LO):
                        mm = pe.matmul(late[1] if kt else ps_l[:], ones[:], pr[:, u % 2, m, 2 * T * kt:2 * T + T * kt],
                                       start=kt == 0 and m == HI, stop=kt == 1 and m == LO, skip_group_check=True)
                mm.then_inc(pv_done.sem, 1)

            def output(step, g):
                _, b, tt = step
                pe.wait_ge(wo_hi.sem, wo_hi.at(g, GRP))
                pe.wait_ge(wo_lo.sem, wo_lo.at(g, GRP))
                pe.wait_ge(y_hi.sem, y_hi.at(g, 2 * b + 2))
                pe.wait_ge(y_lo.sem, y_lo.at(g, 2 * b + 2))
                bank, i = take(step, g), 0
                for h in range(GRP):
                    for a, m in PARTS:
                        mm = pe.matmul(bank[:], y[:, b % 2, a, h, tt * P:(tt + 1) * P], wo[:, m, h, :],
                                       start=i == 0, stop=i == 3 * GRP - 1)
                        i += 1
                mm.then_inc(full.sem, 1)

            def body(g, last):
                for step in sched:
                    if step[0] == "scores":
                        scores(step[1], g)
                    elif step[0] == "pv":
                        values(step[1], g)
                    else:
                        {"proj": project, "vtr": turn_values, "max": coarse_scores, "row": shift_row,
                         "wo": output}[step[0]](step, g)

            loop(pe, body)

        @blk.scalar
        def _(act):
            act.sem_inc(exp_done.sem, 2)
            for c in range(C):
                act.wait_ge(x_in.sem, 16 * C)
                act.activation(xt[:, HI, c, :], x_stage(c), ACT.Copy).then_inc(x_hi.sem, 1)

            def split_w(g):
                act.wait_ge(w_in.sem, w_in.at(g, 16))
                for c in range(C):
                    act.activation(w[:, HI, c, :], raw[:, c, :], ACT.Copy).then_inc(w_hi.sem, 1)

            split_w(0)

            def body(g, last):
                for step in sched:
                    kind, *arg = step
                    if step in place:
                        k = place[step]
                        bank = ring[k % 2]
                    if kind == "proj" and arg[1] == TILE_V:
                        act.wait_ge(full.sem, full.at(g, k + 1))
                        act.activation(vt[:], bank[:], ACT.Copy).then_inc(vt_made.sem, 1)
                        if arg[0] == 0:
                            act.wait_ge(wo_in.sem, wo_in.at(g, 16))
                            for h in range(GRP):
                                act.activation(wo[:, HI, h, :], raw[:, h, 0:D], ACT.Copy).then_inc(wo_hi.sem, 1)
                    elif kind == "proj":
                        r = arg[0] * NR + ROPED.index(arg[1])
                        act.wait_ge(full.sem, full.at(g, k + 1))
                        act.wait_ge(rope_sum.sem, rope_sum.at(g, r - 1))
                        act.activation(swapped[0:64, r % 2, :], bank[64:128, :], ACT.Copy)
                        act.activation(swapped[64:128, r % 2, :], bank[0:64, :], ACT.Copy)\
                           .then_inc(was_swapped.sem, 1)
                    elif kind == "vtr":
                        act.wait_ge(full.sem, full.at(g, k + 1))
                        act.activation(v[:, HI].rearrange("p t d -> p (t d)"), bank[:], ACT.Copy).then_inc(v_hi.sem, 1)
                    elif kind == "row":
                        act.wait_ge(full.sem, full.at(g, k + 1))
                        act.activation(row[:, arg[0] % 2, arg[1], :], bank[0:1, :], ACT.Copy).then_inc(row_made.sem, 1)
                    elif kind == "scores":
                        u = arg[0]
                        act.wait_ge(s_made.sem, s_made.at(g, u + 1))
                        act.wait_ge(p_lo.sem, p_lo.at(g, u - 1))
                        act.activation(pf[:, u % 2, :], ps_s[u % 2][:, 0:3 * T], ACT.Exp, scale=SCALE_A)\
                           .then_inc(exp_done.sem, 1)
                        act.wait_ge(masked.sem, masked.at(g, 2 * u + 2))
                        if u >= 2:
                            act.wait_ge(pv_done.sem, pv_done.at(g, u - 1))
                        act.activation(pr[:, u % 2, HI, :], pf[:, u % 2, :], ACT.Copy).then_inc(p_hi.sem, 1)
                        if u >= 4 and not last:
                            c = u - 4
                            act.wait_ge(full.sem, full.at(g, place[("proj", 1, ROPED[-1])] + 1))
                            act.wait_ge(w_in.sem, w_in.at(g + 1, 16))
                            act.activation(w[:, HI, c, :], raw[:, c, :], ACT.Copy).then_inc(w_hi.sem, 1)

            loop(act, body)

        @blk.vector
        def _(dve):
            dve.sem_inc(acc_done.sem, 2)
            dve.sem_inc(p_lo.sem, 2)
            dve.sem_inc(y_made.sem, 1)
            dve.sem_inc(rope_sum.sem, 2)
            dve.memset(f(ones[:]), 1.0).then_inc(const_made.sem, 1)
            dve.wait_ge(consts_in.sem, 80)
            dve.tensor_copy(idr[:], idf[:]).then_inc(const_made.sem, 1)

            def rope_end(g, r):
                n, j = divmod(r, NR)
                dve.wait_ge(was_turned.sem, was_turned.at(g, r + 1))
                dve.wait_ge(was_cos.sem, was_cos.at(g, r + 1))
                dve.tensor_tensor(roped[:, r % 2, :], roped[:, r % 2, :], swapped[:, r % 2, :], ALU.add)\
                   .then_inc(rope_sum.sem, 1)
                dve.wait_ge(rope_sum.sem, rope_sum.at(g, r + 1))
                dve.tensor_copy(qk[:, HI, j, :], roped[:, r % 2, :]).then_inc(rope_hi.sem, 1)

            def body(g, last):
                for step in sched:
                    kind, *arg = step
                    if step in place:
                        k = place[step]
                        bank = ring[k % 2]
                    if kind == "proj" and arg[1] != TILE_V:
                        r = arg[0] * NR + ROPED.index(arg[1])
                        dve.wait_ge(was_swapped.sem, was_swapped.at(g, r + 1))
                        dve.wait_ge(rope_lo.sem, rope_lo.at(g, r - 1))
                        dve.tensor_tensor(roped[:, r % 2, :], bank[:], cos[:], ALU.mult).then_inc(was_cos.sem, 1)
                        if r % NR:
                            rope_end(g, r - 1)
                        if r % NR == NR - 1:
                            rope_end(g, r)
                    elif kind == "vtr":
                        dve.wait_ge(v_hi.sem, v_hi.at(g, arg[0] + 1))
                        dve.tensor_tensor(v[:, LO].rearrange("p t d -> p (t d)"), bank[:],
                                          f(v[:, HI].rearrange("p t d -> p (t d)")), ALU.subtract)\
                           .then_inc(v_lo.sem, 1)
                    elif kind == "max":
                        b, h = arg
                        for qt in range(2):
                            if qt == 0:
                                dve.wait_ge(full.sem, full.at(g, k + 1))
                                dve.sem_inc(held.sem, 1)
                            dve.tensor_tensor_reduce(junk[:, qt, :], bank[:, qt * T:(qt + 1) * T], msk[:, qt, :], 1.0, NEG,
                                                     ALU.add, ALU.max, neg[:, b, h, qt:qt + 1]).then_inc(mx_made.sem, 1)
                        dve.wait_ge(mx_made.sem, mx_made.at(g, 2 * (b * GRP + h) + 2))
                        if h == GRP - 1:
                            dve.tensor_scalar(negr[:, b, :, :], neg[:, b, :, :], -1.0, None, ALU.mult)\
                               .then_inc(neg_made.sem, 1)
                    elif kind == "scores":
                        u = arg[0]
                        dve.wait_ge(p_hi.sem, p_hi.at(g, u + 1))
                        dve.tensor_tensor(pr[:, u % 2, LO, :], pf[:, u % 2, :], f(pr[:, u % 2, HI, :]), ALU.subtract)\
                           .then_inc(p_lo.sem, 1)
                    elif kind == "pv":
                        u = arg[0]
                        b, hp = u // 2, u % 2
                        dve.wait_ge(pv_done.sem, pv_done.at(g, u + 1))
                        dve.reciprocal(rsum[:], ps_l[:]).then_inc(r_made.sem, 1)
                        dve.wait_ge(r_made.sem, r_made.at(g, u + 1))
                        dve.wait_ge(y_lo.sem, y_lo.at(g, u - 1))
                        dve.tensor_tensor(yf[:, u % 2, :], ps_o[:], rsum[:], ALU.mult).then_inc(y_made.sem, 1)
                        dve.wait_ge(y_made.sem, y_made.at(g, u + 1))
                        dve.tensor_copy(y[:, b % 2, HI, 2 * hp:2 * hp + 2, :].rearrange("p h q -> p (h q)"),
                                        yf[:, u % 2, :]).then_inc(y_hi.sem, 1)
                    elif kind == "wo":
                        b, tt = arg
                        dve.wait_ge(full.sem, full.at(g, k + 1))
                        dve.tensor_tensor(acc[:, 2 * b + tt, :], bank[:], acc[:, 2 * b + tt, :], ALU.add)\
                           .then_inc(acc_done.sem, 1)

            loop(dve, body)
            dve.wait_ge(acc_done.sem, acc_done.at(KVH - 1, 2 * B))

        @blk.gpsimd
        def _(pool):
            pool.sem_inc(rope_lo.sem, 2)
            pool.sem_inc(y_lo.sem, 2)
            for c in range(C):
                pool.wait_ge(x_hi.sem, c + 1)
                pool.tensor_tensor(xt[:, LO, c, :], x_stage(c), f(xt[:, HI, c, :]), ALU.subtract).then_inc(x_lo.sem, 1)

            def split_w(g, c):
                pool.wait_ge(w_hi.sem, w_hi.at(g, c + 1))
                pool.tensor_tensor(w[:, LO, c, :], raw[:, c, :], f(w[:, HI, c, :]), ALU.subtract).then_inc(w_lo.sem, 1)

            for c in range(C):
                split_w(0, c)

            def rope_low(g, r):
                pool.wait_ge(rope_hi.sem, rope_hi.at(g, r + 1))
                pool.tensor_tensor(qk[:, LO, r % NR, :], roped[:, r % 2, :], f(qk[:, HI, r % NR, :]), ALU.subtract)\
                    .then_inc(rope_lo.sem, 1)

            def body(g, last):
                for step in sched:
                    kind, *arg = step
                    if kind == "proj" and arg[1] == TILE_V and arg[0] == 0:
                        for h in range(GRP):
                            pool.wait_ge(wo_hi.sem, wo_hi.at(g, h + 1))
                            pool.tensor_tensor(wo[:, LO, h, :], raw[:, h, 0:D], f(wo[:, HI, h, :]), ALU.subtract)\
                                .then_inc(wo_lo.sem, 1)
                    elif kind == "proj" and arg[1] != TILE_V:
                        r = arg[0] * NR + ROPED.index(arg[1])
                        pool.wait_ge(was_swapped.sem, was_swapped.at(g, r + 1))
                        pool.tensor_tensor(swapped[:, r % 2, :], swapped[:, r % 2, :], sin[:], ALU.mult)\
                            .then_inc(was_turned.sem, 1)
                        if r % NR:
                            rope_low(g, r - 1)
                        if r % NR == NR - 1:
                            rope_low(g, r)
                    elif kind == "scores":
                        u = arg[0]
                        pool.wait_ge(exp_done.sem, exp_done.at(g, u + 1))
                        pool.sem_inc(held.sem, 1)
                        for i, blocks in enumerate((pf[:, u % 2, 0:2 * T].rearrange("p (h q) -> p h q", h=2)[:, :, 0:P],
                                                    pf[:, u % 2, 2 * T:3 * T].rearrange("p (h q) -> p h q", h=2))):
                            pool.affine_select(out=blocks, in_=blocks, pattern=[[0, 2], [1, P]], compare_op=ALU.is_ge,
                                               fill=0.0, base=0, channel_multiplier=-1).then_inc(masked.sem, 1)
                        if u >= 4 and not last:
                            split_w(g + 1, u - 4)
                    elif kind == "pv":
                        u = arg[0]
                        b, hp = u // 2, u % 2
                        pool.wait_ge(y_hi.sem, y_hi.at(g, u + 1))
                        pool.tensor_tensor(y[:, b % 2, LO, 2 * hp:2 * hp + 2, :].rearrange("p h q -> p (h q)"),
                                           yf[:, u % 2, :],
                                           f(y[:, b % 2, HI, 2 * hp:2 * hp + 2, :].rearrange("p h q -> p (h q)")),
                                           ALU.subtract).then_inc(y_lo.sem, 1)

            loop(pool, body)



def between(nc, eye, wq, acc, x1_dram, x1t_dram, q_dram):
    with ExitStack() as st:
        def sb(name, shape, dt=F32):
            return st.enter_context(nc.sbuf_tensor(name, shape, dt))

        def sem(name, start=0):
            return Sem(nc, st, name, 0, start).sem

        idf = sb("m_idf", [P, P])
        stats, mv = sb("m_stats", [P, TILES, 6]), sb("m_mv", [P, TILES, 2])
        std, rstd = sb("m_std", [P, TILES]), sb("m_rstd", [P, TILES])
        x1t = sb("m_x1t", [P, C, TOK])
        xt = sb("m_xt", [P, 2, C, TOK], F32R)
        wraw = sb("m_wraw", [P, C, H2 * HD2])
        w = sb("m_w", [P, 2, C, H2 * HD2], F32R)
        q = sb("m_q", [HD2, 4, 2, HALF], F32R)
        ps_t = [st.enter_context(nc.psum_tensor(f"m_t{i}", [P, BANK], F32)) for i in range(2)]
        ps_q = [st.enter_context(nc.psum_tensor(f"m_q{i}", [P, BANK], F32)) for i in range(4)]

        eye_in, w_in = sem("m_eye_in"), sem("m_w_in")
        w_hi, w_lo = sem("m_w_hi"), sem("m_w_lo")
        stat_done, mean_done, eps_done, std_done, rstd_done, x1_done = (
            sem(f"m_{k}") for k in ("stat_done", "mean_done", "eps_done", "std_done", "rstd_done", "x1_done"))
        turned, xt_hi, xt_f, xt_lo = sem("m_turned"), sem("m_xt_hi"), sem("m_xt_f"), sem("m_xt_lo")
        q_full, q_hi, q_lo = sem("m_q_full"), sem("m_q_hi"), sem("m_q_lo")
        q_out = [sem(f"m_q_out{i}") for i in range(4)]
        out = sem("m_out")

        steps = [(h, n) for h in range(H2) for n in range(NHALF)]
        blk = st.enter_context(nc.Block())

        @blk.sync
        def _(sp):
            sp.dma_start(idf[:], eye).then_inc(eye_in, 16)
            for c in range(C):
                sp.dma_start(wraw[:, c, :], wq[:, c, :]).then_inc(w_in, 16)
            sp.wait_ge(x1_done, TILES)
            sp.dma_start(x1_dram, acc[:]).then_inc(out, 16)
            sp.wait_ge(xt_f, TILES)
            sp.dma_start(x1t_dram, x1t[:]).then_inc(out, 16)
            for k, (h, n) in enumerate(steps):
                sp.wait_ge(q_hi, k + 1)
                sp.wait_ge(q_lo, k + 1)
                for b in range(2):
                    sp.dma_start(q_dram[2 * n + b, h // G2, :, :, h % G2, :], f(q[:, k % 4, :, b * T:(b + 1) * T]))\
                      .then_inc(q_out[k % 4], 16)
            for i in range(4):
                sp.wait_ge(q_out[i], 32 * (len(steps) // 4))
            sp.wait_ge(out, 32)

        @blk.tensor
        def _(pe):
            pe.wait_ge(eye_in, 16)
            for t in range(TILES):
                pe.wait_ge(x1_done, t + 1)
                if t >= 2:
                    pe.wait_ge(xt_f, t - 1)
                for c in range(C):
                    mm = pe.transpose(ps_t[t % 2][:, c * P:(c + 1) * P], acc[:, t, c * P:(c + 1) * P], idf[:])
                mm.then_inc(turned, 1)
            pe.wait_ge(w_hi, C)
            pe.wait_ge(w_lo, C)
            pe.wait_ge(xt_hi, TILES)
            pe.wait_ge(xt_lo, TILES)
            for k, (h, n) in enumerate(steps):
                if k >= 4:
                    pe.wait_ge(q_lo, k - 3)
                i = 0
                for c in range(C):
                    for a, m in PARTS:
                        mm = pe.matmul(ps_q[k % 4][0:HD2, :], w[:, a, c, h * HD2:(h + 1) * HD2],
                                       xt[:, m, c, n * HALF:(n + 1) * HALF], start=i == 0, stop=i == 3 * C - 1)
                        i += 1
                mm.then_inc(q_full, 1)

        @blk.scalar
        def _(act):
            act.wait_ge(eps_done, 1)
            act.activation(std[:], mv[:, :, 1], ACT.Sqrt).then_inc(std_done, 1)
            for c in range(C):
                act.wait_ge(w_in, 16 * C)
                act.activation(w[:, HI, c, :], wraw[:, c, :], ACT.Copy).then_inc(w_hi, 1)
            for t in range(TILES):
                act.wait_ge(turned, t + 1)
                act.activation(x1t[:, :, t * P:(t + 1) * P], ps_t[t % 2][:].rearrange("p (c t) -> p c t", c=C), ACT.Copy)\
                   .then_inc(xt_f, 1)
            for k, (h, n) in enumerate(steps):
                act.wait_ge(q_full, k + 1)
                if k >= 4:
                    act.wait_ge(q_out[k % 4], 32 * (k // 4))
                act.activation(q[:, k % 4, HI, :], ps_q[k % 4][0:HD2, :], ACT.Copy).then_inc(q_hi, 1)

        @blk.vector
        def _(dve):
            for t in range(TILES):
                dve.bn_stats(stats[:, t, :], acc[:, t, :]).then_inc(stat_done, 1)
            for t in range(TILES):
                dve.wait_ge(stat_done, t + 1)
                dve.bn_aggr(mv[:, t, :], stats[:, t, :]).then_inc(mean_done, 1)
            dve.wait_ge(mean_done, TILES)
            dve.tensor_scalar(mv[:, :, 1], mv[:, :, 1], EPS, None, ALU.add).then_inc(eps_done, 1)
            dve.wait_ge(std_done, 1)
            dve.reciprocal(rstd[:], std[:]).then_inc(rstd_done, 1)
            dve.wait_ge(rstd_done, 1)
            for t in range(TILES):
                dve.tensor_scalar(acc[:, t, :], acc[:, t, :], mv[:, t, 0:1], rstd[:, t:t + 1], ALU.subtract, ALU.mult)\
                   .then_inc(x1_done, 1)
            for t in range(TILES):
                at = slice(t * P, (t + 1) * P)
                dve.wait_ge(xt_f, t + 1)
                dve.tensor_copy(xt[:, HI, :, at], x1t[:, :, at]).then_inc(xt_hi, 1)
                dve.wait_ge(xt_hi, t + 1)
                dve.tensor_tensor(xt[:, LO, :, at], x1t[:, :, at], f(xt[:, HI, :, at]), ALU.subtract).then_inc(xt_lo, 1)
            for k, (h, n) in enumerate(steps):
                dve.wait_ge(q_hi, k + 1)
                dve.tensor_tensor(q[:, k % 4, LO, :], ps_q[k % 4][0:HD2, :], f(q[:, k % 4, HI, :]), ALU.subtract)\
                   .then_inc(q_lo, 1)

        @blk.gpsimd
        def _(pool):
            for c in range(C):
                pool.wait_ge(w_hi, c + 1)
                pool.tensor_tensor(w[:, LO, c, :], wraw[:, c, :], f(w[:, HI, c, :]), ALU.subtract).then_inc(w_lo, 1)



CH = 256
CHUNKS = [(i * CH, CH) for i in range(6)] + [(6 * CH, S2 - 6 * CH)]
CHMAX = CHUNKS[-1][1]
TILES_OF_CHUNK = [[2 * i, 2 * i + 1] for i in range(6)] + [[14, 12, 13]]
GROUPS = 2 * KV2
PAIRS = (NT2 + 1) // 2
STEPS = GROUPS * PAIRS
MAXW = ((0, 2 * BANK), (2 * BANK, S2 - 2 * BANK))


def projections():
    s = []
    for j in range(len(CHUNKS)):
        s += [("k", j, kv) for kv in range(KV2)] + [("v", j, t) for t in TILES_OF_CHUNK[j]]
    return s


def schedule_b():
    s = []
    proj = projections()
    last_v = [p for p in proj if p[0] == "v" and p[1] == len(CHUNKS) - 1]
    s += [("proj", k) for k, p in enumerate(proj) if p not in last_v]
    maxes = [("max", 0, i) for i in range(8)]
    for p in last_v:
        s += maxes[:2] + [("proj", proj.index(p))]
        maxes = maxes[2:]
    s += maxes + [("row", 0)]
    for k in range(STEPS):
        g, j = divmod(k, PAIRS)
        more = g + 1 < GROUPS
        if more and j == 0:
            s += [("max", g + 1, 0)]
        if more and j == PAIRS - 1:
            s += [("row", g + 1)]
        s += [("scores", k)]
        if more and j < PAIRS - 1:
            s += [("max", g + 1, j + 1)]
        if k >= 2:
            s += [("pv", k - 2)]
        if g and j == 3:
            s += [("sums", g - 1)]
        if g and j == 4:
            s += [("spread", g - 1)]
    return s + [("pv", STEPS - 2), ("pv", STEPS - 1), ("sums", GROUPS - 1), ("spread", GROUPS - 1)]


def cross_attention(nc, ctx_t, wk, wv, eye, x1t_dram, q_dram, y_dram):
    sched = schedule_b()
    proj = projections()
    NP = len(proj)
    NCH = len(CHUNKS)

    with ExitStack() as st:
        def sb(name, shape, dt=F32):
            return st.enter_context(nc.sbuf_tensor(name, shape, dt))

        def sem(name, per=0, start=0):
            return Sem(nc, st, name, per, start)

        kt = sb("b_kt", [ROWB + 1, 2, KV2, S2], F32R)
        v = sb("b_v", [P, 2, NT2, KV2, HD2 + 1], F32R)
        w_k, w_v = sb("b_wk", [P, 2, C, KV2 * HD2], F32R), sb("b_wv", [P, 2, C, KV2 * HD2], F32R)
        q = sb("b_q", [ROWB + 1, 2, 2, G2 * T], F32R)
        hraw = sb("b_hraw", [P, C, CHMAX])
        hid = sb("b_hid", [P, 2, 2, C, CHMAX], F32R)
        pf = sb("b_pf", [P, 2, 2 * BANK])
        pr = sb("b_pr", [P, 2, 2, 2 * BANK], F32R)
        o = sb("b_o", [HD2 + 1, BANK])
        yf = sb("b_yf", [HD2, BANK])
        y = sb("b_y", [HD2, 2, BANK], F32R)
        mx = sb("b_mx", [P, 2, 4, 2])
        neg = sb("b_neg", [P, 2, 4], F32R)
        rec = sb("b_rec", [P, 4])
        idf, idr = sb("b_idf", [P, P]), sb("b_idr", [P, P], F32R)

        ps_s = [st.enter_context(nc.psum_tensor(f"b_s{i}", [P, 2 * BANK], F32)) for i in range(2)]
        ps_m = st.enter_context(nc.psum_tensor("b_m", [P, 2 * BANK], F32))
        ps_o = st.enter_context(nc.psum_tensor("b_o_ps", [P, BANK], F32))
        ps_x = st.enter_context(nc.psum_tensor("b_x", [P, BANK], F32))

        w_in, eye_in = sem("b_w_in"), sem("b_eye_in")
        w_hi, w_lo, const_made = sem("b_w_hi"), sem("b_w_lo"), sem("b_const_made")
        h_in = sem("b_h_in", 16 * NCH + 16)
        h_hi, h_lo = sem("b_h_hi", NCH), sem("b_h_lo", NCH * C, 1)
        q_in = [sem(f"b_q_in{i}", 32) for i in range(2)]
        full, kv_hi, kv_lo = sem("b_full", NP), sem("b_kv_hi", NP), sem("b_kv_lo", NP)
        m_full, mx_made = sem("b_m_full", 8 * GROUPS), sem("b_mx_made", 8 * GROUPS, 1)
        neg_made, row_full, row_made = sem("b_neg_made", GROUPS), sem("b_row_full", GROUPS), sem("b_row_made", GROUPS)
        s_made, exp_done = sem("b_s_made", STEPS, 40), sem("b_exp_done", STEPS, 2)
        p_hi, p_lo, pv_done = sem("b_p_hi", STEPS), sem("b_p_lo", STEPS, 2), sem("b_pv_done", STEPS)
        o_out, sums, recips, spread = sem("b_o_out", GROUPS, 1), sem("b_sums", GROUPS), sem("b_recips", GROUPS), sem("b_spread", GROUPS)
        y_made, y_hi, y_lo = sem("b_y_made", GROUPS, 1), sem("b_y_hi", GROUPS), sem("b_y_lo", GROUPS, 1)
        y_out = sem("b_y_out", 16 * GROUPS, 16)
        held = sem("b_held")

        blk = st.enter_context(nc.Block())

        def bank_of(k):
            s = ps_s[(k % 4) // 2]
            return s[:, (k % 2) * BANK:(k % 2 + 1) * BANK]

        def keys_of(k):
            j = k % PAIRS
            return [(i, 2 * j + i) for i in range(2) if 2 * j + i < NT2]

        def shape_of(k):
            tiles = keys_of(k)
            return KT2[tiles[-1][1]][1], BANK * len(tiles)

        def w_stage(c):
            n = KV2 * HD2
            return pf[:].rearrange("p a b -> p (a b)")[:, c * n:(c + 1) * n]

        def split_hidden(act, b, j):
            n = CHUNKS[j][1]
            act.wait_ge(h_in.sem, h_in.at(b, 16 * (j + 1) + (16 if j == NCH - 1 else 0)))
            if j >= 2:
                act.wait_ge(full.sem, full.at(b, max(k for k, p in enumerate(proj) if p[1] == j - 2) + 1))
            act.activation(hid[:, j % 2, HI, :, 0:n], hraw[:, :, 0:n], ACT.Copy).then_inc(h_hi.sem, 1)

        @blk.sync
        def _(sp):
            sp.dma_start(idf[:], eye).then_inc(eye_in.sem, 16)
            for i, src in enumerate((wk, wv)):
                if i:
                    sp.wait_ge(w_lo.sem, C)
                sp.dma_start(pf[:].rearrange("p a b -> p (a b)")[:, 0:C * KV2 * HD2], src).then_inc(w_in.sem, 16)
            for b in range(B):
                for j, (c0, n) in enumerate(CHUNKS):
                    sp.wait_ge(h_lo.sem, h_lo.at(b, j * C))
                    own = min(n, CTXP - c0)
                    sp.dma_start(hraw[:, :, 0:own],
                                 ctx_t[b, :, :, c0:c0 + own]).then_inc(h_in.sem, 16)
                    if own < n:
                        sp.dma_start(hraw[:, :, own:n], x1t_dram[:, :, b * T:(b + 1) * T]).then_inc(h_in.sem, 16)
                for kv in range(2):
                    sp.wait_ge(s_made.sem, s_made.at(b, (kv - 1) * 2 * PAIRS))
                    sp.dma_start(f(q[0:HD2, kv]), q_dram[b, kv].rearrange("d r h t -> d r (h t)"))\
                      .then_inc(q_in[kv].sem, 16)
                for g in range(GROUPS):
                    sp.wait_ge(y_lo.sem, y_lo.at(b, g + 1))
                    sp.wait_ge(y_hi.sem, y_hi.at(b, g + 1))
                    sp.dma_start(y_dram[:, :, 2 * g:2 * g + 2, b * T:(b + 1) * T],
                                 f(y[:]).rearrange("d r (h t) -> d r h t", h=2)).then_inc(y_out.sem, 16)
                    if g in (1, 3):
                        kv = (g - 1) // 2 + 2
                        sp.wait_ge(s_made.sem, s_made.at(b, (g + 1) * PAIRS))
                        sp.dma_start(f(q[0:HD2, kv % 2]),
                                     q_dram[b, kv].rearrange("d r h t -> d r (h t)"))\
                          .then_inc(q_in[kv % 2].sem, 16)
            sp.wait_ge(y_out.sem, y_out.at(B - 1, 16 * GROUPS))

        @blk.tensor
        def _(pe):
            pe.wait_ge(w_hi.sem, 2 * C)
            pe.wait_ge(w_lo.sem, 2 * C)
            pe.wait_ge(const_made.sem, 8)

            def project(k, b):
                kind, j, i = proj[k]
                c0, n = CHUNKS[j]
                if (kind, i) == ("k", 0):
                    pe.wait_ge(h_hi.sem, h_hi.at(b, j + 1))
                    pe.wait_ge(h_lo.sem, h_lo.at(b, (j + 1) * C))
                if k >= 4:
                    pe.wait_ge(kv_lo.sem, kv_lo.at(b, k - 3))
                else:
                    pe.wait_ge(exp_done.sem, exp_done.at(b, 0))
                bank, s = bank_of(k), 0
                for c in range(C):
                    for a, m in PARTS:
                        if kind == "k":
                            mm = pe.matmul(bank[0:HD2, 0:n], w_k[:, a, c, i * HD2:(i + 1) * HD2],
                                           hid[:, j % 2, m, c, 0:n], start=s == 0, stop=s == 3 * C - 1)
                        else:
                            t0, rows = KT2[i]
                            mm = pe.matmul(bank[0:rows, 0:KV2 * HD2], hid[:, j % 2, a, c, t0 - c0:t0 - c0 + rows],
                                           w_v[:, m, c, :], start=s == 0, stop=s == 3 * C - 1)
                        s += 1
                mm.then_inc(full.sem, 1)

            def coarse(g, i, b):
                kv, hp = divmod(g, 2)
                t, half = divmod(i, 2)
                if g == 0 and i == 0:
                    pe.wait_ge(kv_hi.sem, kv_hi.at(b, proj.index(("k", NCH - 1, KV2 - 1)) + 1))
                if hp == 0 and i == 0:
                    pe.wait_ge(q_in[kv % 2].sem, q_in[kv % 2].at(b, 16 * (kv // 2 + 1)))
                pe.wait_ge(mx_made.sem, mx_made.at(b, 8 * g + i))
                c0, n = MAXW[half]
                for x in range(0, n, BANK):
                    mm = pe.matmul(ps_m[:, x:min(x + BANK, n)], q[0:HD2, kv % 2, HI, hp * BANK + t * P:hp * BANK + (t + 1) * P],
                                   kt[0:HD2, HI, kv, c0 + x:c0 + min(x + BANK, n)], start=True, stop=True)
                mm.then_inc(m_full.sem, 1)

            def shift_row(g, b):
                pe.wait_ge(neg_made.sem, neg_made.at(b, g + 1))
                pe.wait_ge(y_made.sem, y_made.at(b, max(g - 1, 0)))
                if g:
                    pe.wait_ge(row_made.sem, row_made.at(b, g))
                for t in range(4):
                    mm = pe.transpose(ps_x[0:1, t * P:(t + 1) * P].bitcast(F32R), neg[:, g % 2, t:t + 1], idr[:])
                mm.then_inc(row_full.sem, 1)

            def scores(k, b):
                g = k // PAIRS
                kv, hp = divmod(g, 2)
                if k == 0:
                    pe.wait_ge(kv_lo.sem, kv_lo.at(b, NP))
                if k % PAIRS == 0:
                    pe.wait_ge(row_made.sem, row_made.at(b, g + 1))
                pe.wait_ge(exp_done.sem, exp_done.at(b, k - 1))
                for i, t in keys_of(k):
                    t0, rows = KT2[t]
                    for s, (a, m) in enumerate(PARTS):
                        mm = pe.matmul(ps_s[k % 2][0:rows, i * BANK:(i + 1) * BANK], kt[:, a, kv, t0:t0 + rows],
                                       q[:, kv % 2, m, hp * BANK:(hp + 1) * BANK], start=s == 0, stop=s == 2)
                mm.then_inc(s_made.sem, 1)

            def values(k, b):
                g, j = divmod(k, PAIRS)
                pe.wait_ge(p_hi.sem, p_hi.at(b, k + 1))
                pe.wait_ge(p_lo.sem, p_lo.at(b, k + 1))
                if j == 0:
                    pe.wait_ge(o_out.sem, o_out.at(b, g))
                for i, t in keys_of(k):
                    rows = KT2[t][1]
                    for s, (a, m) in enumerate(PARTS):
                        mm = pe.matmul(ps_o[0:HD2 + 1, :], v[0:rows, a, t, g // 2, :],
                                       pr[0:rows, k % 2, m, i * BANK:(i + 1) * BANK],
                                       start=t == 0 and s == 0, stop=t == NT2 - 1 and s == 2)
                mm.then_inc(pv_done.sem, 1)

            def sum_columns(g, b):
                pe.wait_ge(o_out.sem, o_out.at(b, g + 1))
                pe.wait_ge(row_made.sem, row_made.at(b, min(g + 2, GROUPS)))
                pe.sem_inc(held.sem, 1)
                for t in range(4):
                    mm = pe.transpose(ps_x[:, t:t + 1], o[HD2:HD2 + 1, t * P:(t + 1) * P], idf[HD2:HD2 + 1, HD2:HD2 + 1])
                mm.then_inc(sums.sem, 1)

            def spread_recips(g, b):
                pe.wait_ge(recips.sem, recips.at(b, g + 1))
                for t in range(4):
                    mm = pe.matmul(ps_x[0:HD2, t * P:(t + 1) * P], rec[:, t:t + 1].to_broadcast([P, HD2]), idf[:],
                                   start=True, stop=True)
                mm.then_inc(spread.sem, 1)

            with pe.Fori(0, B) as b:
                for kind, *arg in sched:
                    {"proj": project, "max": coarse, "row": shift_row, "scores": scores, "pv": values,
                     "sums": sum_columns, "spread": spread_recips}[kind](*arg, b)

        @blk.scalar
        def _(act):
            act.sem_inc(exp_done.sem, 2)
            act.sem_inc(o_out.sem, 1)
            for i, wt in enumerate((w_k, w_v)):
                act.wait_ge(w_in.sem, 16 * (i + 1))
                for c in range(C):
                    act.activation(wt[:, HI, c, :], w_stage(c), ACT.Copy).then_inc(w_hi.sem, 1)
            with act.Fori(0, B) as b:
                for kind, *arg in sched:
                    if kind == "proj":
                        k = arg[0]
                        what, j, i = proj[k]
                        c0, n = CHUNKS[j]
                        if (what, i) == ("k", 0):
                            if j == 0:
                                split_hidden(act, b, 0)
                            if j + 1 < NCH:
                                split_hidden(act, b, j + 1)
                        act.wait_ge(full.sem, full.at(b, k + 1))
                        if what == "k":
                            act.activation(kt[0:HD2, HI, i, c0:c0 + n], bank_of(k)[0:HD2, 0:n], ACT.Copy).then_inc(kv_hi.sem, 1)
                        else:
                            rows = KT2[i][1]
                            act.activation(v[0:rows, HI, i, :, 0:HD2],
                                           bank_of(k)[0:rows, 0:KV2 * HD2].rearrange("p (h d) -> p h d", h=KV2), ACT.Copy)\
                               .then_inc(kv_hi.sem, 1)
                    elif kind == "row":
                        g = arg[0]
                        kv, hp = divmod(g, 2)
                        act.wait_ge(row_full.sem, row_full.at(b, g + 1))
                        act.activation(q[ROWB:ROWB + 1, kv % 2, HI, hp * BANK:(hp + 1) * BANK], ps_x[0:1, :], ACT.Copy)\
                           .then_inc(row_made.sem, 1)
                    elif kind == "scores":
                        k = arg[0]
                        rows, n = shape_of(k)
                        act.wait_ge(s_made.sem, s_made.at(b, k + 1))
                        act.wait_ge(p_lo.sem, p_lo.at(b, k - 1))
                        act.activation(pf[0:rows, k % 2, 0:n], ps_s[k % 2][0:rows, 0:n], ACT.Exp, scale=SCALE_B)\
                           .then_inc(exp_done.sem, 1)
                        act.wait_ge(exp_done.sem, exp_done.at(b, k + 1))
                        if k >= 2:
                            act.wait_ge(pv_done.sem, pv_done.at(b, k - 1))
                        act.activation(pr[0:rows, k % 2, HI, 0:n], pf[0:rows, k % 2, 0:n], ACT.Copy).then_inc(p_hi.sem, 1)
                    elif kind == "pv" and arg[0] % PAIRS == PAIRS - 1:
                        k = arg[0]
                        g = k // PAIRS
                        act.wait_ge(pv_done.sem, pv_done.at(b, k + 1))
                        act.wait_ge(y_made.sem, y_made.at(b, g))
                        act.activation(o[:], ps_o[0:HD2 + 1, :], ACT.Copy).then_inc(o_out.sem, 1)

        @blk.vector
        def _(dve):
            dve.sem_inc(mx_made.sem, 1)
            dve.sem_inc(p_lo.sem, 2)
            dve.sem_inc(y_made.sem, 1)
            for ap, value in ((v[:, HI, :, :, HD2], 1.0), (v[:, LO, :, :, HD2], 0.0), (kt[ROWB:ROWB + 1, HI], 1.0),
                              (kt[ROWB:ROWB + 1, LO], 0.0), (q[ROWB:ROWB + 1, 0, LO], 0.0), (q[ROWB:ROWB + 1, 1, LO], 0.0)):
                dve.memset(f(ap), value).then_inc(const_made.sem, 1)
            dve.wait_ge(eye_in.sem, 16)
            dve.tensor_copy(idr[:], idf[:]).then_inc(const_made.sem, 2)
            with dve.Fori(0, B) as b:
                for kind, *arg in sched:
                    if kind == "proj":
                        k = arg[0]
                        what, j, i = proj[k]
                        c0, n = CHUNKS[j]
                        dve.wait_ge(kv_hi.sem, kv_hi.at(b, k + 1))
                        if what == "k":
                            dve.tensor_tensor(kt[0:HD2, LO, i, c0:c0 + n], bank_of(k)[0:HD2, 0:n],
                                              f(kt[0:HD2, HI, i, c0:c0 + n]), ALU.subtract).then_inc(kv_lo.sem, 1)
                        else:
                            rows = KT2[i][1]
                            dve.tensor_tensor(v[0:rows, LO, i, :, 0:HD2],
                                              bank_of(k)[0:rows, 0:KV2 * HD2].rearrange("p (h d) -> p h d", h=KV2),
                                              f(v[0:rows, HI, i, :, 0:HD2]), ALU.subtract).then_inc(kv_lo.sem, 1)
                    elif kind == "max":
                        g, i = arg
                        t, half = divmod(i, 2)
                        dve.wait_ge(m_full.sem, m_full.at(b, 8 * g + i + 1))
                        dve.reduce_max(mx[:, g % 2, t, half:half + 1], ps_m[:, 0:MAXW[half][1]], X).then_inc(mx_made.sem, 1)
                        if i == 7:
                            dve.wait_ge(mx_made.sem, mx_made.at(b, 8 * g + 8))
                            dve.reduce_max(neg[:, g % 2, :], mx[:, g % 2], X, negate=True).then_inc(neg_made.sem, 1)
                    elif kind == "scores":
                        k = arg[0]
                        rows, n = shape_of(k)
                        dve.wait_ge(p_hi.sem, p_hi.at(b, k + 1))
                        dve.tensor_tensor(pr[0:rows, k % 2, LO, 0:n], pf[0:rows, k % 2, 0:n], f(pr[0:rows, k % 2, HI, 0:n]),
                                          ALU.subtract).then_inc(p_lo.sem, 1)
                    elif kind == "sums":
                        g = arg[0]
                        dve.wait_ge(sums.sem, sums.at(b, g + 1))
                        dve.reciprocal(rec[:], ps_x[:, 0:4]).then_inc(recips.sem, 1)
                    elif kind == "spread":
                        g = arg[0]
                        dve.wait_ge(spread.sem, spread.at(b, g + 1))
                        dve.wait_ge(y_lo.sem, y_lo.at(b, g))
                        dve.tensor_tensor(yf[:], ps_x[0:HD2, :], o[0:HD2, :], ALU.mult).then_inc(y_made.sem, 1)
                        dve.wait_ge(y_made.sem, y_made.at(b, g + 1))
                        dve.wait_ge(y_out.sem, y_out.at(b, 16 * g))
                        dve.tensor_copy(y[:, HI, :], yf[:]).then_inc(y_hi.sem, 1)

        @blk.gpsimd
        def _(pool):
            pool.sem_inc(h_lo.sem, 1)
            pool.sem_inc(y_lo.sem, 1)
            pool.sem_inc(s_made.sem, 40)
            pool.sem_inc(y_out.sem, 16)
            for i, wt in enumerate((w_k, w_v)):
                for c in range(C):
                    pool.wait_ge(w_hi.sem, i * C + c + 1)
                    pool.tensor_tensor(wt[:, LO, c, :], w_stage(c), f(wt[:, HI, c, :]), ALU.subtract).then_inc(w_lo.sem, 1)
            with pool.Fori(0, B) as b:
                for j, (c0, n) in enumerate(CHUNKS):
                    pool.wait_ge(h_hi.sem, h_hi.at(b, j + 1))
                    for c in range(C):
                        pool.tensor_tensor(hid[:, j % 2, LO, c, 0:n], hraw[:, c, 0:n], f(hid[:, j % 2, HI, c, 0:n]),
                                           ALU.subtract).then_inc(h_lo.sem, 1)
                for g in range(GROUPS):
                    pool.wait_ge(y_hi.sem, y_hi.at(b, g + 1))
                    pool.tensor_tensor(y[:, LO, :], yf[:], f(y[:, HI, :]), ALU.subtract).then_inc(y_lo.sem, 1)



def finish(nc, wo, w_t, lora_a, lora_bt, lora_w, bias, eye, x1_dram, y_dram, out_dram):
    NRK = 128
    ALPHA_OVER_RANK = 2.0
    with ExitStack() as st:
        def sb(name, shape, dt=F32):
            return st.enter_context(nc.sbuf_tensor(name, shape, dt))

        def sem(name):
            return st.enter_context(nc.semaphore(name))

        x1 = sb("c_x1", [P, TILES, D])
        y = sb("c_y", [HD2, 2, 2, H2, T], F32R)
        woraw = sb("c_woraw", [HD2, 4, D])
        wo_s = sb("c_wo", [HD2, 2, H2, D], F32R)
        wt, la = sb("c_wt", [P, C, D]), sb("c_la", [NRK, D])
        lb, lw, bias_s, idf = sb("c_lb", [NRK, D]), sb("c_lw", [NRK, 1]), sb("c_bias", [P, D]), sb("c_idf", [P, P])
        ws = sb("c_ws", [P, 2, C, D], F32R)
        x2 = sb("c_x2", [P, 2, D])
        x2t = sb("c_x2t", [P, 2, D], F32R)
        z = sb("c_z", [P, 2, D])
        stats, mv = sb("c_stats", [P, 2, 6]), sb("c_mv", [P, 2, 2])
        std, rstd = sb("c_std", [P, 2]), sb("c_rstd", [P, 2])
        ps_w = [st.enter_context(nc.psum_tensor(f"c_w{i}", [P, BANK], F32)) for i in range(2)]
        ps_y = [st.enter_context(nc.psum_tensor(f"c_y{i}", [P, BANK], F32)) for i in range(2)]
        ps_t, ps_f = (st.enter_context(nc.psum_tensor(f"c_{k}_ps", [P, BANK], F32)) for k in "tf")

        names = ("small_in wt_in wo_in lb_done w_full w_sum w_hi w_lo wo_hi wo_lo x1_in y_full turned t_hi t_lo "
                 "f_full z_done stat_done mean_done eps_done std_done rstd_done normed biased").split()
        (small_in, wt_in, wo_in, lb_done, w_full, w_sum, w_hi, w_lo, wo_hi, wo_lo, x1_in, y_full, turned, t_hi, t_lo,
         f_full, z_done, stat_done, mean_done, eps_done, std_done, rstd_done, normed, biased) = (
            sem(f"c_{n}") for n in names)
        out_done = [sem(f"c_out_done{i}") for i in range(2)]
        y_in = [sem(f"c_y_in{i}") for i in range(2)]

        norms = []
        for t in range(TILES + 1):
            norms += [(t, 0)] * (t < TILES) + [(t - 1, 1)] * (t >= 1)
        nth = {x: i for i, x in enumerate(norms)}
        blk = st.enter_context(nc.Block())

        @blk.sync
        def _(sp):
            for h in range(4):
                if h:
                    sp.wait_ge(wo_lo, 4 * h)
                sp.dma_start(woraw[:], wo[:, 4 * h:4 * h + 4, :]).then_inc(wo_in, 16)
                if h == 0:
                    for dst, src in ((la, lora_a), (lb, lora_bt), (lw, lora_w), (idf, eye)):
                        sp.dma_start(dst[:], src).then_inc(small_in, 16)
                    sp.dma_start(wt[:], w_t).then_inc(wt_in, 16)
                    sp.dma_start(bias_s[:], bias.to_broadcast([P, D])).then_inc(small_in, 16)
                    sp.dma_start(x1[:], x1_dram).then_inc(x1_in, 16)
                if h < 2:
                    sp.dma_start(f(y[:, h]), y_dram[:, :, :, h * T:(h + 1) * T]).then_inc(y_in[h], 16)
            for b in range(2, B):
                sp.wait_ge(y_full, 2 * (b - 1))
                sp.dma_start(f(y[:, b % 2]), y_dram[:, :, :, b * T:(b + 1) * T]).then_inc(y_in[b % 2], 16)
            for t in range(TILES):
                sp.wait_ge(normed, nth[(t, 1)] + 1)
                sp.dma_start(out_dram[t * P:(t + 1) * P, :], z[:, t % 2, :]).then_inc(out_done[t % 2], 16)
            for i in range(2):
                sp.wait_ge(out_done[i], 16 * (TILES // 2))

        @blk.tensor
        def _(pe):
            pe.wait_ge(small_in, 80)
            pe.wait_ge(lb_done, 1)
            for c in range(C):
                if c >= 2:
                    pe.wait_ge(w_sum, c - 1)
                pe.matmul(ps_w[c % 2][:], la[:, c * P:(c + 1) * P], lb[:], start=True, stop=True).then_inc(w_full, 1)
            pe.wait_ge(wo_hi, H2)
            pe.wait_ge(wo_lo, H2)

            def project(t):
                b = t // 2
                pe.wait_ge(y_in[b % 2], 16 * (b // 2 + 1))
                if t >= 2:
                    pe.wait_ge(z_done, nth[(t - 2, 0)] + 1)
                i = 0
                for h in range(H2):
                    for a, m in PARTS:
                        mm = pe.matmul(ps_y[t % 2][:], y[:, b % 2, a, h, (t % 2) * P:(t % 2 + 1) * P], wo_s[:, m, h, :],
                                       start=i == 0, stop=i == 3 * H2 - 1)
                        i += 1
                mm.then_inc(y_full, 1)

            def turn(t):
                pe.wait_ge(normed, nth[(t, 0)] + 1)
                if t:
                    pe.wait_ge(t_lo, t)
                for c in range(C):
                    mm = pe.transpose(ps_t[:, c * P:(c + 1) * P], x2[:, t % 2, c * P:(c + 1) * P], idf[:])
                mm.then_inc(turned, 1)

            def feed(t):
                pe.wait_ge(t_hi, t + 1)
                pe.wait_ge(t_lo, t + 1)
                pe.wait_ge(w_hi, C)
                pe.wait_ge(w_lo, C)
                if t:
                    pe.wait_ge(z_done, nth[(t - 1, 1)] + 1)
                i = 0
                for c in range(C):
                    for a, m in PARTS:
                        mm = pe.matmul(ps_f[:], x2t[:, a, c * P:(c + 1) * P], ws[:, m, c, :], start=i == 0, stop=i == 3 * C - 1)
                        i += 1
                mm.then_inc(f_full, 1)

            for t in range(TILES + 1):
                if t < TILES:
                    project(t)
                if t >= 1:
                    turn(t - 1)
                    feed(t - 1)

        @blk.scalar
        def _(act):
            for h in range(H2):
                act.wait_ge(wo_in, 16 * (h // 4 + 1))
                act.activation(wo_s[:, HI, h, :], woraw[:, h % 4, :], ACT.Copy).then_inc(wo_hi, 1)
            for c in range(C):
                act.wait_ge(w_sum, c + 1)
                act.activation(ws[:, HI, c, :], wt[:, c, :], ACT.Copy).then_inc(w_hi, 1)
            for i, (t, which) in enumerate(norms):
                act.wait_ge(eps_done, i + 1)
                act.activation(std[:, i % 2:i % 2 + 1], mv[:, i % 2, 1:2], ACT.Sqrt).then_inc(std_done, 1)
                if which == 0:
                    act.wait_ge(turned, t + 1)
                    if t:
                        act.wait_ge(f_full, t)
                    act.activation(x2t[:, HI, :], ps_t[:], ACT.Copy).then_inc(t_hi, 1)

        @blk.vector
        def _(dve):
            dve.wait_ge(small_in, 80)
            dve.tensor_scalar(lb[:], lb[:], lw[:, 0:1], ALPHA_OVER_RANK, ALU.mult, ALU.mult).then_inc(lb_done, 1)
            dve.wait_ge(wt_in, 16)
            for c in range(C):
                dve.wait_ge(w_full, c + 1)
                dve.tensor_tensor(wt[:, c, :], ps_w[c % 2][:], wt[:, c, :], ALU.add).then_inc(w_sum, 1)
            dve.wait_ge(x1_in, 16)
            for i, (t, which) in enumerate(norms):
                s = i % 2
                if which == 0:
                    dve.wait_ge(y_full, t + 1)
                    dve.tensor_tensor(x2[:, t % 2, :], ps_y[t % 2][:], x1[:, t, :], ALU.add).then_inc(z_done, 1)
                    row = x2[:, t % 2, :]
                else:
                    dve.wait_ge(turned, t + 1)
                    dve.tensor_tensor(x2[:, t % 2, :], x2[:, t % 2, :], bias_s[:], ALU.add).then_inc(biased, 1)
                    dve.wait_ge(t_hi, t + 1)
                    dve.tensor_tensor(x2t[:, LO, :], ps_t[:], f(x2t[:, HI, :]), ALU.subtract).then_inc(t_lo, 1)
                    dve.wait_ge(f_full, t + 1)
                    dve.wait_ge(biased, t + 1)
                    if t >= 2:
                        dve.wait_ge(out_done[t % 2], 16 * (t // 2))
                    dve.tensor_tensor(z[:, t % 2, :], ps_f[:], x2[:, t % 2, :], ALU.add).then_inc(z_done, 1)
                    row = z[:, t % 2, :]
                dve.wait_ge(z_done, i + 1)
                dve.bn_stats(stats[:, s, :], row).then_inc(stat_done, 1)
                dve.wait_ge(stat_done, i + 1)
                dve.bn_aggr(mv[:, s, :], stats[:, s, :]).then_inc(mean_done, 1)
                dve.wait_ge(mean_done, i + 1)
                dve.tensor_scalar(mv[:, s, 1:2], mv[:, s, 1:2], EPS, None, ALU.add).then_inc(eps_done, 1)
                dve.wait_ge(std_done, i + 1)
                dve.reciprocal(rstd[:, s:s + 1], std[:, s:s + 1]).then_inc(rstd_done, 1)
                dve.wait_ge(rstd_done, i + 1)
                dve.tensor_scalar(row, row, mv[:, s, 0:1], rstd[:, s:s + 1], ALU.subtract, ALU.mult).then_inc(normed, 1)

        @blk.gpsimd
        def _(pool):
            for h in range(H2):
                pool.wait_ge(wo_hi, h + 1)
                pool.tensor_tensor(wo_s[:, LO, h, :], woraw[:, h % 4, :], f(wo_s[:, HI, h, :]), ALU.subtract).then_inc(wo_lo, 1)
            for c in range(C):
                pool.wait_ge(w_hi, c + 1)
                pool.tensor_tensor(ws[:, LO, c, :], wt[:, c, :], f(ws[:, HI, c, :]), ALU.subtract).then_inc(w_lo, 1)



def program(nc, x_t, x_rows, w_qkv, w_o, cos_t, sin_t, mask, eye, ctx_t, wq, wk, wv, wo2, w_t, lora_a, lora_bt,
            lora_w, bias, out):
    x1_dram = nc.dram_tensor("x1_rows", [P, TILES, D], F32).ap()
    x1t_dram = nc.dram_tensor("x1_t", [P, C, TOK], F32).ap()
    q_dram = nc.dram_tensor("queries", [B, KV2, HD2, 2, G2, T], F32).ap()
    y_dram = nc.dram_tensor("attended", [HD2, 2, H2, TOK], F32).ap()
    with ExitStack() as st:
        acc = st.enter_context(nc.sbuf_tensor("acc", [P, TILES, D], F32))
        self_attention(nc, x_t, x_rows, w_qkv, w_o, cos_t, sin_t, mask, eye, acc)
        between(nc, eye, wq, acc, x1_dram, x1t_dram, q_dram)
    cross_attention(nc, ctx_t, wk, wv, eye, x1t_dram, q_dram, y_dram)
    finish(nc, wo2, w_t, lora_a, lora_bt, lora_w, bias, eye, x1_dram, y_dram, out)


def kernel(x, ctx_4096, L0_attn_w_qkv, L0_attn_w_o, L0_xattn_Wq, L0_xattn_Wk, L0_xattn_Wv, L0_xattn_Wo,
           L0_ffn_lora_A, L0_ffn_lora_B, L0_ffn_W, L0_ffn_bias, L0_ffn_lora_weights):
    import concourse.bacc as bacc
    from concourse.bass_utils import run_bass_kernel_spmd

    def chunked(w):
        return w.reshape(C, P, -1).transpose(1, 0, 2)

    x, ctx = np.asarray(x), np.asarray(ctx_4096)
    rows = x.reshape(TOK, D)
    w = np.asarray(L0_attn_w_qkv).reshape(C, P, -1)
    q_cols, kv_cols = KVH * GRP * HD, KVH * HD
    w = np.concatenate([w[:, :, :q_cols].reshape(C, P, KVH, GRP * HD),
                        w[:, :, q_cols:q_cols + kv_cols].reshape(C, P, KVH, HD),
                        w[:, :, q_cols + kv_cols:].reshape(C, P, KVH, HD)], axis=-1)
    inv = (1.0 / np.power(np.float32(10000.0), np.arange(0, HD, 2, dtype=np.float32) / np.float32(HD))).astype(np.float32)
    angle = (np.arange(T, dtype=np.float32)[None, :] * inv[:, None]).astype(np.float32)
    cos, sin = np.cos(angle), np.sin(angle)
    keys, queries = np.arange(T)[None, None, :], np.arange(P)[:, None, None] + P * np.arange(2)[None, :, None]
    arrays = {
        "x_t": chunked(rows.T),
        "x_rows": rows.reshape(TILES, P, D).transpose(1, 0, 2),
        "w_qkv": w.transpose(2, 1, 0, 3),
        "w_o": np.asarray(L0_attn_w_o).reshape(KVH, GRP, HD, D).transpose(0, 2, 1, 3),
        "cos_t": np.tile(np.concatenate([cos, cos]), (1, HALF // T)),
        "sin_t": np.tile(np.concatenate([-sin, sin]), (1, HALF // T)),
        "mask": np.where(keys <= queries, 0.0, NEG).astype(np.float32),
        "eye": np.eye(P, dtype=np.float32),
        "ctx_t": np.concatenate([ctx, ctx[:, -1:]], axis=1).reshape(B, CTXP, C, P).transpose(0, 3, 2, 1),
        "wq": chunked(np.asarray(L0_xattn_Wq).T),
        "wk": chunked(np.asarray(L0_xattn_Wk).T).reshape(P, -1),
        "wv": chunked(np.asarray(L0_xattn_Wv).T).reshape(P, -1),
        "wo2": np.asarray(L0_xattn_Wo).T.reshape(H2, HD2, D).transpose(1, 0, 2),
        "w_t": chunked(np.asarray(L0_ffn_W).T),
        "lora_a": np.asarray(L0_ffn_lora_A).reshape(-1, D),
        "lora_bt": np.asarray(L0_ffn_lora_B).transpose(0, 2, 1).reshape(-1, D),
        "lora_w": np.repeat(np.asarray(L0_ffn_lora_weights), 16).reshape(-1, 1),
        "bias": np.asarray(L0_ffn_bias).reshape(1, D),
    }
    arrays = {k: np.ascontiguousarray(a) for k, a in arrays.items()}
    nc = bacc.Bacc("TRN2", target_bir_lowering=False, num_devices=1)
    aps = {k: nc.dram_tensor(f"in_{k}", a.shape, mybir.dt.from_np(a.dtype), kind="ExternalInput").ap()
           for k, a in arrays.items()}
    out = nc.dram_tensor("out_0", (TOK, D), F32, kind="ExternalOutput").ap()
    program(nc, out=out, **aps)
    r = run_bass_kernel_spmd(nc, [{f"in_{k}": a for k, a in arrays.items()}], core_ids=[0])
    return r.results[0]["out_0"].reshape(B, T, D)
```

```python
from contextlib import ExitStack

import concourse.bass as bass
import numpy as np
from concourse import mybir

F32 = mybir.dt.float32
F32R = mybir.dt.float32r
ALU = mybir.AluOpType
ACT = mybir.ActivationFunctionType
X = mybir.AxisListType.X

P = 128
BANK = 512
HI, LO = 0, 1
PARTS = ((HI, HI), (HI, LO), (LO, HI))
NEG = -1e30

B, T, D = 4, 256, 512
TOK = B * T
C = D // P
TILES = TOK // P
EPS = 1e-5

KVH, GRP, HD = 8, 4, 128
NHALF, HALF = 2, 512
SCALE_A = HD ** -0.5
FEAT_A = (GRP + 2) * HD

CTX, KV2, G2, HD2 = 1601, 4, 4, 96
H2 = KV2 * G2
CTXP = CTX + 1
S2 = CTXP + T
SCALE_B = HD2 ** -0.5
KT2 = [(i * P, P) for i in range(12)] + [(CTXP, P), (CTXP + P, P), (12 * P, CTX - 12 * P)]
NT2 = len(KT2)
CHUNKS2 = [(0, 512), (512, 512), (1024, 512), (1536, S2 - 1536)]
ROWB = HD2


def f(ap):
    return ap.bitcast(F32)


class Sem:

    def __init__(self, nc, stack, name, per=0, start=0):
        self.sem, self.per, self.start = stack.enter_context(nc.semaphore(name)), per, start

    def at(self, g, k):
        return g * self.per + (k + self.start)



TILE_V, TILE_K = GRP + 1, GRP
ROPED = (TILE_K, *range(GRP))
UNITS = 2 * B


def schedule_a(last=False):
    here = lambda *steps: [(s, 0) for s in steps]
    ahead = lambda *steps: [] if last else [(s, 1) for s in steps]
    proj = lambda n, *tiles: [("proj", n, t) for t in tiles]
    mx = lambda b, *heads: [("max", b, h) for h in heads]
    rows = lambda b: [("row", b, 0), ("row", b, 1)]
    wo = lambda b: [("wo", b, 0), ("wo", b, 1)]
    return (
        here(*proj(1, TILE_V), ("scores", 0), ("split_wo", 0), *proj(1, TILE_K), ("split_wo", 1), *mx(1, 0), ("low", 0))
        + here(*proj(1, 0), ("split_wo", 2), *mx(1, 1), ("scores", 1), ("pv", 0), ("split_wo", 3))
        + here(*proj(1, 1), *mx(1, 2), ("low", 1), *proj(1, 2), *mx(1, 3))
        + here(("pv", 1), *proj(1, 3), *rows(1))
        + here(("scores", 2), *wo(0)[:1], ("low", 2), *wo(0)[1:], ("pv", 2), ("scores", 3), *mx(2, 0))
        + ahead(("split_w", 0)) + here(*mx(2, 1, 2), ("low", 3), *mx(2, 3), ("pv", 3), ("vtr", 1)) + ahead(("split_w", 1))
        + here(*rows(2), ("scores", 4), *wo(1)[:1]) + ahead(("split_w", 2)) + here(*mx(3, 0), ("low", 4), *wo(1)[1:])
        + here(*mx(3, 1), ("pv", 4)) + ahead(("split_w", 3)) + here(("scores", 5), *mx(3, 2, 3), ("low", 5))
        + ahead(*proj(0, TILE_V)) + here(*rows(3), ("pv", 5), ("scores", 6)) + ahead(*proj(0, TILE_K)) + here(("low", 6))
        + here(*wo(2)[:1], ("pv", 6), ("scores", 7)) + ahead(*proj(0, 0)) + here(("low", 7)) + ahead(*proj(0, 1))
        + here(*wo(2)[1:], ("pv", 7)) + ahead(("vtr", 0), *proj(0, 2), *mx(0, 0), *proj(0, 3), *mx(0, 1))
        + here(*wo(3)[:1]) + ahead(*mx(0, 2), ) + here(*wo(3)[1:]) + ahead(*mx(0, 3), *rows(0)))


def schedule_a_first():
    return ([(("split_w", c), 0) for c in range(C)] + [(("proj", 0, t), 0) for t in (TILE_V, *ROPED)]
            + [(("vtr", 0), 0)] + [(("max", 0, h), 0) for h in range(GRP)] + [(("row", 0, hp), 0) for hp in range(2)])


RINGED = ("proj", "vtr", "max", "row", "wo")


def self_attention(nc, x_t, x_rows, w_qkv, w_o, cos_t, sin_t, mask, eye, acc):
    first, usual, final = schedule_a_first(), schedule_a(), schedule_a(last=True)
    ringed_first, ringed = ([step for step, _ in s if step[0] in RINGED] for s in (first, usual))
    FIRST, PER = len(ringed_first), len(ringed)
    assert PER % 2 == 0 and ringed_first[-2:] == ringed[-2:]
    NR = len(ROPED)
    RAW = 2 * C

    with ExitStack() as st:
        def sb(name, shape, dt=F32):
            return st.enter_context(nc.sbuf_tensor(name, shape, dt))

        def sem(name, per=0, start=0):
            return Sem(nc, st, name, per, start)

        xt = sb("a_xt", [P, 2, C, TOK], F32R)
        raw = sb("a_raw", [P, 2, FEAT_A])
        w = sb("a_w", [P, 2, C, FEAT_A], F32R)
        wo = sb("a_wo", [P, 2, GRP, D], F32R)
        cos, sin = sb("a_cos", [P, T]), sb("a_sin", [P, T])
        msk = sb("a_mask", [P, 2, T])
        idf, idr = sb("a_idf", [P, P]), sb("a_idr", [P, P], F32R)
        ones = sb("a_ones", [P, P], F32R)
        swapped = sb("a_swapped", [P, 2, HALF])
        roped = sb("a_roped", [P, 2, HALF])
        qk = sb("a_qk", [P, 2, NHALF, GRP + 1, HALF], F32R)
        vt = sb("a_vt", [P, HALF])
        v = sb("a_v", [P, 2, 4, HD], F32R)
        neg = sb("a_neg", [P, B, GRP, 2])
        negr = sb("a_negr", [P, B, GRP, 2], F32R)
        junk = sb("a_junk", [P, 2, T], mybir.dt.bfloat16)
        row = sb("a_row", [1, 2, 2, HALF], F32R)
        pf = sb("a_pf", [P, 2, 3 * T])
        pr = sb("a_pr", [P, 2, 2, 3 * T], F32R)
        rec = sb("a_rec", [P, HALF // 32])
        recs = sb("a_recs", [P, HALF])
        yf = sb("a_yf", [P, 2, HALF])
        y = sb("a_y", [P, 2, 2, GRP, T], F32R)

        ring = [st.enter_context(nc.psum_tensor(f"a_ring{i}", [P, BANK], F32)) for i in range(2)]
        ps_s = [st.enter_context(nc.psum_tensor(f"a_s{i}", [P, 2 * BANK], F32)) for i in range(2)]
        ps_o = st.enter_context(nc.psum_tensor("a_o", [P, BANK], F32))
        ps_l = st.enter_context(nc.psum_tensor("a_l", [P, BANK], F32))

        x_in, consts_in = sem("a_x_in"), sem("a_consts_in")
        x_hi, x_lo, const_made = sem("a_x_hi"), sem("a_x_lo"), sem("a_const_made")
        raw_in = [sem(f"a_raw_in{i}", 16 * RAW // 2) for i in range(2)]
        w_hi, w_lo = sem("a_w_hi", C), sem("a_w_lo", C)
        wo_hi, wo_lo = sem("a_wo_hi", GRP), sem("a_wo_lo", GRP)
        full = sem("a_ring_full", PER, FIRST)
        was_swapped = sem("a_was_swapped", NHALF * NR)
        was_turned = sem("a_was_turned", NHALF * NR)
        was_cos = sem("a_was_cos", NHALF * NR)
        rope_sum = sem("a_rope_sum", NHALF * NR, 2)
        rope_hi, rope_lo = sem("a_rope_hi", NHALF * NR), sem("a_rope_lo", NHALF * NR, 2)
        vt_made, v_hi, v_lo = sem("a_vt_made", NHALF), sem("a_v_hi", NHALF), sem("a_v_lo", NHALF)
        mx_made, neg_made = sem("a_mx_made", 2 * B * GRP), sem("a_neg_made", B)
        row_made = sem("a_row_made", 2 * B)
        s_made, exp_done, masked = sem("a_s_made", UNITS), sem("a_exp_done", UNITS, 2), sem("a_masked", 2 * UNITS)
        p_hi, p_lo, pv_done = sem("a_p_hi", UNITS), sem("a_p_lo", UNITS, 2), sem("a_pv_done", UNITS)
        columns, recips, recs_made = (sem(f"a_{k}", UNITS) for k in ("columns", "recips", "recs_made"))
        y_made, y_hi, y_lo = sem("a_y_made", UNITS, 1), sem("a_y_hi", UNITS), sem("a_y_lo", UNITS, 2)
        acc_done = sem("a_acc_done", 2 * B)
        held = sem("a_held")

        blk = st.enter_context(nc.Block())

        def run(e, handle):
            def part(sched, g0, k):
                for step, ahead in sched:
                    uses = step[0] in RINGED
                    handle(step, g0, ahead, k if uses else None)
                    k += uses

            part(first, 0, -FIRST)
            with e.Fori(0, KVH - 1) as g:
                part(usual, g, 0)
            part(final, KVH - 1, 0)

        def bank_of(k):
            return ring[(k + FIRST) % 2]

        def left(step, g):
            kind = step[0]
            if kind == "proj" and step[2] == TILE_V:
                return vt_made, vt_made.at(g, step[1] + 1)
            if kind == "proj":
                return was_cos, was_cos.at(g, step[1] * NR + ROPED.index(step[2]) + 1)
            if kind == "vtr":
                return v_lo, v_lo.at(g, step[1] + 1)
            if kind == "max":
                return mx_made, mx_made.at(g, 2 * (step[1] * GRP + step[2]) + 2)
            if kind == "row":
                return row_made, row_made.at(g, 2 * step[1] + step[2] + 1)
            return acc_done, acc_done.at(g, 2 * step[1] + step[2] + 1)

        def x_stage(c):
            return (pf, yf, swapped, roped)[c][:].rearrange("p a b -> p (a b)")[:, 0:TOK]

        def raw_slot(g, j):
            s = raw_in[j % 2]
            return raw[:, j % 2, :], s.sem, s.at(g, 16 * (j // 2 + 1))

        @blk.sync
        def _(sp):
            for c in range(C):
                sp.dma_start(x_stage(c), x_t[:, c, :]).then_inc(x_in.sem, 16)
            for g in range(KVH):
                for j in range(RAW):
                    if j >= 2 or g:
                        s, k = (wo_lo, j - RAW // 2 - 1) if j >= RAW // 2 + 2 else (w_lo, j - 1) if j >= 2 else (wo_lo, j - 1)
                        sp.wait_ge(s.sem, s.at(g, k))
                    src, n = (w_qkv[g, :, j, :], FEAT_A) if j < C else (w_o[g, :, j - C, :], D)
                    sp.dma_start(raw[:, j % 2, 0:n], src).then_inc(raw_in[j % 2].sem, 16)
                    if g == 0 and j == 1:
                        for dst, src in ((cos, cos_t), (sin, sin_t), (msk, mask), (idf, eye), (acc, x_rows)):
                            sp.dma_start(dst[:], src).then_inc(consts_in.sem, 16)

        @blk.tensor
        def _(pe):
            pe.wait_ge(x_hi.sem, C)
            pe.wait_ge(x_lo.sem, C)
            pe.wait_ge(const_made.sem, 2)
            pe.wait_ge(consts_in.sem, 80)
            recent = []

            def take(g0, k):
                if k >= 2 - FIRST:
                    before, ahead = (ringed[k - 2], 0) if 0 <= k < 2 else recent[-2]
                    s, value = left(before, g0 + ahead)
                    pe.wait_ge(s.sem, value)
                return bank_of(k)

            def project(step, g, bank):
                _, n, t = step
                if (n, t) == (0, TILE_V):
                    pe.wait_ge(w_hi.sem, w_hi.at(g, C))
                    pe.wait_ge(w_lo.sem, w_lo.at(g, C))
                i = 0
                for c in range(C):
                    for a, m in PARTS:
                        mm = pe.matmul(bank[:], w[:, a, c, t * HD:(t + 1) * HD],
                                       xt[:, m, c, n * HALF:(n + 1) * HALF], start=i == 0, stop=i == 3 * C - 1)
                        i += 1
                mm.then_inc(full.sem, 1)

            def turn_values(step, g, bank):
                pe.wait_ge(vt_made.sem, vt_made.at(g, step[1] + 1))
                for i in range(4):
                    mm = pe.transpose(bank[:, i * P:(i + 1) * P], vt[:, i * P:(i + 1) * P], idf[:])
                mm.then_inc(full.sem, 1)

            def coarse_scores(step, g, bank):
                _, b, h = step
                n, q0 = b // 2, (b % 2) * T
                pe.wait_ge(rope_hi.sem, rope_hi.at(g, n * NR + h + 2))
                for qt in range(2):
                    mm = pe.matmul(bank[:, qt * T:(qt + 1) * T], qk[:, HI, n, 1 + h, q0 + qt * P:q0 + (qt + 1) * P],
                                   qk[:, HI, n, 0, q0:q0 + T], start=True, stop=True)
                mm.then_inc(full.sem, 1)

            def shift_row(step, g, bank):
                _, b, hp = step
                pe.wait_ge(neg_made.sem, neg_made.at(g, b + 1))
                for i in range(4):
                    h, qt = 2 * hp + i // 2, i % 2
                    mm = pe.transpose(bank[0:1, i * P:(i + 1) * P].bitcast(F32R), negr[:, b, h, qt:qt + 1], idr[:])
                mm.then_inc(full.sem, 1)

            def scores(u, g):
                b, hp = u // 2, u % 2
                n, q0, heads = b // 2, (b % 2) * T, slice(1 + 2 * hp, 3 + 2 * hp)
                pe.wait_ge(row_made.sem, row_made.at(g, u + 1))
                pe.wait_ge(rope_lo.sem, rope_lo.at(g, (n + 1) * NR))
                pe.wait_ge(exp_done.sem, exp_done.at(g, u - 1))
                s = ps_s[u % 2]
                for kt in range(2):
                    out = s[:, 0:BANK] if kt == 0 else s[:, BANK:BANK + T]
                    at = kt * P
                    for i, (a, m) in enumerate(PARTS):
                        pe.matmul(out, qk[:, a, n, 0, q0 + at:q0 + at + P], qk[:, m, n, heads, q0 + at:q0 + T],
                                  start=i == 0, stop=False)
                    shift = row[:, b % 2, hp, :].rearrange("o (h q) -> o h q", h=2)[:, :, at:T]
                    mm = pe.matmul(out, ones[0:1, :], shift, start=False, stop=True)
                mm.then_inc(s_made.sem, 1)

            def values(u, g):
                b = u // 2
                pe.wait_ge(v_lo.sem, v_lo.at(g, b // 2 + 1))
                pe.wait_ge(p_hi.sem, p_hi.at(g, u + 1))
                pe.wait_ge(p_lo.sem, p_lo.at(g, u + 1))
                pe.wait_ge(y_made.sem, y_made.at(g, u))
                late = [x[:].rearrange("p (h q) -> p h q", h=2)[:, :, P:T] for x in (ps_o, ps_l)]
                for kt in range(2):
                    for m in (HI, LO):
                        pe.matmul(late[1] if kt else ps_l[:], ones[:], pr[:, u % 2, m, 2 * T * kt:2 * T + T * kt],
                                  start=kt == 0 and m == HI, stop=kt == 1 and m == LO, skip_group_check=True)
                for kt in range(2):
                    for i, (a, m) in enumerate(PARTS):
                        mm = pe.matmul(late[0] if kt else ps_o[:], v[:, a, 2 * (b % 2) + kt, :],
                                       pr[:, u % 2, m, 2 * T * kt:2 * T + T * kt], start=kt == 0 and i == 0,
                                       stop=kt == 1 and i == 2, skip_group_check=True)
                mm.then_inc(pv_done.sem, 1)

            def output(step, g, bank):
                _, b, tt = step
                pe.wait_ge(wo_hi.sem, wo_hi.at(g, GRP))
                pe.wait_ge(wo_lo.sem, wo_lo.at(g, GRP))
                pe.wait_ge(y_hi.sem, y_hi.at(g, 2 * b + 2))
                pe.wait_ge(y_lo.sem, y_lo.at(g, 2 * b + 2))
                i = 0
                for h in range(GRP):
                    for a, m in PARTS:
                        mm = pe.matmul(bank[:], y[:, b % 2, a, h, tt * P:(tt + 1) * P], wo[:, m, h, :],
                                       start=i == 0, stop=i == 3 * GRP - 1)
                        i += 1
                mm.then_inc(full.sem, 1)

            def handle(step, g0, ahead, k):
                g = g0 + ahead
                if step[0] == "scores":
                    scores(step[1], g)
                elif step[0] == "pv":
                    values(step[1], g)
                elif step[0] in RINGED:
                    bank = take(g0, k)
                    recent.append((step, ahead))
                    {"proj": project, "vtr": turn_values, "max": coarse_scores, "row": shift_row,
                     "wo": output}[step[0]](step, g, bank)

            run(pe, handle)

        @blk.scalar
        def _(act):
            act.sem_inc(exp_done.sem, 2)
            for c in range(C):
                act.wait_ge(x_in.sem, 16 * C)
                act.activation(xt[:, HI, c, :], x_stage(c), ACT.Copy).then_inc(x_hi.sem, 1)

            def handle(step, g0, ahead, k):
                g, (kind, *arg) = g0 + ahead, step
                if k is not None:
                    bank = bank_of(k)
                if kind == "split_w":
                    c = arg[0]
                    src, s, value = raw_slot(g, c)
                    act.wait_ge(s, value)
                    if ahead:
                        act.wait_ge(was_swapped.sem, was_swapped.at(g, 0))
                    act.activation(w[:, HI, c, :], src, ACT.Copy).then_inc(w_hi.sem, 1)
                elif kind == "split_wo":
                    h = arg[0]
                    src, s, value = raw_slot(g, C + h)
                    act.wait_ge(s, value)
                    act.wait_ge(full.sem, full.at(g0, 1))
                    act.activation(wo[:, HI, h, :], src[:, 0:D], ACT.Copy).then_inc(wo_hi.sem, 1)
                elif kind == "proj" and arg[1] == TILE_V:
                    act.wait_ge(full.sem, full.at(g0, k + 1))
                    act.activation(vt[:], bank[:], ACT.Copy).then_inc(vt_made.sem, 1)
                elif kind == "proj":
                    r = arg[0] * NR + ROPED.index(arg[1])
                    act.wait_ge(full.sem, full.at(g0, k + 1))
                    act.wait_ge(rope_sum.sem, rope_sum.at(g, r - 1))
                    act.activation(swapped[0:64, r % 2, :], bank[64:128, :], ACT.Copy)
                    act.activation(swapped[64:128, r % 2, :], bank[0:64, :], ACT.Copy).then_inc(was_swapped.sem, 1)
                elif kind == "vtr":
                    act.wait_ge(full.sem, full.at(g0, k + 1))
                    act.activation(v[:, HI].rearrange("p t d -> p (t d)"), bank[:], ACT.Copy).then_inc(v_hi.sem, 1)
                elif kind == "row":
                    act.wait_ge(full.sem, full.at(g0, k + 1))
                    act.activation(row[:, arg[0] % 2, arg[1], :], bank[0:1, :], ACT.Copy).then_inc(row_made.sem, 1)
                elif kind == "scores":
                    u = arg[0]
                    act.wait_ge(s_made.sem, s_made.at(g, u + 1))
                    act.wait_ge(p_lo.sem, p_lo.at(g, u - 1))
                    act.activation(pf[:, u % 2, :], ps_s[u % 2][:, 0:3 * T], ACT.Exp, scale=SCALE_A)\
                       .then_inc(exp_done.sem, 1)
                elif kind == "low":
                    u = arg[0]
                    act.wait_ge(masked.sem, masked.at(g, 2 * u + 2))
                    if u >= 2:
                        act.wait_ge(pv_done.sem, pv_done.at(g, u - 1))
                    act.activation(pr[:, u % 2, HI, :], pf[:, u % 2, :], ACT.Copy).then_inc(p_hi.sem, 1)

            run(act, handle)

        @blk.vector
        def _(dve):
            dve.sem_inc(p_lo.sem, 2)
            dve.sem_inc(y_made.sem, 1)
            dve.sem_inc(rope_sum.sem, 2)
            dve.memset(f(ones[:]), 1.0).then_inc(const_made.sem, 1)
            dve.wait_ge(consts_in.sem, 80)
            dve.tensor_copy(idr[:], idf[:]).then_inc(const_made.sem, 1)

            def rope_end(g, r):
                n, j = divmod(r, NR)
                dve.wait_ge(was_turned.sem, was_turned.at(g, r + 1))
                dve.wait_ge(was_cos.sem, was_cos.at(g, r + 1))
                dve.tensor_tensor(roped[:, r % 2, :], roped[:, r % 2, :], swapped[:, r % 2, :], ALU.add)\
                   .then_inc(rope_sum.sem, 1)
                dve.wait_ge(rope_sum.sem, rope_sum.at(g, r + 1))
                dve.tensor_copy(qk[:, HI, n, j, :], roped[:, r % 2, :]).then_inc(rope_hi.sem, 1)

            def handle(step, g0, ahead, k):
                g, (kind, *arg) = g0 + ahead, step
                if k is not None:
                    bank = bank_of(k)
                if kind == "proj" and arg[1] != TILE_V:
                    r = arg[0] * NR + ROPED.index(arg[1])
                    dve.wait_ge(was_swapped.sem, was_swapped.at(g, r + 1))
                    dve.wait_ge(rope_lo.sem, rope_lo.at(g, r - 1))
                    dve.tensor_tensor(roped[:, r % 2, :].rearrange("p (b t) -> p b t", t=T),
                                      bank[:].rearrange("p (b t) -> p b t", t=T),
                                      cos[:].rearrange("p (o t) -> p o t", o=1).to_broadcast([P, HALF // T, T]), ALU.mult)\
                       .then_inc(was_cos.sem, 1)
                    rope_end(g, r)
                elif kind == "vtr":
                    dve.wait_ge(v_hi.sem, v_hi.at(g, arg[0] + 1))
                    dve.tensor_tensor(v[:, LO].rearrange("p t d -> p (t d)"), bank[:],
                                      f(v[:, HI].rearrange("p t d -> p (t d)")), ALU.subtract).then_inc(v_lo.sem, 1)
                elif kind == "max":
                    b, h = arg
                    dve.wait_ge(full.sem, full.at(g0, k + 1))
                    dve.sem_inc(held.sem, 1)
                    for qt in range(2):
                        seen = (qt + 1) * P
                        dve.tensor_tensor_reduce(junk[:, qt, 0:seen], bank[:, qt * T:qt * T + seen], msk[:, qt, 0:seen],
                                                 1.0, NEG, ALU.add, ALU.max, neg[:, b, h, qt:qt + 1]).then_inc(mx_made.sem, 1)
                    dve.wait_ge(mx_made.sem, mx_made.at(g, 2 * (b * GRP + h) + 2))
                    if h == GRP - 1:
                        dve.tensor_scalar(negr[:, b, :, :], neg[:, b, :, :], -1.0, None, ALU.mult)\
                           .then_inc(neg_made.sem, 1)
                elif kind == "low":
                    u = arg[0]
                    dve.wait_ge(p_hi.sem, p_hi.at(g, u + 1))
                    dve.tensor_tensor(pr[:, u % 2, LO, :], pf[:, u % 2, :], f(pr[:, u % 2, HI, :]), ALU.subtract)\
                       .then_inc(p_lo.sem, 1)
                elif kind == "pv":
                    u = arg[0]
                    b, hp = u // 2, u % 2
                    dve.wait_ge(pv_done.sem, pv_done.at(g, u + 1))
                    dve.wait_ge(y_lo.sem, y_lo.at(g, u - 1))
                    dve.transpose(yf[:, u % 2, :], ps_l[:]).then_inc(columns.sem, 1)
                    dve.wait_ge(columns.sem, columns.at(g, u + 1))
                    dve.reciprocal(rec[:], yf[:, u % 2, :].rearrange("p (b j) -> p b j", j=32)[:, :, 0]).then_inc(recips.sem, 1)
                    dve.wait_ge(recips.sem, recips.at(g, u + 1))
                    dve.transpose(recs[:], rec[:].rearrange("p (b o) -> p b o", o=1).to_broadcast([P, HALF // 32, 32]))\
                       .then_inc(recs_made.sem, 1)
                    dve.wait_ge(recs_made.sem, recs_made.at(g, u + 1))
                    dve.tensor_tensor(yf[:, u % 2, :], ps_o[:], recs[:], ALU.mult).then_inc(y_made.sem, 1)
                    dve.wait_ge(y_made.sem, y_made.at(g, u + 1))
                    dve.tensor_copy(y[:, b % 2, HI, 2 * hp:2 * hp + 2, :].rearrange("p h q -> p (h q)"),
                                    yf[:, u % 2, :]).then_inc(y_hi.sem, 1)
                elif kind == "wo":
                    b, tt = arg
                    dve.wait_ge(full.sem, full.at(g0, k + 1))
                    dve.tensor_tensor(acc[:, 2 * b + tt, :], bank[:], acc[:, 2 * b + tt, :], ALU.add)\
                       .then_inc(acc_done.sem, 1)

            run(dve, handle)
            dve.wait_ge(acc_done.sem, acc_done.at(KVH - 1, 2 * B))

        @blk.gpsimd
        def _(pool):
            pool.sem_inc(rope_lo.sem, 2)
            pool.sem_inc(y_lo.sem, 2)
            for c in range(C):
                pool.wait_ge(x_hi.sem, c + 1)
                pool.tensor_tensor(xt[:, LO, c, :], x_stage(c), f(xt[:, HI, c, :]), ALU.subtract).then_inc(x_lo.sem, 1)

            def handle(step, g0, ahead, k):
                g, (kind, *arg) = g0 + ahead, step
                if kind == "split_w":
                    c = arg[0]
                    pool.wait_ge(w_hi.sem, w_hi.at(g, c + 1))
                    pool.tensor_tensor(w[:, LO, c, :], raw_slot(g, c)[0], f(w[:, HI, c, :]), ALU.subtract).then_inc(w_lo.sem, 1)
                elif kind == "split_wo":
                    h = arg[0]
                    pool.wait_ge(wo_hi.sem, wo_hi.at(g, h + 1))
                    pool.tensor_tensor(wo[:, LO, h, :], raw_slot(g, C + h)[0][:, 0:D], f(wo[:, HI, h, :]), ALU.subtract)\
                        .then_inc(wo_lo.sem, 1)
                elif kind == "proj" and arg[1] != TILE_V:
                    r = arg[0] * NR + ROPED.index(arg[1])
                    pool.wait_ge(was_swapped.sem, was_swapped.at(g, r + 1))
                    pool.tensor_tensor(swapped[:, r % 2, :].rearrange("p (b t) -> p b t", t=T),
                                       swapped[:, r % 2, :].rearrange("p (b t) -> p b t", t=T),
                                       sin[:].rearrange("p (o t) -> p o t", o=1).to_broadcast([P, HALF // T, T]), ALU.mult)\
                        .then_inc(was_turned.sem, 1)
                    n, j = divmod(r, NR)
                    pool.wait_ge(rope_hi.sem, rope_hi.at(g, r + 1))
                    pool.tensor_tensor(qk[:, LO, n, j, :], roped[:, r % 2, :], f(qk[:, HI, n, j, :]), ALU.subtract)\
                        .then_inc(rope_lo.sem, 1)
                elif kind == "scores":
                    u = arg[0]
                    pool.wait_ge(exp_done.sem, exp_done.at(g, u + 1))
                    pool.sem_inc(held.sem, 1)
                    for blocks in (pf[:, u % 2, 0:2 * T].rearrange("p (h q) -> p h q", h=2)[:, :, 0:P],
                                   pf[:, u % 2, 2 * T:3 * T].rearrange("p (h q) -> p h q", h=2)):
                        pool.affine_select(out=blocks, in_=blocks, pattern=[[0, 2], [1, P]], compare_op=ALU.is_ge,
                                           fill=0.0, base=0, channel_multiplier=-1).then_inc(masked.sem, 1)
                elif kind == "pv":
                    u = arg[0]
                    b, hp = u // 2, u % 2
                    pool.wait_ge(y_hi.sem, y_hi.at(g, u + 1))
                    pool.tensor_tensor(y[:, b % 2, LO, 2 * hp:2 * hp + 2, :].rearrange("p h q -> p (h q)"), yf[:, u % 2, :],
                                       f(y[:, b % 2, HI, 2 * hp:2 * hp + 2, :].rearrange("p h q -> p (h q)")),
                                       ALU.subtract).then_inc(y_lo.sem, 1)

            run(pool, handle)



def between(nc, eye, wq, acc, x1_dram, x1t_dram, q_dram):
    with ExitStack() as st:
        def sb(name, shape, dt=F32):
            return st.enter_context(nc.sbuf_tensor(name, shape, dt))

        def sem(name, start=0):
            return Sem(nc, st, name, 0, start).sem

        idf = sb("m_idf", [P, P])
        stats, mv = sb("m_stats", [P, TILES, 6]), sb("m_mv", [P, TILES, 2])
        std, rstd = sb("m_std", [P, TILES]), sb("m_rstd", [P, TILES])
        x1t = sb("m_x1t", [P, C, TOK])
        xt = sb("m_xt", [P, 2, C, TOK], F32R)
        wraw = sb("m_wraw", [P, C, H2 * HD2])
        w = sb("m_w", [P, 2, C, H2 * HD2], F32R)
        q = sb("m_q", [HD2, 4, 2, HALF], F32R)
        ps_t = [st.enter_context(nc.psum_tensor(f"m_t{i}", [P, BANK], F32)) for i in range(2)]
        ps_q = [st.enter_context(nc.psum_tensor(f"m_q{i}", [P, BANK], F32)) for i in range(4)]

        eye_in, w_in = sem("m_eye_in"), sem("m_w_in")
        w_hi, w_lo = sem("m_w_hi"), sem("m_w_lo")
        stat_done, mean_done, eps_done, std_done, rstd_done, x1_done = (
            sem(f"m_{k}") for k in ("stat_done", "mean_done", "eps_done", "std_done", "rstd_done", "x1_done"))
        turned, xt_hi, xt_f, xt_lo = sem("m_turned"), sem("m_xt_hi"), sem("m_xt_f"), sem("m_xt_lo")
        q_full, q_hi, q_lo = sem("m_q_full"), sem("m_q_hi"), sem("m_q_lo")
        q_out = [sem(f"m_q_out{i}") for i in range(4)]
        out = sem("m_out")

        steps = [(h, n) for h in range(H2) for n in range(NHALF)]
        blk = st.enter_context(nc.Block())

        @blk.sync
        def _(sp):
            sp.dma_start(idf[:], eye).then_inc(eye_in, 16)
            for c in range(C):
                sp.dma_start(wraw[:, c, :], wq[:, c, :]).then_inc(w_in, 16)
            sp.wait_ge(x1_done, TILES)
            sp.dma_start(x1_dram, acc[:]).then_inc(out, 16)
            sp.wait_ge(xt_f, TILES)
            sp.dma_start(x1t_dram, x1t[:]).then_inc(out, 16)
            for k, (h, n) in enumerate(steps):
                sp.wait_ge(q_hi, k + 1)
                sp.wait_ge(q_lo, k + 1)
                for b in range(2):
                    sp.dma_start(q_dram[2 * n + b, h // G2, :, :, h % G2, :], f(q[:, k % 4, :, b * T:(b + 1) * T]))\
                      .then_inc(q_out[k % 4], 16)
            for i in range(4):
                sp.wait_ge(q_out[i], 32 * (len(steps) // 4))
            sp.wait_ge(out, 32)

        @blk.tensor
        def _(pe):
            pe.wait_ge(eye_in, 16)
            for t in range(TILES):
                pe.wait_ge(x1_done, t + 1)
                if t >= 2:
                    pe.wait_ge(xt_f, t - 1)
                for c in range(C):
                    mm = pe.transpose(ps_t[t % 2][:, c * P:(c + 1) * P], acc[:, t, c * P:(c + 1) * P], idf[:])
                mm.then_inc(turned, 1)
            pe.wait_ge(w_hi, C)
            pe.wait_ge(w_lo, C)
            pe.wait_ge(xt_hi, TILES)
            pe.wait_ge(xt_lo, TILES)
            for k, (h, n) in enumerate(steps):
                if k >= 4:
                    pe.wait_ge(q_lo, k - 3)
                i = 0
                for c in range(C):
                    for a, m in PARTS:
                        mm = pe.matmul(ps_q[k % 4][0:HD2, :], w[:, a, c, h * HD2:(h + 1) * HD2],
                                       xt[:, m, c, n * HALF:(n + 1) * HALF], start=i == 0, stop=i == 3 * C - 1)
                        i += 1
                mm.then_inc(q_full, 1)

        @blk.scalar
        def _(act):
            act.wait_ge(eps_done, 1)
            act.activation(std[:], mv[:, :, 1], ACT.Sqrt).then_inc(std_done, 1)
            for c in range(C):
                act.wait_ge(w_in, 16 * C)
                act.activation(w[:, HI, c, :], wraw[:, c, :], ACT.Copy).then_inc(w_hi, 1)
            for t in range(TILES):
                act.wait_ge(turned, t + 1)
                act.activation(x1t[:, :, t * P:(t + 1) * P], ps_t[t % 2][:].rearrange("p (c t) -> p c t", c=C), ACT.Copy)\
                   .then_inc(xt_f, 1)
            for k, (h, n) in enumerate(steps):
                act.wait_ge(q_full, k + 1)
                if k >= 4:
                    act.wait_ge(q_out[k % 4], 32 * (k // 4))
                act.activation(q[:, k % 4, HI, :], ps_q[k % 4][0:HD2, :], ACT.Copy).then_inc(q_hi, 1)

        @blk.vector
        def _(dve):
            for t in range(TILES):
                dve.bn_stats(stats[:, t, :], acc[:, t, :]).then_inc(stat_done, 1)
            for t in range(TILES):
                dve.wait_ge(stat_done, t + 1)
                dve.bn_aggr(mv[:, t, :], stats[:, t, :]).then_inc(mean_done, 1)
            dve.wait_ge(mean_done, TILES)
            dve.tensor_scalar(mv[:, :, 1], mv[:, :, 1], EPS, None, ALU.add).then_inc(eps_done, 1)
            dve.wait_ge(std_done, 1)
            dve.reciprocal(rstd[:], std[:]).then_inc(rstd_done, 1)
            dve.wait_ge(rstd_done, 1)
            for t in range(TILES):
                dve.tensor_scalar(acc[:, t, :], acc[:, t, :], mv[:, t, 0:1], rstd[:, t:t + 1], ALU.subtract, ALU.mult)\
                   .then_inc(x1_done, 1)
            for t in range(TILES):
                at = slice(t * P, (t + 1) * P)
                dve.wait_ge(xt_f, t + 1)
                dve.tensor_copy(xt[:, HI, :, at], x1t[:, :, at]).then_inc(xt_hi, 1)
                dve.wait_ge(xt_hi, t + 1)
                dve.tensor_tensor(xt[:, LO, :, at], x1t[:, :, at], f(xt[:, HI, :, at]), ALU.subtract).then_inc(xt_lo, 1)
            for k, (h, n) in enumerate(steps):
                dve.wait_ge(q_hi, k + 1)
                dve.tensor_tensor(q[:, k % 4, LO, :], ps_q[k % 4][0:HD2, :], f(q[:, k % 4, HI, :]), ALU.subtract)\
                   .then_inc(q_lo, 1)

        @blk.gpsimd
        def _(pool):
            for c in range(C):
                pool.wait_ge(w_hi, c + 1)
                pool.tensor_tensor(w[:, LO, c, :], wraw[:, c, :], f(w[:, HI, c, :]), ALU.subtract).then_inc(w_lo, 1)



CH = 256
CHUNKS = [(i * CH, CH) for i in range(6)] + [(6 * CH, S2 - 6 * CH)]
CHMAX = CHUNKS[-1][1]
TILES_OF_CHUNK = [[2 * i, 2 * i + 1] for i in range(6)] + [[14, 12, 13]]
GROUPS = 2 * KV2
PAIRS = (NT2 + 1) // 2
STEPS = GROUPS * PAIRS
MAXW = ((0, 2 * BANK), (2 * BANK, S2 - 2 * BANK))


def projections():
    s = []
    for j in range(len(CHUNKS)):
        s += [("k", j, kv) for kv in range(KV2)] + [("v", j, t) for t in TILES_OF_CHUNK[j]]
    return s


def schedule_b():
    s = []
    proj = projections()
    last_v = [p for p in proj if p[0] == "v" and p[1] == len(CHUNKS) - 1]
    s += [("proj", k) for k, p in enumerate(proj) if p not in last_v]
    maxes = [("max", 0, i) for i in range(8)]
    for p in last_v:
        s += maxes[:2] + [("proj", proj.index(p))]
        maxes = maxes[2:]
    s += maxes + [("row", 0)]
    for k in range(STEPS):
        g, j = divmod(k, PAIRS)
        more = g + 1 < GROUPS
        if more and j == 0:
            s += [("max", g + 1, 0)]
        s += [("scores", k)]
        if more and j == PAIRS - 1:
            s += [("row", g + 1)]
        if k >= 2:
            s += [("pv", k - 2)]
        if more and j < PAIRS - 1:
            s += [("max", g + 1, j + 1)]
        if g and j == 3:
            s += [("sums", g - 1)]
        if g and j == 4:
            s += [("spread", g - 1)]
    return s + [("split", STEPS - 1), ("pv", STEPS - 2), ("pv", STEPS - 1), ("sums", GROUPS - 1), ("spread", GROUPS - 1)]


def cross_attention(nc, ctx_t, wk, wv, eye, x1t_dram, q_dram, y_dram):
    sched = schedule_b()
    proj = projections()
    NP = len(proj)
    NCH = len(CHUNKS)

    with ExitStack() as st:
        def sb(name, shape, dt=F32):
            return st.enter_context(nc.sbuf_tensor(name, shape, dt))

        def sem(name, per=0, start=0):
            return Sem(nc, st, name, per, start)

        kt = sb("b_kt", [ROWB + 1, 2, KV2, S2], F32R)
        v = sb("b_v", [P, 2, NT2, KV2, HD2 + 1], F32R)
        w_k, w_v = sb("b_wk", [P, 2, C, KV2 * HD2], F32R), sb("b_wv", [P, 2, C, KV2 * HD2], F32R)
        q = sb("b_q", [ROWB + 1, 2, 2, G2 * T], F32R)
        hraw = sb("b_hraw", [P, C, CHMAX])
        hid = sb("b_hid", [P, 2, 2, C, CHMAX], F32R)
        pf = sb("b_pf", [P, 2, 2 * BANK])
        pr = sb("b_pr", [P, 2, 2, 2 * BANK], F32R)
        o = sb("b_o", [HD2 + 1, BANK])
        yf = sb("b_yf", [HD2, BANK])
        y = sb("b_y", [HD2, 2, BANK], F32R)
        mx = sb("b_mx", [P, 2, 4, 2])
        neg = sb("b_neg", [P, 2, 4], F32R)
        rec = sb("b_rec", [P, 4])
        idf, idr = sb("b_idf", [P, P]), sb("b_idr", [P, P], F32R)

        ps_s = [st.enter_context(nc.psum_tensor(f"b_s{i}", [P, 2 * BANK], F32)) for i in range(2)]
        ps_m = st.enter_context(nc.psum_tensor("b_m", [P, 2 * BANK], F32))
        ps_o = st.enter_context(nc.psum_tensor("b_o_ps", [P, BANK], F32))
        ps_x = st.enter_context(nc.psum_tensor("b_x", [P, BANK], F32))

        w_in, eye_in = sem("b_w_in"), sem("b_eye_in")
        w_hi, w_lo, const_made = sem("b_w_hi"), sem("b_w_lo"), sem("b_const_made")
        h_in = sem("b_h_in", 16 * NCH + 16)
        h_hi, h_lo = sem("b_h_hi", NCH), sem("b_h_lo", NCH * C, 1)
        q_in = [sem(f"b_q_in{i}", 32) for i in range(2)]
        full, kv_hi, kv_lo = sem("b_full", NP), sem("b_kv_hi", NP), sem("b_kv_lo", NP)
        m_full, mx_made = sem("b_m_full", 8 * GROUPS), sem("b_mx_made", 8 * GROUPS, 1)
        neg_made, row_full, row_made = sem("b_neg_made", GROUPS), sem("b_row_full", GROUPS), sem("b_row_made", GROUPS)
        s_made, exp_done = sem("b_s_made", STEPS, 40), sem("b_exp_done", STEPS, 2)
        p_hi, p_lo, pv_done = sem("b_p_hi", STEPS), sem("b_p_lo", STEPS, 2), sem("b_pv_done", STEPS)
        o_out, sums, recips, spread = sem("b_o_out", GROUPS, 1), sem("b_sums", GROUPS), sem("b_recips", GROUPS), sem("b_spread", GROUPS)
        y_made, y_hi, y_lo = sem("b_y_made", GROUPS, 1), sem("b_y_hi", GROUPS), sem("b_y_lo", GROUPS, 1)
        y_out = sem("b_y_out", 16 * GROUPS, 16)
        held = sem("b_held")

        blk = st.enter_context(nc.Block())

        def bank_of(k):
            s = ps_s[(k % 4) // 2]
            return s[:, (k % 2) * BANK:(k % 2 + 1) * BANK]

        def keys_of(k):
            j = k % PAIRS
            return [(i, 2 * j + i) for i in range(2) if 2 * j + i < NT2]

        def shape_of(k):
            tiles = keys_of(k)
            return KT2[tiles[-1][1]][1], BANK * len(tiles)

        def w_stage(c):
            n = KV2 * HD2
            return pf[:].rearrange("p a b -> p (a b)")[:, c * n:(c + 1) * n]

        def high_part(act, b, k):
            rows, n = shape_of(k)
            act.wait_ge(exp_done.sem, exp_done.at(b, k + 1))
            if k >= 2:
                act.wait_ge(pv_done.sem, pv_done.at(b, k - 1))
            act.activation(pr[0:rows, k % 2, HI, 0:n], pf[0:rows, k % 2, 0:n], ACT.Copy).then_inc(p_hi.sem, 1)

        def low_part(dve, b, k):
            rows, n = shape_of(k)
            dve.wait_ge(p_hi.sem, p_hi.at(b, k + 1))
            dve.tensor_tensor(pr[0:rows, k % 2, LO, 0:n], pf[0:rows, k % 2, 0:n], f(pr[0:rows, k % 2, HI, 0:n]),
                              ALU.subtract).then_inc(p_lo.sem, 1)

        def split_hidden(act, b, j):
            n = CHUNKS[j][1]
            act.wait_ge(h_in.sem, h_in.at(b, 16 * (j + 1) + (16 if j == NCH - 1 else 0)))
            if j >= 2:
                act.wait_ge(full.sem, full.at(b, max(k for k, p in enumerate(proj) if p[1] == j - 2) + 1))
            act.activation(hid[:, j % 2, HI, :, 0:n], hraw[:, :, 0:n], ACT.Copy).then_inc(h_hi.sem, 1)

        @blk.sync
        def _(sp):
            sp.dma_start(idf[:], eye).then_inc(eye_in.sem, 16)
            for i, src in enumerate((wk, wv)):
                if i:
                    sp.wait_ge(w_lo.sem, C)
                sp.dma_start(pf[:].rearrange("p a b -> p (a b)")[:, 0:C * KV2 * HD2], src).then_inc(w_in.sem, 16)
            for b in range(B):
                for j, (c0, n) in enumerate(CHUNKS):
                    sp.wait_ge(h_lo.sem, h_lo.at(b, j * C))
                    own = min(n, CTXP - c0)
                    sp.dma_start(hraw[:, :, 0:own],
                                 ctx_t[b, :, :, c0:c0 + own]).then_inc(h_in.sem, 16)
                    if own < n:
                        sp.dma_start(hraw[:, :, own:n], x1t_dram[:, :, b * T:(b + 1) * T]).then_inc(h_in.sem, 16)
                for kv in range(2):
                    sp.wait_ge(s_made.sem, s_made.at(b, (kv - 1) * 2 * PAIRS))
                    sp.dma_start(f(q[0:HD2, kv]), q_dram[b, kv].rearrange("d r h t -> d r (h t)"))\
                      .then_inc(q_in[kv].sem, 16)
                for g in range(GROUPS):
                    sp.wait_ge(y_lo.sem, y_lo.at(b, g + 1))
                    sp.wait_ge(y_hi.sem, y_hi.at(b, g + 1))
                    sp.dma_start(y_dram[:, :, 2 * g:2 * g + 2, b * T:(b + 1) * T],
                                 f(y[:]).rearrange("d r (h t) -> d r h t", h=2)).then_inc(y_out.sem, 16)
                    if g in (1, 3):
                        kv = (g - 1) // 2 + 2
                        sp.wait_ge(s_made.sem, s_made.at(b, (g + 1) * PAIRS))
                        sp.dma_start(f(q[0:HD2, kv % 2]),
                                     q_dram[b, kv].rearrange("d r h t -> d r (h t)"))\
                          .then_inc(q_in[kv % 2].sem, 16)
            sp.wait_ge(y_out.sem, y_out.at(B - 1, 16 * GROUPS))

        @blk.tensor
        def _(pe):
            pe.wait_ge(w_hi.sem, 2 * C)
            pe.wait_ge(w_lo.sem, 2 * C)
            pe.wait_ge(const_made.sem, 8)

            def project(k, b):
                kind, j, i = proj[k]
                c0, n = CHUNKS[j]
                if (kind, i) == ("k", 0):
                    pe.wait_ge(h_hi.sem, h_hi.at(b, j + 1))
                    pe.wait_ge(h_lo.sem, h_lo.at(b, (j + 1) * C))
                if k >= 4:
                    pe.wait_ge(kv_lo.sem, kv_lo.at(b, k - 3))
                else:
                    pe.wait_ge(exp_done.sem, exp_done.at(b, 0))
                bank, s = bank_of(k), 0
                for c in range(C):
                    for a, m in PARTS:
                        if kind == "k":
                            mm = pe.matmul(bank[0:HD2, 0:n], w_k[:, a, c, i * HD2:(i + 1) * HD2],
                                           hid[:, j % 2, m, c, 0:n], start=s == 0, stop=s == 3 * C - 1)
                        else:
                            t0, rows = KT2[i]
                            mm = pe.matmul(bank[0:rows, 0:KV2 * HD2], hid[:, j % 2, a, c, t0 - c0:t0 - c0 + rows],
                                           w_v[:, m, c, :], start=s == 0, stop=s == 3 * C - 1)
                        s += 1
                mm.then_inc(full.sem, 1)

            def coarse(g, i, b):
                kv, hp = divmod(g, 2)
                t, half = divmod(i, 2)
                if g == 0 and i == 0:
                    pe.wait_ge(kv_hi.sem, kv_hi.at(b, proj.index(("k", NCH - 1, KV2 - 1)) + 1))
                if hp == 0 and i == 0:
                    pe.wait_ge(q_in[kv % 2].sem, q_in[kv % 2].at(b, 16 * (kv // 2 + 1)))
                pe.wait_ge(mx_made.sem, mx_made.at(b, 8 * g + i))
                c0, n = MAXW[half]
                for x in range(0, n, BANK):
                    mm = pe.matmul(ps_m[:, x:min(x + BANK, n)], q[0:HD2, kv % 2, HI, hp * BANK + t * P:hp * BANK + (t + 1) * P],
                                   kt[0:HD2, HI, kv, c0 + x:c0 + min(x + BANK, n)], start=True, stop=True)
                mm.then_inc(m_full.sem, 1)

            def shift_row(g, b):
                pe.wait_ge(neg_made.sem, neg_made.at(b, g + 1))
                pe.wait_ge(y_made.sem, y_made.at(b, max(g - 1, 0)))
                if g:
                    pe.wait_ge(row_made.sem, row_made.at(b, g))
                for t in range(4):
                    mm = pe.transpose(ps_x[0:1, t * P:(t + 1) * P].bitcast(F32R), neg[:, g % 2, t:t + 1], idr[:])
                mm.then_inc(row_full.sem, 1)

            def scores(k, b):
                g = k // PAIRS
                kv, hp = divmod(g, 2)
                if k == 0:
                    pe.wait_ge(kv_lo.sem, kv_lo.at(b, NP))
                if k % PAIRS == 0:
                    pe.wait_ge(row_made.sem, row_made.at(b, g + 1))
                pe.wait_ge(exp_done.sem, exp_done.at(b, k - 1))
                for i, t in keys_of(k):
                    t0, rows = KT2[t]
                    for s, (a, m) in enumerate(PARTS):
                        mm = pe.matmul(ps_s[k % 2][0:rows, i * BANK:(i + 1) * BANK], kt[:, a, kv, t0:t0 + rows],
                                       q[:, kv % 2, m, hp * BANK:(hp + 1) * BANK], start=s == 0, stop=s == 2)
                mm.then_inc(s_made.sem, 1)

            def values(k, b):
                g, j = divmod(k, PAIRS)
                pe.wait_ge(p_hi.sem, p_hi.at(b, k + 1))
                pe.wait_ge(p_lo.sem, p_lo.at(b, k + 1))
                if j == 0:
                    pe.wait_ge(o_out.sem, o_out.at(b, g))
                for i, t in keys_of(k):
                    rows = KT2[t][1]
                    for s, (a, m) in enumerate(PARTS):
                        mm = pe.matmul(ps_o[0:HD2 + 1, :], v[0:rows, a, t, g // 2, :],
                                       pr[0:rows, k % 2, m, i * BANK:(i + 1) * BANK],
                                       start=t == 0 and s == 0, stop=t == NT2 - 1 and s == 2)
                mm.then_inc(pv_done.sem, 1)

            def sum_columns(g, b):
                pe.wait_ge(o_out.sem, o_out.at(b, g + 1))
                pe.wait_ge(row_made.sem, row_made.at(b, min(g + 2, GROUPS)))
                pe.sem_inc(held.sem, 1)
                for t in range(4):
                    mm = pe.transpose(ps_x[:, t:t + 1], o[HD2:HD2 + 1, t * P:(t + 1) * P], idf[HD2:HD2 + 1, HD2:HD2 + 1])
                mm.then_inc(sums.sem, 1)

            def spread_recips(g, b):
                pe.wait_ge(recips.sem, recips.at(b, g + 1))
                for t in range(4):
                    mm = pe.matmul(ps_x[0:HD2, t * P:(t + 1) * P], rec[:, t:t + 1].to_broadcast([P, HD2]), idf[:],
                                   start=True, stop=True)
                mm.then_inc(spread.sem, 1)

            with pe.Fori(0, B) as b:
                for kind, *arg in sched:
                    if kind == "split":
                        continue
                    {"proj": project, "max": coarse, "row": shift_row, "scores": scores, "pv": values,
                     "sums": sum_columns, "spread": spread_recips}[kind](*arg, b)

        @blk.scalar
        def _(act):
            act.sem_inc(exp_done.sem, 2)
            act.sem_inc(o_out.sem, 1)
            for i, wt in enumerate((w_k, w_v)):
                act.wait_ge(w_in.sem, 16 * (i + 1))
                for c in range(C):
                    act.activation(wt[:, HI, c, :], w_stage(c), ACT.Copy).then_inc(w_hi.sem, 1)
            with act.Fori(0, B) as b:
                for kind, *arg in sched:
                    if kind == "proj":
                        k = arg[0]
                        what, j, i = proj[k]
                        c0, n = CHUNKS[j]
                        if (what, i) == ("k", 0):
                            if j == 0:
                                split_hidden(act, b, 0)
                            if j + 1 < NCH:
                                split_hidden(act, b, j + 1)
                        act.wait_ge(full.sem, full.at(b, k + 1))
                        if what == "k":
                            act.activation(kt[0:HD2, HI, i, c0:c0 + n], bank_of(k)[0:HD2, 0:n], ACT.Copy).then_inc(kv_hi.sem, 1)
                        else:
                            rows = KT2[i][1]
                            act.activation(v[0:rows, HI, i, :, 0:HD2],
                                           bank_of(k)[0:rows, 0:KV2 * HD2].rearrange("p (h d) -> p h d", h=KV2), ACT.Copy)\
                               .then_inc(kv_hi.sem, 1)
                    elif kind == "row":
                        g = arg[0]
                        kv, hp = divmod(g, 2)
                        act.wait_ge(row_full.sem, row_full.at(b, g + 1))
                        act.activation(q[ROWB:ROWB + 1, kv % 2, HI, hp * BANK:(hp + 1) * BANK], ps_x[0:1, :], ACT.Copy)\
                           .then_inc(row_made.sem, 1)
                    elif kind == "scores":
                        k = arg[0]
                        if k:
                            high_part(act, b, k - 1)
                        rows, n = shape_of(k)
                        act.wait_ge(s_made.sem, s_made.at(b, k + 1))
                        act.wait_ge(p_lo.sem, p_lo.at(b, k - 1))
                        act.activation(pf[0:rows, k % 2, 0:n], ps_s[k % 2][0:rows, 0:n], ACT.Exp, scale=SCALE_B)\
                           .then_inc(exp_done.sem, 1)
                    elif kind == "split":
                        high_part(act, b, arg[0])
                    elif kind == "pv" and arg[0] % PAIRS == PAIRS - 1:
                        k = arg[0]
                        g = k // PAIRS
                        act.wait_ge(pv_done.sem, pv_done.at(b, k + 1))
                        act.wait_ge(y_made.sem, y_made.at(b, g))
                        act.activation(o[:], ps_o[0:HD2 + 1, :], ACT.Copy).then_inc(o_out.sem, 1)

        @blk.vector
        def _(dve):
            dve.sem_inc(mx_made.sem, 1)
            dve.sem_inc(p_lo.sem, 2)
            dve.sem_inc(y_made.sem, 1)
            for ap, value in ((v[:, HI, :, :, HD2], 1.0), (v[:, LO, :, :, HD2], 0.0), (kt[ROWB:ROWB + 1, HI], 1.0),
                              (kt[ROWB:ROWB + 1, LO], 0.0), (q[ROWB:ROWB + 1, 0, LO], 0.0), (q[ROWB:ROWB + 1, 1, LO], 0.0)):
                dve.memset(f(ap), value).then_inc(const_made.sem, 1)
            dve.wait_ge(eye_in.sem, 16)
            dve.tensor_copy(idr[:], idf[:]).then_inc(const_made.sem, 2)
            with dve.Fori(0, B) as b:
                for kind, *arg in sched:
                    if kind == "proj":
                        k = arg[0]
                        what, j, i = proj[k]
                        c0, n = CHUNKS[j]
                        dve.wait_ge(kv_hi.sem, kv_hi.at(b, k + 1))
                        if what == "k":
                            dve.tensor_tensor(kt[0:HD2, LO, i, c0:c0 + n], bank_of(k)[0:HD2, 0:n],
                                              f(kt[0:HD2, HI, i, c0:c0 + n]), ALU.subtract).then_inc(kv_lo.sem, 1)
                        else:
                            rows = KT2[i][1]
                            dve.tensor_tensor(v[0:rows, LO, i, :, 0:HD2],
                                              bank_of(k)[0:rows, 0:KV2 * HD2].rearrange("p (h d) -> p h d", h=KV2),
                                              f(v[0:rows, HI, i, :, 0:HD2]), ALU.subtract).then_inc(kv_lo.sem, 1)
                    elif kind == "max":
                        g, i = arg
                        t, half = divmod(i, 2)
                        dve.wait_ge(m_full.sem, m_full.at(b, 8 * g + i + 1))
                        dve.reduce_max(mx[:, g % 2, t, half:half + 1], ps_m[:, 0:MAXW[half][1]], X).then_inc(mx_made.sem, 1)
                        if i == 7:
                            dve.wait_ge(mx_made.sem, mx_made.at(b, 8 * g + 8))
                            dve.reduce_max(neg[:, g % 2, :], mx[:, g % 2], X, negate=True).then_inc(neg_made.sem, 1)
                    elif kind == "scores" and arg[0] or kind == "split":
                        low_part(dve, b, arg[0] - (kind == "scores"))
                    elif kind == "sums":
                        g = arg[0]
                        dve.wait_ge(sums.sem, sums.at(b, g + 1))
                        dve.reciprocal(rec[:], ps_x[:, 0:4]).then_inc(recips.sem, 1)
                    elif kind == "spread":
                        g = arg[0]
                        dve.wait_ge(spread.sem, spread.at(b, g + 1))
                        dve.wait_ge(y_lo.sem, y_lo.at(b, g))
                        dve.tensor_tensor(yf[:], ps_x[0:HD2, :], o[0:HD2, :], ALU.mult).then_inc(y_made.sem, 1)
                        dve.wait_ge(y_made.sem, y_made.at(b, g + 1))
                        dve.wait_ge(y_out.sem, y_out.at(b, 16 * g))
                        dve.tensor_copy(y[:, HI, :], yf[:]).then_inc(y_hi.sem, 1)

        @blk.gpsimd
        def _(pool):
            pool.sem_inc(h_lo.sem, 1)
            pool.sem_inc(y_lo.sem, 1)
            pool.sem_inc(s_made.sem, 40)
            pool.sem_inc(y_out.sem, 16)
            for i, wt in enumerate((w_k, w_v)):
                for c in range(C):
                    pool.wait_ge(w_hi.sem, i * C + c + 1)
                    pool.tensor_tensor(wt[:, LO, c, :], w_stage(c), f(wt[:, HI, c, :]), ALU.subtract).then_inc(w_lo.sem, 1)
            with pool.Fori(0, B) as b:
                for j, (c0, n) in enumerate(CHUNKS):
                    pool.wait_ge(h_hi.sem, h_hi.at(b, j + 1))
                    for c in range(C):
                        pool.tensor_tensor(hid[:, j % 2, LO, c, 0:n], hraw[:, c, 0:n], f(hid[:, j % 2, HI, c, 0:n]),
                                           ALU.subtract).then_inc(h_lo.sem, 1)
                for g in range(GROUPS):
                    pool.wait_ge(y_hi.sem, y_hi.at(b, g + 1))
                    pool.tensor_tensor(y[:, LO, :], yf[:], f(y[:, HI, :]), ALU.subtract).then_inc(y_lo.sem, 1)



def finish(nc, wo, w_t, lora_a, lora_bt, lora_w, bias, eye, x1_dram, y_dram, out_dram):
    NRK = 128
    ALPHA_OVER_RANK = 2.0
    with ExitStack() as st:
        def sb(name, shape, dt=F32):
            return st.enter_context(nc.sbuf_tensor(name, shape, dt))

        def sem(name):
            return st.enter_context(nc.semaphore(name))

        x1 = sb("c_x1", [P, TILES, D])
        y = sb("c_y", [HD2, 2, 2, H2, T], F32R)
        woraw = sb("c_woraw", [HD2, 4, D])
        wo_s = sb("c_wo", [HD2, 2, H2, D], F32R)
        wt, la = sb("c_wt", [P, C, D]), sb("c_la", [NRK, D])
        lb, lw, bias_s, idf = sb("c_lb", [NRK, D]), sb("c_lw", [NRK, 1]), sb("c_bias", [P, D]), sb("c_idf", [P, P])
        ws = sb("c_ws", [P, 2, C, D], F32R)
        x2 = sb("c_x2", [P, 2, D])
        x2t = sb("c_x2t", [P, 2, D], F32R)
        z = sb("c_z", [P, 2, D])
        stats, mv = sb("c_stats", [P, 2, 6]), sb("c_mv", [P, 2, 2])
        std, rstd = sb("c_std", [P, 2]), sb("c_rstd", [P, 2])
        ps_w = [st.enter_context(nc.psum_tensor(f"c_w{i}", [P, BANK], F32)) for i in range(2)]
        ps_y = [st.enter_context(nc.psum_tensor(f"c_y{i}", [P, BANK], F32)) for i in range(2)]
        ps_t, ps_f = (st.enter_context(nc.psum_tensor(f"c_{k}_ps", [P, BANK], F32)) for k in "tf")

        names = ("small_in wt_in wo_in lb_done w_full w_sum w_hi w_lo wo_hi wo_lo x1_in y_full turned t_hi t_lo "
                 "f_full z_done stat_done mean_done eps_done std_done rstd_done normed biased").split()
        (small_in, wt_in, wo_in, lb_done, w_full, w_sum, w_hi, w_lo, wo_hi, wo_lo, x1_in, y_full, turned, t_hi, t_lo,
         f_full, z_done, stat_done, mean_done, eps_done, std_done, rstd_done, normed, biased) = (
            sem(f"c_{n}") for n in names)
        out_done = [sem(f"c_out_done{i}") for i in range(2)]
        y_in = [sem(f"c_y_in{i}") for i in range(2)]

        norms = []
        for t in range(TILES + 1):
            norms += [(t, 0)] * (t < TILES) + [(t - 1, 1)] * (t >= 1)
        nth = {x: i for i, x in enumerate(norms)}
        blk = st.enter_context(nc.Block())

        @blk.sync
        def _(sp):
            for h in range(4):
                if h:
                    sp.wait_ge(wo_lo, 4 * h)
                sp.dma_start(woraw[:], wo[:, 4 * h:4 * h + 4, :]).then_inc(wo_in, 16)
                if h == 0:
                    for dst, src in ((la, lora_a), (lb, lora_bt), (lw, lora_w), (idf, eye)):
                        sp.dma_start(dst[:], src).then_inc(small_in, 16)
                    sp.dma_start(wt[:], w_t).then_inc(wt_in, 16)
                    sp.dma_start(bias_s[:], bias.to_broadcast([P, D])).then_inc(small_in, 16)
                    sp.dma_start(x1[:], x1_dram).then_inc(x1_in, 16)
                if h < 2:
                    sp.dma_start(f(y[:, h]), y_dram[:, :, :, h * T:(h + 1) * T]).then_inc(y_in[h], 16)
            for b in range(2, B):
                sp.wait_ge(y_full, 2 * (b - 1))
                sp.dma_start(f(y[:, b % 2]), y_dram[:, :, :, b * T:(b + 1) * T]).then_inc(y_in[b % 2], 16)
            for t in range(TILES):
                sp.wait_ge(normed, nth[(t, 1)] + 1)
                sp.dma_start(out_dram[t * P:(t + 1) * P, :], z[:, t % 2, :]).then_inc(out_done[t % 2], 16)
            for i in range(2):
                sp.wait_ge(out_done[i], 16 * (TILES // 2))

        @blk.tensor
        def _(pe):
            pe.wait_ge(small_in, 80)
            pe.wait_ge(lb_done, 1)
            for c in range(C):
                if c >= 2:
                    pe.wait_ge(w_sum, c - 1)
                pe.matmul(ps_w[c % 2][:], la[:, c * P:(c + 1) * P], lb[:], start=True, stop=True).then_inc(w_full, 1)
            pe.wait_ge(wo_hi, H2)
            pe.wait_ge(wo_lo, H2)

            def project(t):
                b = t // 2
                pe.wait_ge(y_in[b % 2], 16 * (b // 2 + 1))
                if t >= 2:
                    pe.wait_ge(z_done, nth[(t - 2, 0)] + 1)
                i = 0
                for h in range(H2):
                    for a, m in PARTS:
                        mm = pe.matmul(ps_y[t % 2][:], y[:, b % 2, a, h, (t % 2) * P:(t % 2 + 1) * P], wo_s[:, m, h, :],
                                       start=i == 0, stop=i == 3 * H2 - 1)
                        i += 1
                mm.then_inc(y_full, 1)

            def turn(t):
                pe.wait_ge(normed, nth[(t, 0)] + 1)
                if t:
                    pe.wait_ge(t_lo, t)
                for c in range(C):
                    mm = pe.transpose(ps_t[:, c * P:(c + 1) * P], x2[:, t % 2, c * P:(c + 1) * P], idf[:])
                mm.then_inc(turned, 1)

            def feed(t):
                pe.wait_ge(t_hi, t + 1)
                pe.wait_ge(t_lo, t + 1)
                pe.wait_ge(w_hi, C)
                pe.wait_ge(w_lo, C)
                if t:
                    pe.wait_ge(z_done, nth[(t - 1, 1)] + 1)
                i = 0
                for c in range(C):
                    for a, m in PARTS:
                        mm = pe.matmul(ps_f[:], x2t[:, a, c * P:(c + 1) * P], ws[:, m, c, :], start=i == 0, stop=i == 3 * C - 1)
                        i += 1
                mm.then_inc(f_full, 1)

            for t in range(TILES + 1):
                if t < TILES:
                    project(t)
                if t >= 1:
                    turn(t - 1)
                    feed(t - 1)

        @blk.scalar
        def _(act):
            for h in range(H2):
                act.wait_ge(wo_in, 16 * (h // 4 + 1))
                act.activation(wo_s[:, HI, h, :], woraw[:, h % 4, :], ACT.Copy).then_inc(wo_hi, 1)
            for c in range(C):
                act.wait_ge(w_sum, c + 1)
                act.activation(ws[:, HI, c, :], wt[:, c, :], ACT.Copy).then_inc(w_hi, 1)
            for i, (t, which) in enumerate(norms):
                act.wait_ge(eps_done, i + 1)
                act.activation(std[:, i % 2:i % 2 + 1], mv[:, i % 2, 1:2], ACT.Sqrt).then_inc(std_done, 1)
                if which == 0:
                    act.wait_ge(turned, t + 1)
                    if t:
                        act.wait_ge(f_full, t)
                    act.activation(x2t[:, HI, :], ps_t[:], ACT.Copy).then_inc(t_hi, 1)

        @blk.vector
        def _(dve):
            dve.wait_ge(small_in, 80)
            dve.tensor_scalar(lb[:], lb[:], lw[:, 0:1], ALPHA_OVER_RANK, ALU.mult, ALU.mult).then_inc(lb_done, 1)
            dve.wait_ge(wt_in, 16)
            for c in range(C):
                dve.wait_ge(w_full, c + 1)
                dve.tensor_tensor(wt[:, c, :], ps_w[c % 2][:], wt[:, c, :], ALU.add).then_inc(w_sum, 1)
            dve.wait_ge(x1_in, 16)
            for i, (t, which) in enumerate(norms):
                s = i % 2
                if which == 0:
                    dve.wait_ge(y_full, t + 1)
                    dve.tensor_tensor(x2[:, t % 2, :], ps_y[t % 2][:], x1[:, t, :], ALU.add).then_inc(z_done, 1)
                    row = x2[:, t % 2, :]
                else:
                    dve.wait_ge(turned, t + 1)
                    dve.tensor_tensor(x2[:, t % 2, :], x2[:, t % 2, :], bias_s[:], ALU.add).then_inc(biased, 1)
                    dve.wait_ge(t_hi, t + 1)
                    dve.tensor_tensor(x2t[:, LO, :], ps_t[:], f(x2t[:, HI, :]), ALU.subtract).then_inc(t_lo, 1)
                    dve.wait_ge(f_full, t + 1)
                    dve.wait_ge(biased, t + 1)
                    if t >= 2:
                        dve.wait_ge(out_done[t % 2], 16 * (t // 2))
                    dve.tensor_tensor(z[:, t % 2, :], ps_f[:], x2[:, t % 2, :], ALU.add).then_inc(z_done, 1)
                    row = z[:, t % 2, :]
                dve.wait_ge(z_done, i + 1)
                dve.bn_stats(stats[:, s, :], row).then_inc(stat_done, 1)
                dve.wait_ge(stat_done, i + 1)
                dve.bn_aggr(mv[:, s, :], stats[:, s, :]).then_inc(mean_done, 1)
                dve.wait_ge(mean_done, i + 1)
                dve.tensor_scalar(mv[:, s, 1:2], mv[:, s, 1:2], EPS, None, ALU.add).then_inc(eps_done, 1)
                dve.wait_ge(std_done, i + 1)
                dve.reciprocal(rstd[:, s:s + 1], std[:, s:s + 1]).then_inc(rstd_done, 1)
                dve.wait_ge(rstd_done, i + 1)
                dve.tensor_scalar(row, row, mv[:, s, 0:1], rstd[:, s:s + 1], ALU.subtract, ALU.mult).then_inc(normed, 1)

        @blk.gpsimd
        def _(pool):
            for h in range(H2):
                pool.wait_ge(wo_hi, h + 1)
                pool.tensor_tensor(wo_s[:, LO, h, :], woraw[:, h % 4, :], f(wo_s[:, HI, h, :]), ALU.subtract).then_inc(wo_lo, 1)
            for c in range(C):
                pool.wait_ge(w_hi, c + 1)
                pool.tensor_tensor(ws[:, LO, c, :], wt[:, c, :], f(ws[:, HI, c, :]), ALU.subtract).then_inc(w_lo, 1)



def program(nc, x_t, x_rows, w_qkv, w_o, cos_t, sin_t, mask, eye, ctx_t, wq, wk, wv, wo2, w_t, lora_a, lora_bt,
            lora_w, bias, out):
    x1_dram = nc.dram_tensor("x1_rows", [P, TILES, D], F32).ap()
    x1t_dram = nc.dram_tensor("x1_t", [P, C, TOK], F32).ap()
    q_dram = nc.dram_tensor("queries", [B, KV2, HD2, 2, G2, T], F32).ap()
    y_dram = nc.dram_tensor("attended", [HD2, 2, H2, TOK], F32).ap()
    with ExitStack() as st:
        acc = st.enter_context(nc.sbuf_tensor("acc", [P, TILES, D], F32))
        self_attention(nc, x_t, x_rows, w_qkv, w_o, cos_t, sin_t, mask, eye, acc)
        between(nc, eye, wq, acc, x1_dram, x1t_dram, q_dram)
    cross_attention(nc, ctx_t, wk, wv, eye, x1t_dram, q_dram, y_dram)
    finish(nc, wo2, w_t, lora_a, lora_bt, lora_w, bias, eye, x1_dram, y_dram, out)


def kernel(x, ctx_4096, L0_attn_w_qkv, L0_attn_w_o, L0_xattn_Wq, L0_xattn_Wk, L0_xattn_Wv, L0_xattn_Wo,
           L0_ffn_lora_A, L0_ffn_lora_B, L0_ffn_W, L0_ffn_bias, L0_ffn_lora_weights):
    import concourse.bacc as bacc
    from concourse.bass_utils import run_bass_kernel_spmd

    def chunked(w):
        return w.reshape(C, P, -1).transpose(1, 0, 2)

    x, ctx = np.asarray(x), np.asarray(ctx_4096)
    rows = x.reshape(TOK, D)
    w = np.asarray(L0_attn_w_qkv).reshape(C, P, -1)
    q_cols, kv_cols = KVH * GRP * HD, KVH * HD
    w = np.concatenate([w[:, :, :q_cols].reshape(C, P, KVH, GRP * HD),
                        w[:, :, q_cols:q_cols + kv_cols].reshape(C, P, KVH, HD),
                        w[:, :, q_cols + kv_cols:].reshape(C, P, KVH, HD)], axis=-1)
    inv = (1.0 / np.power(np.float32(10000.0), np.arange(0, HD, 2, dtype=np.float32) / np.float32(HD))).astype(np.float32)
    angle = (np.arange(T, dtype=np.float32)[None, :] * inv[:, None]).astype(np.float32)
    cos, sin = np.cos(angle), np.sin(angle)
    keys, queries = np.arange(T)[None, None, :], np.arange(P)[:, None, None] + P * np.arange(2)[None, :, None]
    arrays = {
        "x_t": chunked(rows.T),
        "x_rows": rows.reshape(TILES, P, D).transpose(1, 0, 2),
        "w_qkv": w.transpose(2, 1, 0, 3),
        "w_o": np.asarray(L0_attn_w_o).reshape(KVH, GRP, HD, D).transpose(0, 2, 1, 3),
        "cos_t": np.concatenate([cos, cos]),
        "sin_t": np.concatenate([-sin, sin]),
        "mask": np.where(keys <= queries, 0.0, NEG).astype(np.float32),
        "eye": np.eye(P, dtype=np.float32),
        "ctx_t": np.concatenate([ctx, ctx[:, -1:]], axis=1).reshape(B, CTXP, C, P).transpose(0, 3, 2, 1),
        "wq": chunked(np.asarray(L0_xattn_Wq).T),
        "wk": chunked(np.asarray(L0_xattn_Wk).T).reshape(P, -1),
        "wv": chunked(np.asarray(L0_xattn_Wv).T).reshape(P, -1),
        "wo2": np.asarray(L0_xattn_Wo).T.reshape(H2, HD2, D).transpose(1, 0, 2),
        "w_t": chunked(np.asarray(L0_ffn_W).T),
        "lora_a": np.asarray(L0_ffn_lora_A).reshape(-1, D),
        "lora_bt": np.asarray(L0_ffn_lora_B).transpose(0, 2, 1).reshape(-1, D),
        "lora_w": np.repeat(np.asarray(L0_ffn_lora_weights), 16).reshape(-1, 1),
        "bias": np.asarray(L0_ffn_bias).reshape(1, D),
    }
    arrays = {k: np.ascontiguousarray(a) for k, a in arrays.items()}
    nc = bacc.Bacc("TRN2", target_bir_lowering=False, num_devices=1)
    aps = {k: nc.dram_tensor(f"in_{k}", a.shape, mybir.dt.from_np(a.dtype), kind="ExternalInput").ap()
           for k, a in arrays.items()}
    out = nc.dram_tensor("out_0", (TOK, D), F32, kind="ExternalOutput").ap()
    program(nc, out=out, **aps)
    r = run_bass_kernel_spmd(nc, [{f"in_{k}": a for k, a in arrays.items()}], core_ids=[0])
    return r.results[0]["out_0"].reshape(B, T, D)
```

```python
from contextlib import ExitStack

import concourse.bass as bass
import numpy as np
from concourse import mybir

F32 = mybir.dt.float32
F32R = mybir.dt.float32r
ALU = mybir.AluOpType
ACT = mybir.ActivationFunctionType
X = mybir.AxisListType.X

P = 128
BANK = 512
HI, LO = 0, 1
PARTS = ((HI, HI), (HI, LO), (LO, HI))
NEG = -1e30

B, T, D = 4, 256, 512
TOK = B * T
C = D // P
TILES = TOK // P
EPS = 1e-5

KVH, GRP, HD = 8, 4, 128
NHALF, HALF = 2, 512
SCALE_A = HD ** -0.5
FEAT_A = (GRP + 2) * HD

CTX, KV2, G2, HD2 = 1601, 4, 4, 96
H2 = KV2 * G2
CTXP = CTX + 1
S2 = CTXP + T
SCALE_B = HD2 ** -0.5
KT2 = [(i * P, P) for i in range(12)] + [(CTXP, P), (CTXP + P, P), (12 * P, CTX - 12 * P)]
NT2 = len(KT2)
CHUNKS2 = [(0, 512), (512, 512), (1024, 512), (1536, S2 - 1536)]
ROWB = HD2


def f(ap):
    return ap.bitcast(F32)


class Sem:

    def __init__(self, nc, stack, name, per=0, start=0):
        self.sem, self.per, self.start = stack.enter_context(nc.semaphore(name)), per, start

    def at(self, g, k):
        return g * self.per + (k + self.start)



TILE_V, TILE_K = GRP + 1, GRP
ROPED = (TILE_K, *range(GRP))
UNITS = 2 * B

USUAL = {
    "pe": """
        proj.1.4 max.1.0 proj.1.5 scores.0 vtr.1 proj.1.0 max.1.1 pv.0 proj.1.1 scores.1 max.1.2 proj.1.2
        scores.2 max.1.3 pv.1 proj.1.3 max.2.0 wo.0.0 max.2.1 scores.3 max.2.2 max.2.3 pv.2 scores.4 wo.0.1 pv.3
        max.3.0 max.3.1 max.3.2 scores.5 pv.4 wo.1.0 wo.1.1 proj.0.5+ max.3.3 scores.6 pv.5 vtr.0+ proj.0.4+
        scores.7 pv.6 proj.0.0+ wo.2.0 proj.0.1+ pv.7 max.0.0+ proj.0.2+ wo.2.1 proj.0.3+ wo.3.0 wo.3.1 max.0.1+
        max.0.2+ max.0.3+""",
    "act": """
        swap.1.4 vt.1 hi_qk.1.4 split_wo.0 exp.0 split_wo.1 low.0 vhi.1 swap.1.0 split_wo.2 hi_qk.1.0 hi_y.0
        exp.1 swap.1.1 low.1 split_wo.3 swap.1.2 hi_qk.1.1 hi_qk.1.2 exp.2 hi_y.1 low.2 swap.1.3 hi_qk.1.3 exp.3
        split_w.0+ low.3 split_w.1+ exp.4 hi_y.2 low.4 split_w.2+ split_w.3+ hi_y.3 exp.5 low.5 vt.0+ hi_y.4
        exp.6 low.6 hi_y.5 swap.0.4+ vhi.0+ exp.7 low.7 hi_y.6 swap.0.0+ hi_qk.0.4+ hi_qk.0.0+ swap.0.1+
        hi_qk.0.1+ swap.0.2+ hi_y.7 swap.0.3+ hi_qk.0.2+ hi_qk.0.3+""",
    "dve": """
        tops.1.0 rope.1.4 lo.0 vlo.1 rope.1.0 norm.0 tops.1.1 tops.1.2 lo.1 rope.1.1 rope.1.2 norm.1 tops.1.3
        tops.2.0 rope.1.3 add.0.0 lo.2 tops.2.1 norm.2 lo.3 tops.2.2 add.0.1 tops.2.3 norm.3 lo.4 tops.3.0 lo.5
        tops.3.1 tops.3.2 add.1.0 norm.4 add.1.1 tops.3.3 norm.5 lo.6 vlo.0+ norm.6 rope.0.4+ lo.7 add.2.0
        rope.0.0+ rope.0.1+ norm.7 tops.0.0+ rope.0.2+ add.2.1 add.3.0 rope.0.3+ add.3.1 tops.0.1+ tops.0.2+
        tops.0.3+""",
    "pool": """
        turn.1.4 low_qk.1.4 mask.0 low_wo.0 turn.1.0 low_wo.1 low_qk.1.0 low_wo.2 low_y.0 mask.1 turn.1.1
        low_wo.3 turn.1.2 low_qk.1.1 mask.2 low_y.1 turn.1.3 low_qk.1.2 low_qk.1.3 mask.3 low_w.0+ low_w.1+
        low_y.2 mask.4 low_y.3 mask.5 low_w.2+ low_w.3+ low_y.4 mask.6 mask.7 low_y.5 turn.0.4+ turn.0.0+
        low_y.6 low_qk.0.4+ turn.0.1+ turn.0.2+ low_qk.0.0+ low_y.7 turn.0.3+ low_qk.0.1+ low_qk.0.2+
        low_qk.0.3+""",
}
BEFORE = {
    "pe": """
        proj.0.5 proj.0.4 vtr.0 proj.0.0 proj.0.1 proj.0.2 proj.0.3 max.0.0 max.0.1 max.0.2 max.0.3""",
    "act": """
        split_x.0 split_w.0 split_x.1 split_w.1 split_x.2 split_w.2 split_x.3 split_w.3 vt.0 split_x.4 vhi.0
        swap.0.4 swap.0.0 hi_qk.0.4 swap.0.1 hi_qk.0.0 swap.0.2 hi_qk.0.1 split_x.5 split_x.6 swap.0.3 hi_qk.0.2
        split_x.7 hi_qk.0.3""",
    "dve": """
        low_w.0 low_w.1 low_x.0 low_x.1 low_x.2 low_w.2 low_x.3 low_w.3 low_x.4 consts vlo.0 rope.0.4 rope.0.0
        acc rope.0.1 rope.0.2 tops.0.0 low_x.5 rope.0.3 low_x.6 low_x.7 tops.0.1 tops.0.2 tops.0.3""",
    "pool": """
        consts turn.0.4 turn.0.0 low_qk.0.4 turn.0.1 low_qk.0.0 turn.0.2 low_qk.0.1 turn.0.3 low_qk.0.2
        low_qk.0.3""",
}
RINGED = ("proj", "max", "wo")
RING = 3
READS = {"vtr": "proj", "vt": "proj", "vhi": "proj", "vlo": "proj", "swap": "proj", "rope": "proj", "tops": "max",
         "add": "wo"}


def steps(orders, engine, last=False):
    return [((kind, *map(int, numbers)), int(token.endswith("+")))
            for token in orders[engine].split() for kind, *numbers in [token.rstrip("+").split(".")]
            if not (last and token.endswith("+"))]


def ring_places(orders, start=0, last=False):
    ringed = [x for x in steps(orders, "pe", last) if x[0][0] in RINGED]
    return {x: start + i for i, x in enumerate(ringed)}


def self_attention(nc, x_t, x_rows, w_qkv, w_o, cos_t, sin_t, mask, eye, idf, acc, w, raw, last_load):
    FIRST, PER = len(ring_places(BEFORE)), len(ring_places(USUAL))
    ringed_first, ringed = ([step for step, _ in ring_places(x)] for x in (BEFORE, USUAL))
    assert PER % RING == 0 and ringed_first[-RING:] == ringed[-RING:]
    NR = len(ROPED)
    RAW = 2 * C

    with ExitStack() as st:
        def sb(name, shape, dt=F32):
            return st.enter_context(nc.sbuf_tensor(name, shape, dt))

        def sem(name, per=0, start=0):
            return Sem(nc, st, name, per, start)

        xt = sb("a_xt", [P, 2, C, TOK], F32R)
        wo = sb("a_wo", [P, 2, GRP, D], F32R)
        cos, sin = sb("a_cos", [P, T]), sb("a_sin", [P, T])
        msk = sb("a_mask", [P, 2, T])
        negid = sb("a_negid", [P, P])
        ones = sb("a_ones", [P, P], F32R)
        swapped = sb("a_swapped", [P, 2, HALF])
        roped = sb("a_roped", [P, 2, HALF])
        qk = sb("a_qk", [P, 2, NHALF, GRP + 1, HALF], F32R)
        vt = sb("a_vt", [P, HALF])
        v = sb("a_v", [P, NHALF, 2, 4, HD], F32R)
        top = sb("a_top", [P, B, GRP, 2])
        junk = sb("a_junk", [P, 2, T], mybir.dt.bfloat16)
        shift = sb("a_shift", [P, 2, 2, HALF], F32R)
        pf = sb("a_pf", [P, 2, 3 * T])
        pr = sb("a_pr", [P, 2, 2, 3 * T], F32R)
        rec = sb("a_rec", [P, HALF // 32])
        recs = sb("a_recs", [P, HALF])
        yf = sb("a_yf", [P, 2, HALF])
        y = sb("a_y", [P, 2, 2, GRP, T], F32R)

        ring = [st.enter_context(nc.psum_tensor(f"a_ring{i}", [P, BANK], F32)) for i in range(RING)]
        ps_s = st.enter_context(nc.psum_tensor("a_s", [P, 3 * BANK], F32))
        ps_o = st.enter_context(nc.psum_tensor("a_o", [P, BANK], F32))
        ps_l = st.enter_context(nc.psum_tensor("a_l", [P, BANK], F32))

        late_in = sem("a_late_in")
        x_in, consts_in, acc_in = [sem(f"a_x_in{i}") for i in range(NHALF * C)], sem("a_consts_in"), sem("a_acc_in")
        x_hi, const_made = sem("a_x_hi"), sem("a_const_made")
        x_lo = sem("a_x_lo")
        raw_in = [sem(f"a_raw_in{i}", 16 * RAW // 2) for i in range(2)]
        w_hi, w_lo = sem("a_w_hi", C), sem("a_w_lo", C)
        wo_hi, wo_lo = sem("a_wo_hi", GRP), sem("a_wo_lo", GRP)
        full = sem("a_ring_full", PER, FIRST)
        was_swapped = sem("a_was_swapped", NHALF * NR)
        was_turned = sem("a_was_turned", NHALF * NR)
        was_cos = sem("a_was_cos", NHALF * NR)
        rope_sum = sem("a_rope_sum", NHALF * NR, 2)
        rope_hi, rope_lo = sem("a_rope_hi", NHALF * NR), sem("a_rope_lo", NHALF * NR, 2)
        vt_made, v_hi, v_lo = sem("a_vt_made", NHALF), sem("a_v_hi", NHALF), sem("a_v_lo", NHALF)
        v_turned = sem("a_v_turned", NHALF)
        mx_made, shift_made = sem("a_mx_made", 2 * B * GRP), sem("a_shift_made", UNITS)
        s_made, exp_done, masked = sem("a_s_made", UNITS), sem("a_exp_done", UNITS, 2), sem("a_masked", 2 * UNITS)
        p_hi, p_lo, pv_done = sem("a_p_hi", UNITS), sem("a_p_lo", UNITS, 2), sem("a_pv_done", UNITS)
        columns, recips, recs_made = (sem(f"a_{k}", UNITS, start) for k, start in
                                      (("columns", 1), ("recips", 0), ("recs_made", 0)))
        y_made, y_hi, y_lo = sem("a_y_made", UNITS, 1), sem("a_y_hi", UNITS), sem("a_y_lo", UNITS, 2)
        acc_done = sem("a_acc_done", 2 * B)
        held = sem("a_held")

        blk = st.enter_context(nc.Block())

        def run(e, engine, handle):
            def part(orders, g0, start=0, last=False):
                place = ring_places(orders, start, last)
                for step, ahead in steps(orders, engine, last):
                    kind, *numbers = step
                    if READS.get(kind) == "proj" and len(numbers) == 1:
                        numbers.append(TILE_V)
                    handle(step, g0, ahead, place.get(((READS.get(kind, kind), *numbers), ahead)))

            part(BEFORE, 0, start=-FIRST)
            with e.Fori(0, KVH - 1) as g:
                part(USUAL, g)
            part(USUAL, KVH - 1, last=True)

        def bank_of(k):
            return ring[(k + FIRST) % RING]

        def tile(u, kt):
            short = slice(2 * T, 3 * T) if u % 2 == 0 else slice(0, T)
            long = slice(0, 2 * T) if u % 2 == 0 else slice(T, 3 * T)
            return short if kt else long

        def left(step, g):
            kind = step[0]
            if kind == "proj" and step[2] == TILE_V:
                return v_lo, v_lo.at(g, step[1] + 1)
            if kind == "proj":
                return was_cos, was_cos.at(g, step[1] * NR + ROPED.index(step[2]) + 1)
            if kind == "max":
                return mx_made, mx_made.at(g, 2 * (step[1] * GRP + step[2]) + 2)
            return acc_done, acc_done.at(g, 2 * step[1] + step[2] + 1)

        def x_part(i):
            n, c = divmod(i, C)
            stage = ((swapped, roped), (pf, yf))[n][c // 2][:].rearrange("p a b -> p (a b)")
            return stage[:, c % 2 * HALF:(c % 2 + 1) * HALF], lambda part: xt[:, part, c, n * HALF:(n + 1) * HALF]

        def low_w(e, g, c):
            e.wait_ge(w_hi.sem, w_hi.at(g, c + 1))
            e.tensor_tensor(w[:, LO, c, :], raw_slot(g, c)[0], f(w[:, HI, c, :]), ALU.subtract).then_inc(w_lo.sem, 1)

        def raw_slot(g, j):
            s = raw_in[j % 2]
            return raw[:, j % 2, :], s.sem, s.at(g, 16 * (j // 2 + 1))

        @blk.sync
        def _(sp):
            def load_x(i):
                n, c = divmod(i, C)
                sp.dma_start(x_part(i)[0], x_t[:, c, n * HALF:(n + 1) * HALF]).then_inc(x_in[i].sem, 16)

            for g in range(KVH):
                for j in range(RAW):
                    if g == 0 and j < C:
                        load_x(j)
                    if j >= 2 or g:
                        s, k = (w_lo, j - 1) if 2 <= j < C + 2 else (wo_lo, j - C - 1 if j > C else j - 1)
                        sp.wait_ge(s.sem, s.at(g, k))
                    src, n = (w_qkv[g, :, j, :], FEAT_A) if j < C else (w_o[g, :, j - C, :], D)
                    sp.dma_start(raw[:, j % 2, 0:n], src).then_inc(raw_in[j % 2].sem, 16)
                    if g == 0 and j == C - 1:
                        for dst, src in ((cos, cos_t), (sin, sin_t), (idf, eye), (msk, mask)):
                            sp.dma_start(dst[:], src).then_inc(consts_in.sem, 16)
                        for i in range(C, NHALF * C):
                            load_x(i)
                        sp.dma_start(acc[:], x_rows).then_inc(acc_in.sem, 16)

            sp.wait_ge(was_swapped.sem, was_swapped.at(KVH - 1, NHALF * NR))
            sp.dma_start(*last_load).then_inc(late_in.sem, 16)
            sp.wait_ge(late_in.sem, 16)

        @blk.tensor
        def _(pe):
            recent = []

            def take(g0, k):
                if k >= RING - FIRST:
                    before, ahead = (ringed[k - RING], 0) if 0 <= k < RING else recent[-RING]
                    s, value = left(before, g0 + ahead)
                    pe.wait_ge(s.sem, value)
                return bank_of(k)

            def project(step, g, bank, ahead):
                _, n, t = step
                i = 0
                for c in range(C):
                    if (n, t) == (0, TILE_V):
                        pe.wait_ge(w_hi.sem, w_hi.at(g, c + 1))
                        pe.wait_ge(w_lo.sem, w_lo.at(g, c + 1))
                        if not ahead:
                            pe.wait_ge(x_lo.sem, c + 1)
                    for a, m in PARTS:
                        mm = pe.matmul(bank[:], w[:, a, c, t * HD:(t + 1) * HD],
                                       xt[:, m, c, n * HALF:(n + 1) * HALF], start=i == 0, stop=i == 3 * C - 1)
                        i += 1
                mm.then_inc(full.sem, 1)

            def turn_values(step, g, bank):
                pe.wait_ge(vt_made.sem, vt_made.at(g, step[1] + 1))
                for i in range(4):
                    mm = pe.transpose(bank[:, i * P:(i + 1) * P], vt[:, i * P:(i + 1) * P], idf[:])
                mm.then_inc(v_turned.sem, 1)

            def coarse_scores(step, g, bank):
                _, b, h = step
                n, q0 = b // 2, (b % 2) * T
                pe.wait_ge(rope_hi.sem, rope_hi.at(g, n * NR + h + 2))
                for qt in range(2):
                    mm = pe.matmul(bank[:, qt * T:(qt + 1) * T], qk[:, HI, n, 1 + h, q0 + qt * P:q0 + (qt + 1) * P],
                                   qk[:, HI, n, 0, q0:q0 + T], start=True, stop=True)
                mm.then_inc(full.sem, 1)

            def scores(u, g):
                b, hp = u // 2, u % 2
                n, q0, heads = b // 2, (b % 2) * T, slice(1 + 2 * hp, 3 + 2 * hp)
                pe.wait_ge(shift_made.sem, shift_made.at(g, u + 1))
                pe.wait_ge(rope_lo.sem, rope_lo.at(g, (n + 1) * NR))
                s = ps_s[:, 3 * T * (u % 2):3 * T * (u % 2 + 1)]
                for kt in range(2):
                    pe.wait_ge(exp_done.sem, exp_done.at(g, u - 1 + kt))
                    out = s[:, tile(u, kt)]
                    at = kt * P
                    for i, (a, m) in enumerate(PARTS):
                        pe.matmul(out, qk[:, a, n, 0, q0 + at:q0 + at + P], qk[:, m, n, heads, q0 + at:q0 + T],
                                  start=i == 0, stop=False)
                    mm = pe.matmul(out, ones[:], shift[:, b % 2, hp, :].rearrange("p (h q) -> p h q", h=2)[:, :, at:T],
                                   start=False, stop=True)
                mm.then_inc(s_made.sem, 1)

            def values(u, g):
                b = u // 2
                pe.wait_ge(v_lo.sem, v_lo.at(g, b // 2 + 1))
                pe.wait_ge(p_hi.sem, p_hi.at(g, u + 1))
                pe.wait_ge(p_lo.sem, p_lo.at(g, u + 1))
                pe.wait_ge(columns.sem, columns.at(g, u))
                late = [x[:].rearrange("p (h q) -> p h q", h=2)[:, :, P:T] for x in (ps_o, ps_l)]
                for kt in range(2):
                    for m in (HI, LO):
                        pe.matmul(late[1] if kt else ps_l[:], ones[:], pr[:, u % 2, m, tile(u, kt)],
                                  start=kt == 0 and m == HI, stop=kt == 1 and m == LO, skip_group_check=True)
                pe.wait_ge(y_made.sem, y_made.at(g, u))
                for kt in range(2):
                    for i, (a, m) in enumerate(PARTS):
                        mm = pe.matmul(late[0] if kt else ps_o[:], v[:, b // 2, a, 2 * (b % 2) + kt, :],
                                       pr[:, u % 2, m, tile(u, kt)], start=kt == 0 and i == 0,
                                       stop=kt == 1 and i == 2, skip_group_check=True)
                mm.then_inc(pv_done.sem, 1)

            def output(step, g, bank):
                _, b, tt = step
                pe.wait_ge(wo_hi.sem, wo_hi.at(g, GRP))
                pe.wait_ge(wo_lo.sem, wo_lo.at(g, GRP))
                pe.wait_ge(y_hi.sem, y_hi.at(g, 2 * b + 2))
                pe.wait_ge(y_lo.sem, y_lo.at(g, 2 * b + 2))
                i = 0
                for h in range(GRP):
                    for a, m in PARTS:
                        mm = pe.matmul(bank[:], y[:, b % 2, a, h, tt * P:(tt + 1) * P], wo[:, m, h, :],
                                       start=i == 0, stop=i == 3 * GRP - 1)
                        i += 1
                mm.then_inc(full.sem, 1)

            def handle(step, g0, ahead, k):
                g = g0 + ahead
                if step[0] == "scores":
                    scores(step[1], g)
                elif step[0] == "pv":
                    values(step[1], g)
                elif step[0] == "vtr":
                    if not ahead and step[1] == 0:
                        pe.wait_ge(consts_in.sem, 64)
                    turn_values(step, g, bank_of(k))
                elif step[0] in RINGED:
                    bank = take(g0, k)
                    recent.append((step, ahead))
                    if step[0] == "proj":
                        project(step, g, bank, ahead)
                    elif step[0] == "max":
                        coarse_scores(step, g, bank)
                        if k == -1:
                            pe.wait_ge(x_lo.sem, NHALF * C)
                            pe.wait_ge(const_made.sem, 1)
                    else:
                        output(step, g, bank)

            run(pe, "pe", handle)

        @blk.scalar
        def _(act):
            act.sem_inc(exp_done.sem, 2)

            def handle(step, g0, ahead, k):
                g, (kind, *arg) = g0 + ahead, step
                if k is not None:
                    bank = bank_of(k)
                if kind == "split_x":
                    act.wait_ge(x_in[arg[0]].sem, 16)
                    stage, x = x_part(arg[0])
                    act.activation(x(HI), stage, ACT.Copy).then_inc(x_hi.sem, 1)
                elif kind == "split_w":
                    c = arg[0]
                    src, s, value = raw_slot(g, c)
                    act.wait_ge(s, value)
                    if ahead:
                        act.wait_ge(was_swapped.sem, was_swapped.at(g, 0))
                    act.activation(w[:, HI, c, :], src, ACT.Copy).then_inc(w_hi.sem, 1)
                elif kind == "split_wo":
                    h = arg[0]
                    src, s, value = raw_slot(g, C + h)
                    act.wait_ge(s, value)
                    act.wait_ge(full.sem, full.at(g0, 1))
                    act.activation(wo[:, HI, h, :], src[:, 0:D], ACT.Copy).then_inc(wo_hi.sem, 1)
                elif kind == "vt":
                    act.wait_ge(full.sem, full.at(g0, k + 1))
                    act.activation(vt[:], bank[:], ACT.Copy).then_inc(vt_made.sem, 1)
                elif kind == "swap":
                    r = arg[0] * NR + ROPED.index(arg[1])
                    act.wait_ge(full.sem, full.at(g0, k + 1))
                    act.wait_ge(rope_sum.sem, rope_sum.at(g, r - 1))
                    act.activation(swapped[0:64, r % 2, :], bank[64:128, :], ACT.Copy)
                    act.activation(swapped[64:128, r % 2, :], bank[0:64, :], ACT.Copy).then_inc(was_swapped.sem, 1)
                elif kind == "hi_qk":
                    n, j = arg[0], ROPED.index(arg[1])
                    act.wait_ge(rope_sum.sem, rope_sum.at(g, n * NR + j + 1))
                    act.activation(qk[:, HI, n, j, :], roped[:, (n * NR + j) % 2, :], ACT.Copy).then_inc(rope_hi.sem, 1)
                elif kind == "hi_y":
                    u = arg[0]
                    b, hp = u // 2, u % 2
                    act.wait_ge(y_made.sem, y_made.at(g, u + 1))
                    act.activation(y[:, b % 2, HI, 2 * hp:2 * hp + 2, :].rearrange("p h q -> p (h q)"), yf[:, u % 2, :],
                                   ACT.Copy).then_inc(y_hi.sem, 1)
                elif kind == "vhi":
                    n = arg[0]
                    act.wait_ge(v_turned.sem, v_turned.at(g, n + 1))
                    act.activation(v[:, n, HI].rearrange("p t d -> p (t d)"), bank[:], ACT.Copy).then_inc(v_hi.sem, 1)
                elif kind == "exp":
                    u = arg[0]
                    act.wait_ge(s_made.sem, s_made.at(g, u + 1))
                    act.wait_ge(p_lo.sem, p_lo.at(g, u - 1))
                    act.activation(pf[:, u % 2, :], ps_s[:, 3 * T * (u % 2):3 * T * (u % 2 + 1)], ACT.Exp, scale=SCALE_A)\
                       .then_inc(exp_done.sem, 1)
                elif kind == "low":
                    u = arg[0]
                    act.wait_ge(masked.sem, masked.at(g, 2 * u + 2))
                    if u >= 2:
                        act.wait_ge(pv_done.sem, pv_done.at(g, u - 1))
                    act.activation(pr[:, u % 2, HI, :], pf[:, u % 2, :], ACT.Copy).then_inc(p_hi.sem, 1)

            run(act, "act", handle)

        @blk.vector
        def _(dve):
            dve.sem_inc(p_lo.sem, 2)
            dve.sem_inc(y_made.sem, 1)
            dve.sem_inc(columns.sem, 1)
            dve.sem_inc(rope_sum.sem, 2)
            dve.memset(f(ones[:]), 1.0).then_inc(const_made.sem, 1)

            def rope_end(g, r):
                dve.wait_ge(was_turned.sem, was_turned.at(g, r + 1))
                dve.wait_ge(was_cos.sem, was_cos.at(g, r + 1))
                dve.tensor_tensor(roped[:, r % 2, :], roped[:, r % 2, :], swapped[:, r % 2, :], ALU.add)\
                   .then_inc(rope_sum.sem, 1)

            def handle(step, g0, ahead, k):
                g, (kind, *arg) = g0 + ahead, step
                if k is not None:
                    bank = bank_of(k)
                if kind == "low_x":
                    i = arg[0]
                    dve.wait_ge(x_hi.sem, i + 1)
                    stage, x = x_part(i)
                    dve.tensor_tensor(x(LO), stage, f(x(HI)), ALU.subtract).then_inc(x_lo.sem, 1)
                elif kind == "low_w":
                    low_w(dve, g, arg[0])
                elif kind == "consts":
                    dve.wait_ge(consts_in.sem, 64)
                    dve.tensor_scalar(negid[:], idf[:], -1.0, None, ALU.mult).then_inc(const_made.sem, 1)
                    dve.wait_ge(const_made.sem, 2)
                elif kind == "acc":
                    dve.wait_ge(acc_in.sem, 16)
                elif kind == "rope":
                    r = arg[0] * NR + ROPED.index(arg[1])
                    dve.wait_ge(was_swapped.sem, was_swapped.at(g, r + 1))
                    dve.wait_ge(rope_lo.sem, rope_lo.at(g, r - 1))
                    dve.tensor_tensor(roped[:, r % 2, :].rearrange("p (b t) -> p b t", t=T),
                                      bank[:].rearrange("p (b t) -> p b t", t=T),
                                      cos[:].rearrange("p (o t) -> p o t", o=1).to_broadcast([P, HALF // T, T]), ALU.mult)\
                       .then_inc(was_cos.sem, 1)
                    rope_end(g, r)
                elif kind == "vlo":
                    n = arg[0]
                    dve.wait_ge(v_hi.sem, v_hi.at(g, n + 1))
                    dve.tensor_tensor(v[:, n, LO].rearrange("p t d -> p (t d)"), bank[:],
                                      f(v[:, n, HI].rearrange("p t d -> p (t d)")), ALU.subtract).then_inc(v_lo.sem, 1)
                elif kind == "tops":
                    b, h = arg
                    dve.wait_ge(full.sem, full.at(g0, k + 1))
                    dve.sem_inc(held.sem, 1)
                    for qt in range(2):
                        seen = (qt + 1) * P
                        dve.tensor_tensor_reduce(junk[:, qt, 0:seen], bank[:, qt * T:qt * T + seen], msk[:, qt, 0:seen],
                                                 1.0, NEG, ALU.add, ALU.max, top[:, b, h, qt:qt + 1]).then_inc(mx_made.sem, 1)
                    dve.wait_ge(mx_made.sem, mx_made.at(g, 2 * (b * GRP + h) + 2))
                    if h % 2:
                        dve.tensor_tensor(shift[:, b % 2, h // 2, :].rearrange("p (t q) -> p t q", q=P),
                                          negid[:].rearrange("p (o q) -> p o q", o=1).to_broadcast([P, 4, P]),
                                          top[:, b, h - 1:h + 1, :].rearrange("p h (t o) -> p (h t) o", o=1)
                                          .to_broadcast([P, 4, P]), ALU.mult).then_inc(shift_made.sem, 1)
                elif kind == "lo":
                    u = arg[0]
                    dve.wait_ge(p_hi.sem, p_hi.at(g, u + 1))
                    dve.tensor_tensor(pr[:, u % 2, LO, :], pf[:, u % 2, :], f(pr[:, u % 2, HI, :]), ALU.subtract)\
                       .then_inc(p_lo.sem, 1)
                elif kind == "norm":
                    u = arg[0]
                    b, hp = u // 2, u % 2
                    dve.wait_ge(pv_done.sem, pv_done.at(g, u + 1))
                    dve.wait_ge(y_lo.sem, y_lo.at(g, u - 1))
                    dve.transpose(yf[:, u % 2, :], ps_l[:]).then_inc(columns.sem, 1)
                    dve.wait_ge(columns.sem, columns.at(g, u + 1))
                    dve.reciprocal(rec[:], yf[:, u % 2, :].rearrange("p (b j) -> p b j", j=32)[:, :, 0]).then_inc(recips.sem, 1)
                    dve.wait_ge(recips.sem, recips.at(g, u + 1))
                    dve.transpose(recs[:], rec[:].rearrange("p (b o) -> p b o", o=1).to_broadcast([P, HALF // 32, 32]))\
                       .then_inc(recs_made.sem, 1)
                    dve.wait_ge(recs_made.sem, recs_made.at(g, u + 1))
                    dve.tensor_tensor(yf[:, u % 2, :], ps_o[:], recs[:], ALU.mult).then_inc(y_made.sem, 1)
                elif kind == "add":
                    b, tt = arg
                    dve.wait_ge(full.sem, full.at(g0, k + 1))
                    dve.tensor_tensor(acc[:, 2 * b + tt, :], bank[:], acc[:, 2 * b + tt, :], ALU.add)\
                       .then_inc(acc_done.sem, 1)

            run(dve, "dve", handle)
            dve.wait_ge(acc_done.sem, acc_done.at(KVH - 1, 2 * B))

        @blk.gpsimd
        def _(pool):
            pool.sem_inc(rope_lo.sem, 2)
            pool.sem_inc(y_lo.sem, 2)

            def handle(step, g0, ahead, k):
                g, (kind, *arg) = g0 + ahead, step
                if kind == "consts":
                    pool.wait_ge(consts_in.sem, 64)
                elif kind == "low_w":
                    low_w(pool, g, arg[0])
                elif kind == "low_wo":
                    h = arg[0]
                    pool.wait_ge(wo_hi.sem, wo_hi.at(g, h + 1))
                    pool.tensor_tensor(wo[:, LO, h, :], raw_slot(g, C + h)[0][:, 0:D], f(wo[:, HI, h, :]), ALU.subtract)\
                        .then_inc(wo_lo.sem, 1)
                elif kind == "turn":
                    r = arg[0] * NR + ROPED.index(arg[1])
                    pool.wait_ge(was_swapped.sem, was_swapped.at(g, r + 1))
                    pool.tensor_tensor(swapped[:, r % 2, :].rearrange("p (b t) -> p b t", t=T),
                                       swapped[:, r % 2, :].rearrange("p (b t) -> p b t", t=T),
                                       sin[:].rearrange("p (o t) -> p o t", o=1).to_broadcast([P, HALF // T, T]), ALU.mult)\
                        .then_inc(was_turned.sem, 1)
                elif kind == "low_qk":
                    n, j = arg[0], ROPED.index(arg[1])
                    r = n * NR + j
                    pool.wait_ge(rope_hi.sem, rope_hi.at(g, r + 1))
                    pool.tensor_tensor(qk[:, LO, n, j, :], roped[:, r % 2, :], f(qk[:, HI, n, j, :]), ALU.subtract)\
                        .then_inc(rope_lo.sem, 1)
                elif kind == "mask":
                    u = arg[0]
                    pool.wait_ge(exp_done.sem, exp_done.at(g, u + 1))
                    pool.sem_inc(held.sem, 1)
                    for kt in range(2):
                        blocks = pf[:, u % 2, tile(u, kt)].rearrange("p (h q) -> p h q", h=2)[:, :, 0:P]
                        pool.affine_select(out=blocks, in_=blocks, pattern=[[0, 2], [1, P]], compare_op=ALU.is_ge,
                                           fill=0.0, base=0, channel_multiplier=-1).then_inc(masked.sem, 1)
                elif kind == "low_y":
                    u = arg[0]
                    b, hp = u // 2, u % 2
                    pool.wait_ge(y_hi.sem, y_hi.at(g, u + 1))
                    pool.tensor_tensor(y[:, b % 2, LO, 2 * hp:2 * hp + 2, :].rearrange("p h q -> p (h q)"), yf[:, u % 2, :],
                                       f(y[:, b % 2, HI, 2 * hp:2 * hp + 2, :].rearrange("p h q -> p (h q)")),
                                       ALU.subtract).then_inc(y_lo.sem, 1)

            run(pool, "pool", handle)



EDGE = -(-KV2 * S2 // P)

def between(nc, idf, wraw, acc, wk, wv, ctx_t, w_kv, hraw, hid, x1_dram, x1t_dram, q_dram, q_out, edges):
    FT = H2 * HD2 // P
    WT = 3
    HT = TILES // NHALF
    with ExitStack() as st:
        def sb(name, shape, dt=F32):
            return st.enter_context(nc.sbuf_tensor(name, shape, dt))

        def sem(name):
            return st.enter_context(nc.semaphore(f"m_{name}"))

        stats, mv = sb("m_stats", [P, TILES, 6]), sb("m_mv", [P, TILES, 2])
        std, rstd = sb("m_std", [P, TILES]), sb("m_rstd", [P, TILES])
        x1t = sb("m_x1t", [P, C, TOK])
        xt = sb("m_xt", [P, 2, C, TOK], F32R)
        w = sb("m_w", [P, 2, C, H2 * HD2], F32R)
        kvraw = sb("m_kvraw", [P, 2, C, KV2 * HD2])
        q = sb("m_q", [P, 4, HALF])
        edge = sb("m_edge", [P, 2, EDGE], F32R)
        ps_t = [st.enter_context(nc.psum_tensor(f"m_t{i}", [P, BANK], F32)) for i in range(2)]
        ps_q = [st.enter_context(nc.psum_tensor(f"m_q{i}", [P, BANK], F32)) for i in range(4)]

        kv_in, h_in, w_hi, w_lo, kv_hi, kv_lo, h_hi, h_lo = (
            sem(k) for k in ("kv_in", "h_in", "w_hi", "w_lo", "kv_hi", "kv_lo", "h_hi", "h_lo"))
        stat_done, mean_done, eps_done, std_done, rstd_done, x1_done = (
            sem(k) for k in ("stat_done", "mean_done", "eps_done", "std_done", "rstd_done", "x1_done"))
        turned, xt_f, xt_hi, xt_lo = sem("turned"), sem("xt_f"), sem("xt_hi"), sem("xt_lo")
        q_full, q_made = sem("q_full"), sem("q_made")
        out, edge_made = sem("out"), sem("edge_made")

        steps = [(n, t) for n in range(NHALF) for t in range(FT)]
        blk = st.enter_context(nc.Block())

        @blk.sync
        def _(sp):
            for i, src in enumerate((wk, wv)):
                sp.dma_start(kvraw[:, i].rearrange("p c n -> p (c n)"), src).then_inc(kv_in, 16)
            sp.dma_start(hraw[:, :, 0:CHUNKS[0][1]], ctx_t[0, :, :, 0:CHUNKS[0][1]]).then_inc(h_in, 16)
            sp.wait_ge(edge_made, 2)
            sp.dma_start(edges.rearrange("o r (p n) -> p (o r) n", p=P), f(edge[:])).then_inc(out, 16)
            sp.wait_ge(x1_done, TILES)
            sp.dma_start(x1_dram, acc[:]).then_inc(out, 16)
            sp.wait_ge(xt_f, TILES)
            sp.dma_start(x1t_dram, x1t[:]).then_inc(out, 16)
            for k, (n, t) in enumerate(steps):
                sp.wait_ge(q_made, k + 1)
                sp.dma_start(q_dram[t * P:(t + 1) * P, n * HALF:(n + 1) * HALF], q[:, k % 4, :]).then_inc(q_out[k % 4], 16)
            sp.wait_ge(out, 48)

        @blk.tensor
        def _(pe):
            def turn(t):
                pe.wait_ge(x1_done, t + 1)
                if t >= 2:
                    pe.wait_ge(xt_f, t - 1)
                for c in range(C):
                    mm = pe.transpose(ps_t[t % 2][:, c * P:(c + 1) * P], acc[:, t, c * P:(c + 1) * P], idf[:])
                mm.then_inc(turned, 1)

            for t in range(HT):
                turn(t)
            for k, (n, ft) in enumerate(steps):
                if 1 <= k <= HT:
                    turn(HT + k - 1)
                if ft == 0:
                    pe.wait_ge(xt_lo, (n + 1) * HT)
                if n == 0 and ft % WT == 0:
                    pe.wait_ge(w_lo, ft // WT + 1)
                if k >= 4:
                    pe.wait_ge(q_made, k - 3)
                i = 0
                for c in range(C):
                    for a, m in PARTS:
                        mm = pe.matmul(ps_q[k % 4][:], w[:, a, c, ft * P:(ft + 1) * P],
                                       xt[:, m, c, n * HALF:(n + 1) * HALF], start=i == 0, stop=i == 3 * C - 1)
                        i += 1
                mm.then_inc(q_full, 1)

        @blk.scalar
        def _(act):
            def split_w(i):
                at = slice(i * WT * P, (i + 1) * WT * P)
                act.activation(w[:, HI, :, at], wraw[:, :, at], ACT.Copy).then_inc(w_hi, 1)

            split_w(0)
            for n in range(NHALF):
                act.wait_ge(eps_done, n + 1)
                act.activation(std[:, n * HT:(n + 1) * HT], mv[:, n * HT:(n + 1) * HT, 1], ACT.Sqrt).then_inc(std_done, 1)
                if n:
                    split_w(3)
                for t in range(n * HT, (n + 1) * HT):
                    act.wait_ge(turned, t + 1)
                    act.activation(x1t[:, :, t * P:(t + 1) * P], ps_t[t % 2][:].rearrange("p (c t) -> p c t", c=C),
                                   ACT.Copy).then_inc(xt_f, 1)
                if n == 0:
                    split_w(1)
                    split_w(2)
            act.wait_ge(kv_in, 32)
            for k, (n, ft) in enumerate(steps):
                act.wait_ge(q_full, k + 1)
                if k >= 4:
                    act.wait_ge(q_out[k % 4], 16 * (k // 4))
                act.activation(q[:, k % 4, :], ps_q[k % 4][:], ACT.Copy).then_inc(q_made, 1)
                if k == 2 * C:
                    act.wait_ge(h_in, 16)
                    act.activation(hid[:, 0, HI, :, 0:CHUNKS[0][1]], hraw[:, :, 0:CHUNKS[0][1]], ACT.Copy).then_inc(h_hi, 1)
                if k < 2 * C:
                    if k == 0:
                        act.wait_ge(w_lo, FT // WT)
                    i, c = divmod(k, C)
                    act.activation(w_kv[:, HI, i, c, :], kvraw[:, i, c, :], ACT.Copy).then_inc(kv_hi, 1)

        @blk.vector
        def _(dve):
            for part, value in ((HI, 1.0), (LO, 0.0)):
                dve.memset(f(edge[:, part, :]), value).then_inc(edge_made, 1)
            for n in range(NHALF):
                half = slice(n * HT, (n + 1) * HT)
                tiles = range(n * HT, (n + 1) * HT)
                for t in tiles:
                    dve.bn_stats(stats[:, t, :], acc[:, t, :]).then_inc(stat_done, 1)
                for t in tiles:
                    dve.wait_ge(stat_done, t + 1)
                    dve.bn_aggr(mv[:, t, :], stats[:, t, :]).then_inc(mean_done, 1)
                dve.wait_ge(mean_done, (n + 1) * HT)
                dve.tensor_scalar(mv[:, half, 1], mv[:, half, 1], EPS, None, ALU.add).then_inc(eps_done, 1)
                dve.wait_ge(std_done, n + 1)
                dve.reciprocal(rstd[:, half], std[:, half]).then_inc(rstd_done, 1)
                dve.wait_ge(rstd_done, n + 1)
                for t in tiles:
                    dve.tensor_scalar(acc[:, t, :], acc[:, t, :], mv[:, t, 0:1], rstd[:, t:t + 1], ALU.subtract, ALU.mult)\
                       .then_inc(x1_done, 1)
                for t in tiles:
                    at = slice(t * P, (t + 1) * P)
                    dve.wait_ge(xt_f, t + 1)
                    dve.tensor_copy(xt[:, HI, :, at], x1t[:, :, at]).then_inc(xt_hi, 1)
                    dve.wait_ge(xt_hi, t + 1)
                    dve.tensor_tensor(xt[:, LO, :, at], x1t[:, :, at], f(xt[:, HI, :, at]), ALU.subtract).then_inc(xt_lo, 1)

        @blk.gpsimd
        def _(pool):
            for i in range(FT // WT):
                at = slice(i * WT * P, (i + 1) * WT * P)
                pool.wait_ge(w_hi, i + 1)
                pool.tensor_tensor(w[:, LO, :, at], wraw[:, :, at], f(w[:, HI, :, at]), ALU.subtract).then_inc(w_lo, 1)
            for k in range(2 * C):
                i, c = divmod(k, C)
                pool.wait_ge(kv_hi, k + 1)
                pool.tensor_tensor(w_kv[:, LO, i, c, :], kvraw[:, i, c, :], f(w_kv[:, HI, i, c, :]), ALU.subtract)\
                    .then_inc(kv_lo, 1)
            pool.wait_ge(h_hi, 1)
            n = CHUNKS[0][1]
            pool.tensor_tensor(hid[:, 0, LO, :, 0:n], hraw[:, :, 0:n], f(hid[:, 0, HI, :, 0:n]), ALU.subtract)\
                .then_inc(h_lo, 1)



CH = 256
CHUNKS = [(i * CH, CH) for i in range(6)] + [(6 * CH, S2 - 6 * CH)]
CHMAX = CHUNKS[-1][1]
TILES_OF_CHUNK = [[2 * i, 2 * i + 1] for i in range(6)] + [[14, 12, 13]]
KTILES = KV2 * HD2 // P
GROUPS = 2 * KV2
PAIRS = (NT2 + 1) // 2
STEPS = GROUPS * PAIRS
MAXW = ((0, 2 * BANK), (2 * BANK, S2 - 2 * BANK))


def projections():
    s = []
    for j in range(len(CHUNKS)):
        s += [("k", j, i) for i in range(KTILES)] + [("v", j, t) for t in TILES_OF_CHUNK[j]]
    late = s.pop(s.index(("v", len(CHUNKS) - 2, TILES_OF_CHUNK[-2][1])))
    s.insert(s.index(("v", len(CHUNKS) - 1, TILES_OF_CHUNK[-1][0])), late)
    return s


def schedule_b(last=False):
    s = []
    proj = projections()
    with_max = [("v", 4, t) for t in TILES_OF_CHUNK[4]] + [("k", 5, 1), ("v", 5, TILES_OF_CHUNK[5][0])] + proj[-4:]
    for k, p in enumerate(proj):
        if p[0] == "k" and p[2] == 0 and p[1] + 1 < len(CHUNKS):
            s += [("hidden", p[1] + 1)]
        if p in with_max:
            s += [("max", 0, with_max.index(p))]
        s += [("proj", k)]
        if p in (("k", 1, 2), ("k", 3, 2)):
            s += [("queries", p[1] // 2)]
    s += [("row", 0)]
    for k in range(STEPS):
        g, j = divmod(k, PAIRS)
        more = g + 1 < GROUPS
        if more and j == 0:
            s += [("max", g + 1, 0)]
        step = [("scores", k)] + [("pv", k - 2)] * (k >= 2)
        s += step if j else step[::-1]
        if more and j == PAIRS - 1:
            s += [("row", g + 1)]
        if more and j < PAIRS - 1:
            s += [("max", g + 1, j + 1)]
        if g and j == 3:
            s += [("sums", g - 1)]
        if g and j == 4:
            s += [("spread", g - 1)]
        if g in (2, 4) and j == 1:
            s += [("queries", g // 2 + 1)]
        if g == GROUPS - 1 and j == 5:
            s += [("hidden", 0, 1)]
    s += [("split", STEPS - 1), ("pv", STEPS - 2), ("pv", STEPS - 1), ("sums", GROUPS - 1), ("spread", GROUPS - 1)]
    ahead = ("hidden", 0, 1)
    return [((x[:-1], 1) if x == ahead else (x, 0)) for x in s if not (last and x == ahead)]


def cross_attention(nc, idf, edges, ctx_t, w_kv, hraw, hid, x1t_dram, q_dram, q_out, y_dram, y_out, last_loads):
    proj = projections()
    NP = len(proj)
    NCH = len(CHUNKS)
    w_k, w_v = w_kv[:, :, 0], w_kv[:, :, 1]

    with ExitStack() as st:
        def sb(name, shape, dt=F32):
            return st.enter_context(nc.sbuf_tensor(name, shape, dt))

        def sem(name, per=0, start=0):
            return Sem(nc, st, name, per, start)

        kt = sb("b_kt", [ROWB + 1, 2, KV2, S2], F32R)
        v = sb("b_v", [P, 2, NT2, KV2, HD2 + 1], F32R)
        q = sb("b_q", [ROWB + 1, 2, 2, G2 * T], F32R)
        qraw = sb("b_qraw", [HD2, G2 * T])
        pf = sb("b_pf", [P, 2, 2 * BANK])
        pr = sb("b_pr", [P, 2, 2, 2 * BANK], F32R)
        o = sb("b_o", [P, BANK])
        y = st.enter_context(nc.sbuf_tensor("b_y", [HD2, 2, BANK], F32, side="right"))
        mx = sb("b_mx", [P, 2, 4, 2])
        neg = sb("b_neg", [P, 2, 4], F32R)
        rec = sb("b_rec", [32, BANK // 32])
        recs = sb("b_recs", [HD2, BANK])
        idr = sb("b_idr", [P, P], F32R)

        ps_s = [st.enter_context(nc.psum_tensor(f"b_s{i}", [P, 2 * BANK], F32)) for i in range(2)]
        ps_m = st.enter_context(nc.psum_tensor("b_m", [P, 2 * BANK], F32))
        ps_o = st.enter_context(nc.psum_tensor("b_o_ps", [P, BANK], F32))
        ps_x = st.enter_context(nc.psum_tensor("b_x", [P, BANK], F32))

        const_made, edges_in, late_in = sem("b_const_made"), sem("b_edges_in"), sem("b_late_in")
        h_in = sem("b_h_in", 16 * NCH + 16)
        h_hi, h_lo = sem("b_h_hi", NCH), sem("b_h_lo", NCH * C)
        q_in, q_hi, q_lo = sem("b_q_in", 16 * KV2), sem("b_q_hi", KV2), sem("b_q_lo", KV2)
        full, kv_hi, kv_lo = sem("b_full", NP), sem("b_kv_hi", NP), sem("b_kv_lo", NP)
        m_full, mx_made = sem("b_m_full", 8 * GROUPS), sem("b_mx_made", 8 * GROUPS, 1)
        neg_made, row_full, row_made = sem("b_neg_made", GROUPS), sem("b_row_full", GROUPS), sem("b_row_made", GROUPS)
        s_made, exp_done = sem("b_s_made", STEPS), sem("b_exp_done", STEPS, 2)
        p_hi, p_lo, pv_done = sem("b_p_hi", STEPS), sem("b_p_lo", STEPS, 2), sem("b_pv_done", STEPS)
        o_out, columns, recips, recs_made, spread = (
            sem(f"b_{k}", GROUPS, start) for k, start in (("o_out", 1), ("columns", 0), ("recips", 0), ("recs_made", 0),
                                                          ("spread", 0)))
        y_made = sem("b_y_made", GROUPS, 1)

        blk = st.enter_context(nc.Block())

        def bank_of(k):
            s = ps_s[(k % 4) // 2]
            return s[:, (k % 2) * BANK:(k % 2 + 1) * BANK]

        def key_parts(i, bank, c0, n):
            own, share = kt[0:HD2, :, i, c0:c0 + n], kt[i * 32:(i + 1) * 32, :, KV2 - 1, c0:c0 + n]
            return (((own[:, HI], own[:, LO]), bank[0:HD2, 0:n]), ((share[:, HI], share[:, LO]), bank[HD2:P, 0:n]))

        def keys_of(k):
            j = k % PAIRS
            return [(i, 2 * j + i) for i in range(2) if 2 * j + i < NT2]

        def shape_of(k):
            tiles = keys_of(k)
            return KT2[tiles[-1][1]][1], BANK * len(tiles)

        def run(e, handle):
            with e.Fori(0, B - 1) as b:
                for step, ahead in schedule_b():
                    handle(step, b + ahead)
            for step, ahead in schedule_b(last=True):
                handle(step, B - 1)

        def high_part(act, b, k):
            rows, n = shape_of(k)
            act.wait_ge(exp_done.sem, exp_done.at(b, k + 1))
            if k >= 2:
                act.wait_ge(pv_done.sem, pv_done.at(b, k - 1))
            act.activation(pr[0:rows, k % 2, HI, 0:n], pf[0:rows, k % 2, 0:n], ACT.Copy).then_inc(p_hi.sem, 1)

        def low_part(dve, b, k):
            rows, n = shape_of(k)
            dve.wait_ge(p_hi.sem, p_hi.at(b, k + 1))
            dve.tensor_tensor(pr[0:rows, k % 2, LO, 0:n], pf[0:rows, k % 2, 0:n], f(pr[0:rows, k % 2, HI, 0:n]),
                              ALU.subtract).then_inc(p_lo.sem, 1)

        def split_hidden(act, b, j):
            n = CHUNKS[j][1]
            act.wait_ge(h_in.sem, h_in.at(b, 16 * (j + 1) + (16 if j == NCH - 1 else 0)))
            if j >= 2:
                act.wait_ge(full.sem, full.at(b, max(k for k, p in enumerate(proj) if p[1] == j - 2) + 1))
            act.activation(hid[:, j % 2, HI, :, 0:n], hraw[:, :, 0:n], ACT.Copy).then_inc(h_hi.sem, 1)

        @blk.sync
        def _(sp):
            def load_chunk(b, j):
                c0, n = CHUNKS[j]
                own = min(n, CTXP - c0)
                sp.dma_start(hraw[:, :, 0:own], ctx_t[b, :, :, c0:c0 + own]).then_inc(h_in.sem, 16)
                if own < n:
                    sp.dma_start(hraw[:, :, own:n], x1t_dram[:, :, b * T:(b + 1) * T]).then_inc(h_in.sem, 16)

            def load_queries(b, kv):
                at = kv * G2 * HD2
                sp.dma_start(qraw[:].rearrange("d (h t) -> d h t", h=G2),
                             q_dram[at:at + G2 * HD2, b * T:(b + 1) * T].rearrange("(h d) t -> d h t", h=G2))\
                  .then_inc(q_in.sem, 16)

            load_chunk(0, 1)
            for s in q_out:
                sp.wait_ge(s, 16 * NHALF * H2 * HD2 // P // len(q_out))
            for dst, src in ((kt[ROWB:ROWB + 1], edges[:, :, 0:KV2 * S2].rearrange("o r (h s) -> o r h s", h=KV2)),
                             (q[ROWB:ROWB + 1, :, LO, :], edges[:, LO:LO + 1, 0:2 * G2 * T].rearrange("o r (h s) -> o (r h) s", h=2))):
                sp.dma_start(f(dst), src).then_inc(edges_in.sem, 16)
            load_queries(0, 0)
            for b in range(B):
                for j in range(2, NCH):
                    sp.wait_ge(h_lo.sem, h_lo.at(b, j * C))
                    load_chunk(b, j)
                    if j == 3:
                        sp.wait_ge(q_lo.sem, q_lo.at(b, 1))
                        load_queries(b, 1)
                sp.wait_ge(h_lo.sem, h_lo.at(b, NCH * C))
                if b + 1 < B:
                    load_chunk(b + 1, 0)
                sp.wait_ge(q_lo.sem, q_lo.at(b, 2))
                load_queries(b, 2)
                if b + 1 == B:
                    sp.wait_ge(full.sem, full.at(b, NP))
                    for s in y_out:
                        sp.wait_ge(s.sem, s.at(1, 0))
                    for dst, src in last_loads:
                        sp.dma_start(dst, src).then_inc(late_in.sem, 16)
                for g in range(GROUPS):
                    sp.wait_ge(y_made.sem, y_made.at(b, g + 1))
                    sp.dma_start(y_dram[2 * g * HD2:2 * (g + 1) * HD2, b * T:(b + 1) * T].rearrange("(h d) t -> d h t", h=2),
                                 y[:, g % 2, :].rearrange("d (h t) -> d h t", h=2)).then_inc(y_out[g % 2].sem, 16)
                    if g == 2:
                        sp.wait_ge(q_lo.sem, q_lo.at(b, 3))
                        load_queries(b, 3)
                    if g == 4 and b + 1 < B:
                        sp.wait_ge(q_lo.sem, q_lo.at(b, 4))
                        load_queries(b + 1, 0)
                    if g == 6 and b + 1 < B:
                        sp.wait_ge(h_lo.sem, h_lo.at(b + 1, C))
                        load_chunk(b + 1, 1)
            sp.wait_ge(late_in.sem, 16 * len(last_loads))

        @blk.tensor
        def _(pe):
            def project(k, b):
                kind, j, i = proj[k]
                c0, n = CHUNKS[j]
                if (kind, i) == ("k", 0):
                    pe.wait_ge(h_hi.sem, h_hi.at(b, j + 1))
                    pe.wait_ge(h_lo.sem, h_lo.at(b, (j + 1) * C))
                if k >= 4:
                    pe.wait_ge(kv_lo.sem, kv_lo.at(b, k - 3))
                else:
                    pe.wait_ge(exp_done.sem, exp_done.at(b, 0))
                bank, s = bank_of(k), 0
                for c in range(C):
                    for a, m in PARTS:
                        if kind == "k":
                            mm = pe.matmul(bank[:, 0:n], w_k[:, a, c, i * P:(i + 1) * P],
                                           hid[:, j % 2, m, c, 0:n], start=s == 0, stop=s == 3 * C - 1)
                        else:
                            t0, rows = KT2[i]
                            mm = pe.matmul(bank[0:rows, 0:KV2 * HD2], hid[:, j % 2, a, c, t0 - c0:t0 - c0 + rows],
                                           w_v[:, m, c, :], start=s == 0, stop=s == 3 * C - 1)
                        s += 1
                mm.then_inc(full.sem, 1)

            def coarse(g, i, b):
                kv, hp = divmod(g, 2)
                half, t = divmod(i, 4)
                if g == 0 and t == 0:
                    last = ("k", NCH - 1 if half else 3, KTILES - 1)
                    pe.wait_ge(kv_hi.sem, kv_hi.at(b, proj.index(last) + 1))
                if hp == 0 and i == 0:
                    pe.wait_ge(q_hi.sem, q_hi.at(b, kv + 1))
                pe.wait_ge(mx_made.sem, mx_made.at(b, 8 * g + i))
                c0, n = MAXW[half]
                for x in range(0, n, BANK):
                    mm = pe.matmul(ps_m[:, x:min(x + BANK, n)], q[0:HD2, kv % 2, HI, hp * BANK + t * P:hp * BANK + (t + 1) * P],
                                   kt[0:HD2, HI, kv, c0 + x:c0 + min(x + BANK, n)], start=True, stop=True)
                mm.then_inc(m_full.sem, 1)

            def shift_row(g, b):
                if g == 0:
                    pe.wait_ge(const_made.sem, 5)
                pe.wait_ge(neg_made.sem, neg_made.at(b, g + 1))
                if g:
                    pe.wait_ge(row_made.sem, row_made.at(b, g))
                for t in range(4):
                    mm = pe.transpose(ps_x[0:1, t * P:(t + 1) * P].bitcast(F32R), neg[:, g % 2, t:t + 1], idr[:])
                mm.then_inc(row_full.sem, 1)

            def scores(k, b):
                g = k // PAIRS
                kv, hp = divmod(g, 2)
                if k == 0:
                    pe.wait_ge(edges_in.sem, 32)
                    pe.wait_ge(kv_lo.sem, kv_lo.at(b, NP))
                if k % PAIRS == 0:
                    pe.wait_ge(row_made.sem, row_made.at(b, g + 1))
                    pe.wait_ge(q_lo.sem, q_lo.at(b, kv + 1))
                pe.wait_ge(exp_done.sem, exp_done.at(b, k - 1))
                for i, t in keys_of(k):
                    t0, rows = KT2[t]
                    for s, (a, m) in enumerate(PARTS):
                        mm = pe.matmul(ps_s[k % 2][0:rows, i * BANK:(i + 1) * BANK], kt[:, a, kv, t0:t0 + rows],
                                       q[:, kv % 2, m, hp * BANK:(hp + 1) * BANK], start=s == 0, stop=s == 2)
                mm.then_inc(s_made.sem, 1)

            def values(k, b):
                g, j = divmod(k, PAIRS)
                pe.wait_ge(p_hi.sem, p_hi.at(b, k + 1))
                pe.wait_ge(p_lo.sem, p_lo.at(b, k + 1))
                if j == 0:
                    pe.wait_ge(o_out.sem, o_out.at(b, g))
                for i, t in keys_of(k):
                    rows = KT2[t][1]
                    for s, (a, m) in enumerate(PARTS):
                        mm = pe.matmul(ps_o[0:HD2 + 1, :], v[0:rows, a, t, g // 2, :],
                                       pr[0:rows, k % 2, m, i * BANK:(i + 1) * BANK],
                                       start=t == 0 and s == 0, stop=t == NT2 - 1 and s == 2)
                mm.then_inc(pv_done.sem, 1)

            def handle(step, b):
                kind, *arg = step
                todo = {"proj": project, "max": coarse, "row": shift_row, "scores": scores, "pv": values}
                if kind in todo:
                    todo[kind](*arg, b)

            run(pe, handle)

        @blk.scalar
        def _(act):
            act.sem_inc(h_hi.sem, 1)
            act.sem_inc(exp_done.sem, 2)
            act.sem_inc(o_out.sem, 1)

            def handle(step, b):
                kind, *arg = step
                if kind == "hidden":
                    split_hidden(act, b, arg[0])
                elif kind == "queries":
                    kv = arg[0]
                    act.wait_ge(q_in.sem, q_in.at(b, 16 * (kv + 1)))
                    if kv >= 2:
                        act.wait_ge(s_made.sem, s_made.at(b, (kv - 1) * 2 * PAIRS))
                    act.activation(q[0:HD2, kv % 2, HI, :], qraw[:], ACT.Copy).then_inc(q_hi.sem, 1)
                elif kind == "proj":
                    k = arg[0]
                    what, j, i = proj[k]
                    c0, n = CHUNKS[j]
                    act.wait_ge(full.sem, full.at(b, k + 1))
                    if what == "k":
                        for dst, src in key_parts(i, bank_of(k), c0, n):
                            s = act.activation(dst[HI], src, ACT.Copy)
                        s.then_inc(kv_hi.sem, 1)
                    else:
                        rows = KT2[i][1]
                        act.activation(v[0:rows, HI, i, :, 0:HD2],
                                       bank_of(k)[0:rows, 0:KV2 * HD2].rearrange("p (h d) -> p h d", h=KV2), ACT.Copy)\
                           .then_inc(kv_hi.sem, 1)
                elif kind == "row":
                    g = arg[0]
                    kv, hp = divmod(g, 2)
                    act.wait_ge(row_full.sem, row_full.at(b, g + 1))
                    act.activation(q[ROWB:ROWB + 1, kv % 2, HI, hp * BANK:(hp + 1) * BANK], ps_x[0:1, :], ACT.Copy)\
                       .then_inc(row_made.sem, 1)
                elif kind == "scores":
                    k = arg[0]
                    if k:
                        high_part(act, b, k - 1)
                    rows, n = shape_of(k)
                    act.wait_ge(s_made.sem, s_made.at(b, k + 1))
                    act.wait_ge(p_lo.sem, p_lo.at(b, k - 1))
                    act.activation(pf[0:rows, k % 2, 0:n], ps_s[k % 2][0:rows, 0:n], ACT.Exp, scale=SCALE_B)\
                       .then_inc(exp_done.sem, 1)
                elif kind == "split":
                    high_part(act, b, arg[0])
                elif kind == "pv" and arg[0] % PAIRS == PAIRS - 1:
                    k = arg[0]
                    g = k // PAIRS
                    act.wait_ge(pv_done.sem, pv_done.at(b, k + 1))
                    act.wait_ge(y_made.sem, y_made.at(b, g))
                    act.activation(o[0:HD2 + 1, :], ps_o[0:HD2 + 1, :], ACT.Copy).then_inc(o_out.sem, 1)
                elif kind == "spread":
                    g = arg[0]
                    act.wait_ge(recs_made.sem, recs_made.at(b, g + 1))
                    for i in range(32, HD2, 32):
                        s = act.activation(recs[i:i + 32, :], recs[0:32, :], ACT.Copy)
                    s.then_inc(spread.sem, 1)

            run(act, handle)

        @blk.vector
        def _(dve):
            dve.sem_inc(mx_made.sem, 1)
            dve.sem_inc(p_lo.sem, 2)
            dve.memset(o[HD2:P, :], 1.0).then_inc(const_made.sem, 1)
            for ap, value in ((v[:, HI, :, :, HD2], 1.0), (v[:, LO, :, :, HD2], 0.0)):
                dve.memset(f(ap), value).then_inc(const_made.sem, 1)
            dve.tensor_copy(idr[:], idf[:]).then_inc(const_made.sem, 2)

            def handle(step, b):
                kind, *arg = step
                if kind == "proj":
                    k = arg[0]
                    what, j, i = proj[k]
                    c0, n = CHUNKS[j]
                    dve.wait_ge(kv_hi.sem, kv_hi.at(b, k + 1))
                    if what == "k":
                        for dst, src in key_parts(i, bank_of(k), c0, n):
                            s = dve.tensor_tensor(dst[LO], src, f(dst[HI]), ALU.subtract)
                        s.then_inc(kv_lo.sem, 1)
                    else:
                        rows = KT2[i][1]
                        dve.tensor_tensor(v[0:rows, LO, i, :, 0:HD2],
                                          bank_of(k)[0:rows, 0:KV2 * HD2].rearrange("p (h d) -> p h d", h=KV2),
                                          f(v[0:rows, HI, i, :, 0:HD2]), ALU.subtract).then_inc(kv_lo.sem, 1)
                elif kind == "max":
                    g, i = arg
                    half, t = divmod(i, 4)
                    dve.wait_ge(m_full.sem, m_full.at(b, 8 * g + i + 1))
                    dve.reduce_max(mx[:, g % 2, t, half:half + 1], ps_m[:, 0:MAXW[half][1]], X).then_inc(mx_made.sem, 1)
                    if i == 7:
                        dve.wait_ge(mx_made.sem, mx_made.at(b, 8 * g + 8))
                        dve.reduce_max(neg[:, g % 2, :], mx[:, g % 2], X, negate=True).then_inc(neg_made.sem, 1)
                elif kind == "scores" and arg[0] or kind == "split":
                    low_part(dve, b, arg[0] - (kind == "scores"))
                elif kind == "sums":
                    g = arg[0]
                    dve.wait_ge(o_out.sem, o_out.at(b, g + 1))
                    dve.wait_ge(y_made.sem, y_made.at(b, g))
                    dve.transpose(recs[0:32, :], o[HD2:P, :]).then_inc(columns.sem, 1)
                    dve.wait_ge(columns.sem, columns.at(b, g + 1))
                    dve.reciprocal(rec[:], recs[0:32, :].rearrange("p (b j) -> p b j", j=32)[:, :, 0]).then_inc(recips.sem, 1)
                    dve.wait_ge(recips.sem, recips.at(b, g + 1))
                    dve.transpose(recs[0:32, :], rec[:].rearrange("p (b o) -> p b o", o=1).to_broadcast([32, BANK // 32, 32]))\
                       .then_inc(recs_made.sem, 1)

            run(dve, handle)

        @blk.gpsimd
        def _(pool):
            for s in y_out:
                pool.sem_inc(s.sem, 16)
            pool.sem_inc(y_made.sem, 1)
            pool.sem_inc(h_in.sem, 16)
            pool.sem_inc(h_lo.sem, C)

            def handle(step, b):
                kind, *arg = step
                if kind == "hidden":
                    j = arg[0]
                    n = CHUNKS[j][1]
                    pool.wait_ge(h_hi.sem, h_hi.at(b, j + 1))
                    for c in range(C):
                        pool.tensor_tensor(hid[:, j % 2, LO, c, 0:n], hraw[:, c, 0:n], f(hid[:, j % 2, HI, c, 0:n]),
                                           ALU.subtract).then_inc(h_lo.sem, 1)
                elif kind == "spread":
                    g = arg[0]
                    pool.wait_ge(spread.sem, spread.at(b, g + 1))
                    s = y_out[g % 2]
                    pool.wait_ge(s.sem, s.at(b, 16 * (g // 2)))
                    pool.tensor_tensor(y[:, g % 2, :], recs[:], o[0:HD2, :], ALU.mult).then_inc(y_made.sem, 1)
                elif kind == "queries":
                    kv = arg[0]
                    pool.wait_ge(q_hi.sem, q_hi.at(b, kv + 1))
                    pool.tensor_tensor(q[0:HD2, kv % 2, LO, :], qraw[:], f(q[0:HD2, kv % 2, HI, :]), ALU.subtract)\
                        .then_inc(q_lo.sem, 1)

            run(pool, handle)



def finish(nc, idf, woraw, y_first, wt, la, lb, lora_w, bias, x1_dram, y_dram, y_out, out_dram):
    ALPHA_OVER_RANK = 2.0
    FT = H2 * HD2 // P
    with ExitStack() as st:
        def sb(name, shape, dt=F32):
            return st.enter_context(nc.sbuf_tensor(name, shape, dt))

        def sem(name):
            return st.enter_context(nc.semaphore(name))

        x1 = sb("c_x1", [P, TILES, D])
        y_later = sb("c_yraw", [P, FT, T])
        y = sb("c_y", [P, 2, 2, FT, T], F32R)
        wo_s = sb("c_wo", [P, 2, FT, D], F32R)
        lw, bias_s = sb("c_lw", [P, 1]), sb("c_bias", [P, D])
        ws = sb("c_ws", [P, 2, C, D], F32R)
        x2 = sb("c_x2", [P, 2, D])
        x2t = sb("c_x2t", [P, 2, D], F32R)
        z = sb("c_z", [P, 2, D])
        stats, mv = sb("c_stats", [P, 2, 6]), sb("c_mv", [P, 2, 2])
        std, rstd = sb("c_std", [P, 2]), sb("c_rstd", [P, 2])
        ps_w = [st.enter_context(nc.psum_tensor(f"c_w{i}", [P, BANK], F32)) for i in range(2)]
        ps_y = [st.enter_context(nc.psum_tensor(f"c_y{i}", [P, BANK], F32)) for i in range(2)]
        ps_t, ps_f = (st.enter_context(nc.psum_tensor(f"c_{k}_ps", [P, BANK], F32)) for k in "tf")

        names = ("lw_in bias_in lb_done w_full w_sum w_hi w_lo wo_hi wo_lo y_in y_hi y_lo y_full turned t_hi t_lo "
                 "f_full z_done stat_done mean_done eps_done std_done rstd_done normed biased").split()
        (lw_in, bias_in, lb_done, w_full, w_sum, w_hi, w_lo, wo_hi, wo_lo, y_in, y_hi, y_lo, y_full, turned, t_hi,
         t_lo, f_full, z_done, stat_done, mean_done, eps_done, std_done, rstd_done, normed, biased) = (
            sem(f"c_{n}") for n in names)
        x1_in = [sem(f"c_x1_in{i}") for i in range(2)]
        out_done = [sem(f"c_out_done{i}") for i in range(2)]

        norms = []
        for t in range(TILES + 1):
            norms += [(t, 0)] * (t < TILES) + [(t - 1, 1)] * (t >= 1)
        nth = {x: i for i, x in enumerate(norms)}
        blk = st.enter_context(nc.Block())

        def yraw(b):
            return y_later if b else y_first

        @blk.sync
        def _(sp):
            sp.dma_start(lw[:], lora_w).then_inc(lw_in, 16)
            sp.dma_start(x1[:, 0:2, :], x1_dram[:, 0:2, :]).then_inc(x1_in[0], 16)
            sp.dma_start(bias_s[:], bias.to_broadcast([P, D])).then_inc(bias_in, 16)
            for s in y_out:
                sp.wait_ge(s.sem, s.at(B - 1, 16 * GROUPS // 2))
            for b in range(1, B):
                if b >= 2:
                    sp.wait_ge(y_lo, FT * b)
                sp.dma_start(y_later[:], y_dram[:, b * T:(b + 1) * T].rearrange("(k p) t -> p k t", p=P)).then_inc(y_in, 16)
                if b == 1:
                    sp.dma_start(x1[:, 2:TILES, :], x1_dram[:, 2:TILES, :]).then_inc(x1_in[1], 16)
            for t in range(TILES):
                sp.wait_ge(normed, nth[(t, 1)] + 1)
                sp.dma_start(out_dram[t * P:(t + 1) * P, :], z[:, t % 2, :]).then_inc(out_done[t % 2], 16)
            for i in range(2):
                sp.wait_ge(out_done[i], 16 * (TILES // 2))

        @blk.tensor
        def _(pe):
            def project(t):
                b = t // 2
                if t >= 2:
                    pe.wait_ge(z_done, nth[(t - 2, 0)] + 1)
                for k in range(FT):
                    if k == FT - 3 and t:
                        turn(t - 1)
                    if t % 2 == 0:
                        pe.wait_ge(y_lo, FT * b + k + 1)
                    if t == 0:
                        pe.wait_ge(wo_lo, k + 1)
                    for i, (a, m) in enumerate(PARTS):
                        mm = pe.matmul(ps_y[t % 2][:], y[:, b % 2, a, k, (t % 2) * P:(t % 2 + 1) * P], wo_s[:, m, k, :],
                                       start=k == 0 and i == 0, stop=k == FT - 1 and i == 2)
                mm.then_inc(y_full, 1)

            def turn(t):
                pe.wait_ge(normed, nth[(t, 0)] + 1)
                if t:
                    pe.wait_ge(t_lo, t)
                for c in range(C):
                    mm = pe.transpose(ps_t[:, c * P:(c + 1) * P], x2[:, t % 2, c * P:(c + 1) * P], idf[:])
                mm.then_inc(turned, 1)

            def feed(t):
                pe.wait_ge(t_hi, t + 1)
                pe.wait_ge(t_lo, t + 1)
                pe.wait_ge(w_lo, C)
                if t:
                    pe.wait_ge(z_done, nth[(t - 1, 1)] + 1)
                i = 0
                for c in range(C):
                    for a, m in PARTS:
                        mm = pe.matmul(ps_f[:], x2t[:, a, c * P:(c + 1) * P], ws[:, m, c, :], start=i == 0, stop=i == 3 * C - 1)
                        i += 1
                mm.then_inc(f_full, 1)

            def adapters():
                pe.wait_ge(lb_done, 1)
                for c in range(C):
                    if c >= 2:
                        pe.wait_ge(w_sum, c - 1)
                    pe.matmul(ps_w[c % 2][:], la[:, c * P:(c + 1) * P], lb[:], start=True, stop=True).then_inc(w_full, 1)

            for t in range(TILES + 1):
                if t < TILES:
                    project(t)
                else:
                    turn(t - 1)
                if t == 0:
                    adapters()
                if t >= 1:
                    feed(t - 1)

        @blk.scalar
        def _(act):
            def split_y(b, k0, n):
                if b >= 1:
                    act.wait_ge(y_in, 16 * b)
                if b >= 2:
                    act.wait_ge(y_full, 2 * (b - 1))
                act.activation(y[:, b % 2, HI, k0:k0 + n, :], yraw(b)[:, k0:k0 + n, :], ACT.Copy).then_inc(y_hi, n)

            for k in range(FT):
                act.activation(wo_s[:, HI, k, :], woraw[:, k, :], ACT.Copy).then_inc(wo_hi, 1)
                split_y(0, k, 1)
            for c in range(C):
                act.wait_ge(w_sum, c + 1)
                act.activation(ws[:, HI, c, :], wt[:, c, :], ACT.Copy).then_inc(w_hi, 1)
            for i, (t, which) in enumerate(norms):
                act.wait_ge(eps_done, i + 1)
                act.activation(std[:, i % 2:i % 2 + 1], mv[:, i % 2, 1:2], ACT.Sqrt).then_inc(std_done, 1)
                if which == 0:
                    if t % 2 == 0 and t // 2 + 1 < B:
                        for k in range(0, FT, 4):
                            split_y(t // 2 + 1, k, 4)
                    act.wait_ge(turned, t + 1)
                    if t:
                        act.wait_ge(f_full, t)
                    act.activation(x2t[:, HI, :], ps_t[:], ACT.Copy).then_inc(t_hi, 1)

        @blk.vector
        def _(dve):
            for k in range(FT):
                dve.wait_ge(wo_hi, k + 1)
                dve.tensor_tensor(wo_s[:, LO, k, :], woraw[:, k, :], f(wo_s[:, HI, k, :]), ALU.subtract).then_inc(wo_lo, 1)
                if k == 3:
                    dve.wait_ge(lw_in, 16)
                    dve.tensor_scalar(lb, lb, lw[:, 0:1], ALPHA_OVER_RANK, ALU.mult, ALU.mult).then_inc(lb_done, 1)
            for c in range(C):
                dve.wait_ge(w_full, c + 1)
                dve.tensor_tensor(wt[:, c, :], ps_w[c % 2][:], wt[:, c, :], ALU.add).then_inc(w_sum, 1)
            dve.wait_ge(bias_in, 16)

            def split_turned(t):
                dve.wait_ge(t_hi, t + 1)
                dve.tensor_tensor(x2t[:, LO, :], ps_t[:], f(x2t[:, HI, :]), ALU.subtract).then_inc(t_lo, 1)

            for i, (t, which) in enumerate(norms):
                s = i % 2
                if which == 0:
                    if t:
                        split_turned(t - 1)
                    dve.wait_ge(y_full, t + 1)
                    dve.wait_ge(x1_in[t >= 2], 16)
                    dve.tensor_tensor(x2[:, t % 2, :], ps_y[t % 2][:], x1[:, t, :], ALU.add).then_inc(z_done, 1)
                    row = x2[:, t % 2, :]
                else:
                    if t == TILES - 1:
                        split_turned(t)
                    dve.wait_ge(turned, t + 1)
                    dve.tensor_tensor(x2[:, t % 2, :], x2[:, t % 2, :], bias_s[:], ALU.add).then_inc(biased, 1)
                    dve.wait_ge(f_full, t + 1)
                    dve.wait_ge(biased, t + 1)
                    if t >= 2:
                        dve.wait_ge(out_done[t % 2], 16 * (t // 2))
                    dve.tensor_tensor(z[:, t % 2, :], ps_f[:], x2[:, t % 2, :], ALU.add).then_inc(z_done, 1)
                    row = z[:, t % 2, :]
                dve.wait_ge(z_done, i + 1)
                dve.bn_stats(stats[:, s, :], row).then_inc(stat_done, 1)
                dve.wait_ge(stat_done, i + 1)
                dve.bn_aggr(mv[:, s, :], stats[:, s, :]).then_inc(mean_done, 1)
                dve.wait_ge(mean_done, i + 1)
                dve.tensor_scalar(mv[:, s, 1:2], mv[:, s, 1:2], EPS, None, ALU.add).then_inc(eps_done, 1)
                dve.wait_ge(std_done, i + 1)
                dve.reciprocal(rstd[:, s:s + 1], std[:, s:s + 1]).then_inc(rstd_done, 1)
                dve.wait_ge(rstd_done, i + 1)
                dve.tensor_scalar(row, row, mv[:, s, 0:1], rstd[:, s:s + 1], ALU.subtract, ALU.mult).then_inc(normed, 1)

        @blk.gpsimd
        def _(pool):
            def split_y(b, k0, n):
                pool.wait_ge(y_hi, FT * b + k0 + n)
                pool.tensor_tensor(y[:, b % 2, LO, k0:k0 + n, :], yraw(b)[:, k0:k0 + n, :], f(y[:, b % 2, HI, k0:k0 + n, :]),
                                   ALU.subtract).then_inc(y_lo, n)

            for k in range(FT):
                split_y(0, k, 1)
            for c in range(C):
                pool.wait_ge(w_hi, c + 1)
                pool.tensor_tensor(ws[:, LO, c, :], wt[:, c, :], f(ws[:, HI, c, :]), ALU.subtract).then_inc(w_lo, 1)
            for b in range(1, B):
                for k in range(0, FT, 4):
                    split_y(b, k, 4)



def program(nc, x_t, x_rows, w_qkv, w_o, cos_t, sin_t, mask, eye, ctx_t, wq, wk, wv, wo2, w_t, lora_a, lora_bt,
            lora_w, bias, out):
    FT = H2 * HD2 // P
    x1_dram = nc.dram_tensor("x1_rows", [P, TILES, D], F32).ap()
    x1t_dram = nc.dram_tensor("x1_t", [P, C, TOK], F32).ap()
    q_dram = nc.dram_tensor("queries", [H2 * HD2, TOK], F32).ap()
    edges = nc.dram_tensor("edges", [1, 2, P * EDGE], F32).ap()
    y_dram = nc.dram_tensor("attended", [H2 * HD2, TOK], F32).ap()
    with ExitStack() as outer:
        def sb(stack, name, shape, dt=F32):
            return stack.enter_context(nc.sbuf_tensor(name, shape, dt))

        def arena(stack, name, nbytes):
            base = nc.sbuf_base
            stack.enter_context(nc.sbuf_tensor(name, [P, nbytes // 4], F32))
            return base

        def at(address, name, shape, dt=F32):
            return nc.alloc_sbuf_tensor_at(name, shape, dt, offset=address)

        idf = sb(outer, "idf", [P, P])
        w_mem = arena(outer, "w_mem", 4 * 2 * C * FEAT_A)
        raw_mem = arena(outer, "raw_mem", 4 * 2 * FEAT_A)
        q_out = [outer.enter_context(nc.semaphore(f"q_out{i}")) for i in range(4)]
        y_out = [Sem(nc, outer, f"y_out{i}", 16 * GROUPS // 2, 16) for i in range(2)]
        with ExitStack() as st:
            acc = st.enter_context(nc.sbuf_tensor("acc", [P, TILES, D], F32, side="right"))
            w_a = at(w_mem, "w_a", [P, 2, C, FEAT_A], F32R)
            wq_raw = at(w_mem, "wq_raw", [P, C, H2 * HD2])
            w_kv = at(w_mem, "w_kv", [P, 2, 2, C, KV2 * HD2], F32R)
            raw = at(raw_mem, "raw_a", [P, 2, FEAT_A])
            hraw = at(raw_mem, "hraw", [P, C, CHMAX])
            self_attention(nc, x_t, x_rows, w_qkv, w_o, cos_t, sin_t, mask, eye, idf, acc, w_a, raw, (wq_raw[:], wq))
            hid_mem = arena(outer, "hid_mem", 4 * 2 * 2 * C * CHMAX)
            hid = at(hid_mem, "hid", [P, 2, 2, C, CHMAX], F32R)
            between(nc, idf, wq_raw, acc, wk, wv, ctx_t, w_kv, hraw, hid, x1_dram, x1t_dram, q_dram, q_out, edges)
        wo_raw = at(w_mem, "wo_raw", [P, FT, D])
        y_first, wt = at(hid_mem, "y_first", [P, FT, T]), at(hid_mem + 4 * FT * T, "wt", [P, C, D])
        lora = at(raw_mem, "lora", [P, 2, D])
        la, lb = lora[:, 0, :], lora[:, 1, :]
        loads = ((y_first[:], y_dram[:, 0:T].rearrange("(k p) t -> p k t", p=P)), (wo_raw[:], wo2), (wt[:], w_t), (la, lora_a),
                 (lb, lora_bt))
        cross_attention(nc, idf, edges, ctx_t, w_kv, hraw, hid, x1t_dram, q_dram, q_out, y_dram, y_out, loads)
        finish(nc, idf, wo_raw, y_first, wt, la, lb, lora_w, bias, x1_dram, y_dram, y_out, out)


def kernel(x, ctx_4096, L0_attn_w_qkv, L0_attn_w_o, L0_xattn_Wq, L0_xattn_Wk, L0_xattn_Wv, L0_xattn_Wo,
           L0_ffn_lora_A, L0_ffn_lora_B, L0_ffn_W, L0_ffn_bias, L0_ffn_lora_weights):
    import concourse.bacc as bacc
    from concourse.bass_utils import run_bass_kernel_spmd

    def chunked(w):
        return w.reshape(C, P, -1).transpose(1, 0, 2)

    x, ctx = np.asarray(x), np.asarray(ctx_4096)
    rows = x.reshape(TOK, D)
    w = np.asarray(L0_attn_w_qkv).reshape(C, P, -1)
    q_cols, kv_cols = KVH * GRP * HD, KVH * HD
    w = np.concatenate([w[:, :, :q_cols].reshape(C, P, KVH, GRP * HD),
                        w[:, :, q_cols:q_cols + kv_cols].reshape(C, P, KVH, HD),
                        w[:, :, q_cols + kv_cols:].reshape(C, P, KVH, HD)], axis=-1)
    inv = (1.0 / np.power(np.float32(10000.0), np.arange(0, HD, 2, dtype=np.float32) / np.float32(HD))).astype(np.float32)
    angle = (np.arange(T, dtype=np.float32)[None, :] * inv[:, None]).astype(np.float32)
    cos, sin = np.cos(angle), np.sin(angle)
    keys, queries = np.arange(T)[None, None, :], np.arange(P)[:, None, None] + P * np.arange(2)[None, :, None]
    wk = np.asarray(L0_xattn_Wk).reshape(KV2, HD2, D)
    wk = np.concatenate([np.concatenate([wk[i], wk[-1, i * 32:(i + 1) * 32]]) for i in range(KTILES)])
    arrays = {
        "x_t": chunked(rows.T),
        "x_rows": rows.reshape(TILES, P, D).transpose(1, 0, 2),
        "w_qkv": w.transpose(2, 1, 0, 3),
        "w_o": np.asarray(L0_attn_w_o).reshape(KVH, GRP, HD, D).transpose(0, 2, 1, 3),
        "cos_t": np.concatenate([cos, cos]),
        "sin_t": np.concatenate([-sin, sin]),
        "mask": np.where(keys <= queries, 0.0, NEG).astype(np.float32),
        "eye": np.eye(P, dtype=np.float32),
        "ctx_t": np.concatenate([ctx, ctx[:, -1:]], axis=1).reshape(B, CTXP, C, P).transpose(0, 3, 2, 1),
        "wq": chunked(np.asarray(L0_xattn_Wq).T),
        "wk": chunked(wk.T).reshape(P, -1),
        "wv": chunked(np.asarray(L0_xattn_Wv).T).reshape(P, -1),
        "wo2": np.asarray(L0_xattn_Wo).T.reshape(-1, P, D).transpose(1, 0, 2),
        "w_t": chunked(np.asarray(L0_ffn_W).T),
        "lora_a": np.asarray(L0_ffn_lora_A).reshape(-1, D),
        "lora_bt": np.asarray(L0_ffn_lora_B).transpose(0, 2, 1).reshape(-1, D),
        "lora_w": np.repeat(np.asarray(L0_ffn_lora_weights), 16).reshape(-1, 1),
        "bias": np.asarray(L0_ffn_bias).reshape(1, D),
    }
    arrays = {k: np.ascontiguousarray(a) for k, a in arrays.items()}
    nc = bacc.Bacc("TRN2", target_bir_lowering=False, num_devices=1)
    aps = {k: nc.dram_tensor(f"in_{k}", a.shape, mybir.dt.from_np(a.dtype), kind="ExternalInput").ap()
           for k, a in arrays.items()}
    out = nc.dram_tensor("out_0", (TOK, D), F32, kind="ExternalOutput").ap()
    program(nc, out=out, **aps)
    r = run_bass_kernel_spmd(nc, [{f"in_{k}": a for k, a in arrays.items()}], core_ids=[0])
    return r.results[0]["out_0"].reshape(B, T, D)
```
